# Optimizing a Trainium2 kernel written in Bass

```python
import numpy as np
import jax
import jax.numpy as jnp

def _softmax(x, axis=-1):
    return jax.nn.softmax(x, axis=axis)

def _gelu(x):
    return jax.nn.gelu(x, approximate=True)

def _silu(x):
    return jax.nn.silu(x)

def _sigmoid(x):
    return jax.nn.sigmoid(x)

def _layernorm(x, axis=-1, eps=1e-05):
    m = jnp.mean(x, axis=axis, keepdims=True)
    v = jnp.var(x, axis=axis, keepdims=True)
    return (x - m) / jnp.sqrt(v + eps)

def _scatter_add(tgt, idx, src, axis=0):
    return tgt.at[idx].add(src)

def _segment_sum(src, seg, n):
    return jax.ops.segment_sum(src, seg, n)
kernel_name = 'mk_decoder_postln_d2_seqx_r8_77da6e'

def setup_inputs(seed: int=0):
    np.random.seed(seed)
    _w = jnp.asarray

    def _rec_inputs():
        import jax
        import jax.numpy as jnp
        _rk = jax.random.key(seed)
        x = 7.22e-05 + 1 * jax.random.normal(jax.random.fold_in(_rk, 1), (32, 64, 512), jnp.float32)
        _lenS = 64 - jax.random.randint(jax.random.fold_in(_rk, 7), (32,), 0, max(1, 64 // 4) + 1, jnp.int32)
        _lenS2 = 64 - jax.random.randint(jax.random.fold_in(_rk, 8), (32,), 0, max(1, 64 // 4) + 1, jnp.int32)
        _ctx_4096P = jax.random.normal(jax.random.fold_in(_rk, 11), (32, 16, 512), jnp.float32)
        _ctx_4096c = jax.random.dirichlet(jax.random.fold_in(_rk, 511), 0.3 * jnp.ones((16,), jnp.float32), (32, 64))
        _ctx_4096t = jnp.einsum('bsk,bkd->bsd', _ctx_4096c, _ctx_4096P)
        _ctx_4096t = _ctx_4096t * jax.lax.rsqrt(jnp.mean(jnp.square(_ctx_4096t)) + 1e-12) * 0.953939
        ctx_4096 = 4.13588e-05 + 0.999923 * (_ctx_4096t + 0.3 * jax.random.normal(jax.random.fold_in(_rk, 611), (32, 64, 512), jnp.float32))
        return (x, ctx_4096)
    x, ctx_4096 = _rec_inputs()

    def _L0_attn_setup():
        import jax, jax.numpy as jnp
        import numpy as np
        import math
        DIM = 512
        N_HEADS = 32
        N_KV_HEADS = 8
        HEAD_DIM = DIM // N_HEADS
        N_REP = N_HEADS // N_KV_HEADS
        ROPE_BASE = 10000.0

        def apply_rotary_emb(x):
            b, s, h, d = x.shape
            inv_freq = 1.0 / ROPE_BASE ** (jnp.arange(0, d, 2, dtype=jnp.float32) / d)
            pos = jnp.arange(s, dtype=jnp.float32)
            ang = pos[:, None] * inv_freq[None, :]
            cos = jnp.cos(ang)[None, :, None, :]
            sin = jnp.sin(ang)[None, :, None, :]
            xr = x.reshape(b, s, h, d // 2, 2)
            x0, x1 = (xr[..., 0], xr[..., 1])
            out = jnp.stack([x0 * cos - x1 * sin, x0 * sin + x1 * cos], axis=-1)
            return out.reshape(b, s, h, d)
        key = jax.random.key(seed)
        ks = jax.random.split(key, 5)
        sc = 1.0 / math.sqrt(DIM)
        return {'x': jax.random.normal(ks[0], (2, 256, DIM), dtype=jnp.float32), 'Wq': jax.random.normal(ks[1], (DIM, N_HEADS * HEAD_DIM), dtype=jnp.float32) * sc, 'Wk': jax.random.normal(ks[2], (DIM, N_KV_HEADS * HEAD_DIM), dtype=jnp.float32) * sc, 'Wv': jax.random.normal(ks[3], (DIM, N_KV_HEADS * HEAD_DIM), dtype=jnp.float32) * sc, 'Wo': jax.random.normal(ks[4], (N_HEADS * HEAD_DIM, DIM), dtype=jnp.float32) * sc}
    _L0_attn_all = _L0_attn_setup()
    _L0_attn_in = {k: v for k, v in _L0_attn_all.items() if k in ('Wq', 'Wk', 'Wv', 'Wo')}
    del _L0_attn_all

    def _L0_xattn_setup():
        import jax, jax.numpy as jnp
        import numpy as np
        HEADS = 8
        WINDOW = 16

        def _pointwise(W, b, t):
            return jnp.einsum('oc,bct->bot', W, t) + b[None, :, None]
        key = jax.random.key(seed)
        ks = jax.random.split(key, 10)
        B, C, T = (4, 64, 512)
        s = 0.02
        return {'x': jax.random.normal(ks[0], (B, C, T), jnp.float32), 'cond': jax.random.normal(ks[1], (B, C, T), jnp.float32), 'Wq': jax.random.normal(ks[2], (C, C), jnp.float32) * s, 'bq': jnp.zeros((C,), jnp.float32), 'Wk': jax.random.normal(ks[3], (C, C), jnp.float32) * s, 'bk': jnp.zeros((C,), jnp.float32), 'Wv': jax.random.normal(ks[4], (C, C), jnp.float32) * s, 'bv': jnp.zeros((C,), jnp.float32), 'Wo': jax.random.normal(ks[5], (C, C), jnp.float32) * s, 'bo': jnp.zeros((C,), jnp.float32)}
    _L0_xattn_all = _L0_xattn_setup()
    _L0_xattn_in = {k: v for k, v in _L0_xattn_all.items() if k in ('Wq', 'bq', 'Wk', 'bk', 'Wv', 'bv', 'Wo', 'bo')}
    del _L0_xattn_all

    def _L0_ffn_setup():
        import jax, jax.numpy as jnp
        import numpy as np
        BLOCK = 32
        WBITS = 4
        ABITS = 16

        def _ste(x, dq):
            return x + jax.lax.stop_gradient(dq - x)

        def block_qdq_weight(w, block=BLOCK, bits=WBITS):
            out_f, in_f = w.shape
            wb = w.reshape(out_f, in_f // block, block)
            qmax = 2 ** (bits - 1) - 1
            scale = jnp.maximum(jnp.max(jnp.abs(wb), axis=-1, keepdims=True) / qmax, 1e-12)
            wq = jnp.clip(jnp.round(wb / scale), -qmax - 1, qmax) * scale
            return _ste(w, wq.reshape(out_f, in_f))

        def act_qdq(x, bits=ABITS):
            qmax = 2 ** bits - 1
            mn = jnp.minimum(jnp.min(x), 0.0)
            mx = jnp.maximum(jnp.max(x), 0.0)
            scale = jnp.maximum((mx - mn) / qmax, 1e-12)
            zp = jnp.clip(jnp.round(-mn / scale), 0, qmax)
            q = jnp.clip(jnp.round(x / scale) + zp, 0, qmax)
            return _ste(x, (q - zp) * scale)

        def fixed_qdq(x, scale, zp=0.0, bits=ABITS):
            qmax = 2 ** bits - 1
            q = jnp.clip(jnp.round(x / scale) + zp, 0, qmax)
            return _ste(x, (q - zp) * scale)
        key = jax.random.key(seed)
        k1, k2, k3, k4 = jax.random.split(key, 4)
        H, I = (512, 1376)
        x = jax.random.normal(k1, (2, 256, H), dtype=jnp.float32)
        w_gate = jax.random.normal(k2, (I, H), dtype=jnp.float32) * H ** (-0.5)
        w_up = jax.random.normal(k3, (I, H), dtype=jnp.float32) * H ** (-0.5)
        w_down = jax.random.normal(k4, (H, I), dtype=jnp.float32) * I ** (-0.5)
        return {'x': x, 'w_gate': w_gate, 'w_up': w_up, 'w_down': w_down}
    _L0_ffn_all = _L0_ffn_setup()
    _L0_ffn_in = {k: v for k, v in _L0_ffn_all.items() if k in ('w_gate', 'w_up', 'w_down')}
    del _L0_ffn_all

    def _L1_attn_setup():
        import jax, jax.numpy as jnp
        import numpy as np
        B, S, HID = (1, 256, 512)
        H, HK, D = (32, 8, 128)
        L = D // 4
        key = jax.random.key(seed)
        ks = jax.random.split(key, 7)
        s = 0.02
        return {'hidden_states': jax.random.normal(ks[0], (B, S, HID), jnp.float32), 'Wq': jax.random.normal(ks[1], (H * D, HID), jnp.float32) * s, 'Wk_down': jax.random.normal(ks[2], (HK * L, HID), jnp.float32) * s, 'Wv_down': jax.random.normal(ks[3], (HK * L, HID), jnp.float32) * s, 'Wk_up': jax.random.normal(ks[4], (HK * D, HK * L), jnp.float32) * s, 'Wv_up': jax.random.normal(ks[5], (HK * D, HK * L), jnp.float32) * s, 'Wo': jax.random.normal(ks[6], (HID, H * D), jnp.float32) * s}
    _L1_attn_all = _L1_attn_setup()
    _L1_attn_in = {k: v for k, v in _L1_attn_all.items() if k in ('Wq', 'Wk_down', 'Wv_down', 'Wk_up', 'Wv_up', 'Wo')}
    del _L1_attn_all

    def _L1_xattn_setup():
        import jax, jax.numpy as jnp
        import numpy as np
        DIM = 64
        HEADS = 8
        DIM_HEAD = 64
        HIDDEN = HEADS * DIM_HEAD
        SCALE = DIM_HEAD ** (-0.5)
        key = jax.random.key(seed)
        ks = jax.random.split(key, 9)
        b, n = (8, 512)
        std = 1.0 / np.sqrt(DIM)
        return {'q': jax.random.normal(ks[0], (b, DIM, n), jnp.float32), 'k': jax.random.normal(ks[1], (b, DIM, n), jnp.float32), 'v': jax.random.normal(ks[2], (b, DIM, n), jnp.float32), 'Wq': jax.random.normal(ks[3], (HIDDEN, DIM), jnp.float32) * std, 'Wk': jax.random.normal(ks[4], (HIDDEN, DIM), jnp.float32) * std, 'Wv': jax.random.normal(ks[5], (HIDDEN, DIM), jnp.float32) * std, 'Wo': jax.random.normal(ks[6], (DIM, HIDDEN), jnp.float32) * (1.0 / np.sqrt(HIDDEN)), 'bo': jax.random.normal(ks[7], (DIM,), jnp.float32) * 0.01, 'g': jnp.ones((1, DIM, 1), jnp.float32)}
    _L1_xattn_all = _L1_xattn_setup()
    _L1_xattn_in = {k: v for k, v in _L1_xattn_all.items() if k in ('Wq', 'Wk', 'Wv', 'Wo', 'bo', 'g')}
    del _L1_xattn_all

    def _L1_ffn_setup():
        import jax, jax.numpy as jnp
        import numpy as np
        HIDDEN = 512
        INTER = 1376
        GROUPSIZE = 128
        PACK = 8

        def dequant_gptq(qweight, scales, zeros, groupsize):
            K = qweight.shape[0] * PACK
            N = qweight.shape[1]
            k = jnp.arange(K)
            q = qweight[k // PACK, :] >> (k % PACK * 4)[:, None] & 15
            n = jnp.arange(N)
            z = zeros[:, n // PACK] >> (n % PACK * 4)[None, :] & 15
            s = scales.astype(jnp.float32)
            zp = (z.astype(jnp.float32) + 1.0) * s
            g = k // groupsize
            return q.astype(jnp.float32) * s[g] - zp[g]
        key = jax.random.key(seed)
        ks = jax.random.split(key, 11)
        imax = 2147483647
        G_h = HIDDEN // GROUPSIZE
        G_i = (INTER + GROUPSIZE - 1) // GROUPSIZE
        x = (jax.random.normal(ks[0], (2, 256, HIDDEN), dtype=jnp.float32) * 0.5).astype(jnp.float16)
        return {'x': x, 'gate_qweight': jax.random.randint(ks[1], (HIDDEN // PACK, INTER), 0, imax, dtype=jnp.int32), 'gate_scales': (jax.random.uniform(ks[2], (G_h, INTER), dtype=jnp.float32) * 0.01 + 0.001).astype(jnp.float16), 'gate_zeros': jax.random.randint(ks[3], (G_h, INTER // PACK), 0, imax, dtype=jnp.int32), 'up_qweight': jax.random.randint(ks[4], (HIDDEN // PACK, INTER), 0, imax, dtype=jnp.int32), 'up_scales': (jax.random.uniform(ks[5], (G_h, INTER), dtype=jnp.float32) * 0.01 + 0.001).astype(jnp.float16), 'up_zeros': jax.random.randint(ks[6], (G_h, INTER // PACK), 0, imax, dtype=jnp.int32), 'down_qweight': jax.random.randint(ks[7], (INTER // PACK, HIDDEN), 0, imax, dtype=jnp.int32), 'down_scales': (jax.random.uniform(ks[8], (G_i, HIDDEN), dtype=jnp.float32) * 0.01 + 0.001).astype(jnp.float16), 'down_zeros': jax.random.randint(ks[9], (G_i, HIDDEN // PACK), 0, imax, dtype=jnp.int32)}
    _L1_ffn_all = _L1_ffn_setup()
    _L1_ffn_in = {k: v for k, v in _L1_ffn_all.items() if k in ('gate_qweight', 'gate_scales', 'gate_zeros', 'up_qweight', 'up_scales', 'up_zeros', 'down_qweight', 'down_scales', 'down_zeros')}
    del _L1_ffn_all
    return {'x': x, 'ctx_4096': ctx_4096, 'L0_attn_Wq': _L0_attn_in['Wq'], 'L0_attn_Wk': _L0_attn_in['Wk'], 'L0_attn_Wv': _L0_attn_in['Wv'], 'L0_attn_Wo': _L0_attn_in['Wo'], 'L0_xattn_Wq': _L0_xattn_in['Wq'], 'L0_xattn_bq': _L0_xattn_in['bq'], 'L0_xattn_Wk': _L0_xattn_in['Wk'], 'L0_xattn_bk': _L0_xattn_in['bk'], 'L0_xattn_Wv': _L0_xattn_in['Wv'], 'L0_xattn_bv': _L0_xattn_in['bv'], 'L0_xattn_Wo': _L0_xattn_in['Wo'], 'L0_xattn_bo': _L0_xattn_in['bo'], 'L0_ffn_w_gate': _L0_ffn_in['w_gate'], 'L0_ffn_w_up': _L0_ffn_in['w_up'], 'L0_ffn_w_down': _L0_ffn_in['w_down'], 'L1_attn_Wq': _L1_attn_in['Wq'], 'L1_attn_Wk_down': _L1_attn_in['Wk_down'], 'L1_attn_Wv_down': _L1_attn_in['Wv_down'], 'L1_attn_Wk_up': _L1_attn_in['Wk_up'], 'L1_attn_Wv_up': _L1_attn_in['Wv_up'], 'L1_attn_Wo': _L1_attn_in['Wo'], 'L1_xattn_Wq': _L1_xattn_in['Wq'], 'L1_xattn_Wk': _L1_xattn_in['Wk'], 'L1_xattn_Wv': _L1_xattn_in['Wv'], 'L1_xattn_Wo': _L1_xattn_in['Wo'], 'L1_xattn_bo': _L1_xattn_in['bo'], 'L1_xattn_g': _L1_xattn_in['g'], 'L1_ffn_gate_qweight': _L1_ffn_in['gate_qweight'], 'L1_ffn_gate_scales': _L1_ffn_in['gate_scales'], 'L1_ffn_gate_zeros': _L1_ffn_in['gate_zeros'], 'L1_ffn_up_qweight': _L1_ffn_in['up_qweight'], 'L1_ffn_up_scales': _L1_ffn_in['up_scales'], 'L1_ffn_up_zeros': _L1_ffn_in['up_zeros'], 'L1_ffn_down_qweight': _L1_ffn_in['down_qweight'], 'L1_ffn_down_scales': _L1_ffn_in['down_scales'], 'L1_ffn_down_zeros': _L1_ffn_in['down_zeros']}

def reference(x, ctx_4096, L0_attn_Wq, L0_attn_Wk, L0_attn_Wv, L0_attn_Wo, L0_xattn_Wq, L0_xattn_bq, L0_xattn_Wk, L0_xattn_bk, L0_xattn_Wv, L0_xattn_bv, L0_xattn_Wo, L0_xattn_bo, L0_ffn_w_gate, L0_ffn_w_up, L0_ffn_w_down, L1_attn_Wq, L1_attn_Wk_down, L1_attn_Wv_down, L1_attn_Wk_up, L1_attn_Wv_up, L1_attn_Wo, L1_xattn_Wq, L1_xattn_Wk, L1_xattn_Wv, L1_xattn_Wo, L1_xattn_bo, L1_xattn_g, L1_ffn_gate_qweight, L1_ffn_gate_scales, L1_ffn_gate_zeros, L1_ffn_up_qweight, L1_ffn_up_scales, L1_ffn_up_zeros, L1_ffn_down_qweight, L1_ffn_down_scales, L1_ffn_down_zeros):
    import jax
    import jax.numpy as jnp

    def _L0_attn_ref(x, Wq, Wk, Wv, Wo):
        import jax, jax.numpy as jnp
        import numpy as np
        import math
        DIM = 512
        N_HEADS = 32
        N_KV_HEADS = 8
        HEAD_DIM = DIM // N_HEADS
        N_REP = N_HEADS // N_KV_HEADS
        ROPE_BASE = 10000.0

        def apply_rotary_emb(x):
            b, s, h, d = x.shape
            inv_freq = 1.0 / ROPE_BASE ** (jnp.arange(0, d, 2, dtype=jnp.float32) / d)
            pos = jnp.arange(s, dtype=jnp.float32)
            ang = pos[:, None] * inv_freq[None, :]
            cos = jnp.cos(ang)[None, :, None, :]
            sin = jnp.sin(ang)[None, :, None, :]
            xr = x.reshape(b, s, h, d // 2, 2)
            x0, x1 = (xr[..., 0], xr[..., 1])
            out = jnp.stack([x0 * cos - x1 * sin, x0 * sin + x1 * cos], axis=-1)
            return out.reshape(b, s, h, d)
        b, s, _ = x.shape
        xq = (x @ Wq).reshape(b, s, N_HEADS, HEAD_DIM)
        xk = (x @ Wk).reshape(b, s, N_KV_HEADS, HEAD_DIM)
        xv = (x @ Wv).reshape(b, s, N_KV_HEADS, HEAD_DIM)
        xq = apply_rotary_emb(xq)
        xk = apply_rotary_emb(xk)
        xk = jnp.repeat(xk, N_REP, axis=2)
        xv = jnp.repeat(xv, N_REP, axis=2)
        scores = jnp.einsum('bqhd,bkhd->bhqk', xq, xk) / math.sqrt(HEAD_DIM)
        causal = jnp.tril(jnp.ones((s, s), dtype=bool))
        scores = jnp.where(causal[None, None], scores, -jnp.inf)
        probs = jax.nn.softmax(scores.astype(jnp.float32), axis=-1).astype(xq.dtype)
        out = jnp.einsum('bhqk,bkhd->bqhd', probs, xv).reshape(b, s, N_HEADS * HEAD_DIM)
        return out @ Wo

    def _L0_xattn_ref(x, cond, Wq, bq, Wk, bk, Wv, bv, Wo, bo):
        import jax, jax.numpy as jnp
        import numpy as np
        HEADS = 8
        WINDOW = 16

        def _pointwise(W, b, t):
            return jnp.einsum('oc,bct->bot', W, t) + b[None, :, None]
        B, C, T = x.shape
        H, W = (HEADS, WINDOW)
        hd = C // H
        scale = hd ** (-0.5)
        pad_left = W // 2
        pad_right = W - pad_left - 1
        q = _pointwise(Wq, bq, x)
        k = _pointwise(Wk, bk, cond)
        v = _pointwise(Wv, bv, cond)
        k = jnp.pad(k, ((0, 0), (0, 0), (pad_left, pad_right)))
        v = jnp.pad(v, ((0, 0), (0, 0), (pad_left, pad_right)))
        idx = jnp.arange(T)[:, None] + jnp.arange(W)[None, :]
        k_win = k[:, :, idx].reshape(B, H, hd, T, W)
        v_win = v[:, :, idx].reshape(B, H, hd, T, W)
        qh = q.reshape(B, H, hd, T)
        dots = jnp.einsum('bhdt,bhdtw->bhtw', qh, k_win) * scale
        attn = jax.nn.softmax(dots, axis=-1)
        out = jnp.einsum('bhtw,bhdtw->bhdt', attn, v_win)
        out = out.reshape(B, C, T)
        return _pointwise(Wo, bo, out)

    def _L0_ffn_ref(x, w_gate, w_up, w_down):
        import jax, jax.numpy as jnp
        import numpy as np
        BLOCK = 32
        WBITS = 4
        ABITS = 16

        def _ste(x, dq):
            return x + jax.lax.stop_gradient(dq - x)

        def block_qdq_weight(w, block=BLOCK, bits=WBITS):
            out_f, in_f = w.shape
            wb = w.reshape(out_f, in_f // block, block)
            qmax = 2 ** (bits - 1) - 1
            scale = jnp.maximum(jnp.max(jnp.abs(wb), axis=-1, keepdims=True) / qmax, 1e-12)
            wq = jnp.clip(jnp.round(wb / scale), -qmax - 1, qmax) * scale
            return _ste(w, wq.reshape(out_f, in_f))

        def act_qdq(x, bits=ABITS):
            qmax = 2 ** bits - 1
            mn = jnp.minimum(jnp.min(x), 0.0)
            mx = jnp.maximum(jnp.max(x), 0.0)
            scale = jnp.maximum((mx - mn) / qmax, 1e-12)
            zp = jnp.clip(jnp.round(-mn / scale), 0, qmax)
            q = jnp.clip(jnp.round(x / scale) + zp, 0, qmax)
            return _ste(x, (q - zp) * scale)

        def fixed_qdq(x, scale, zp=0.0, bits=ABITS):
            qmax = 2 ** bits - 1
            q = jnp.clip(jnp.round(x / scale) + zp, 0, qmax)
            return _ste(x, (q - zp) * scale)
        sigmoid_scale = 1.0 / 65536.0
        wg = block_qdq_weight(w_gate)
        wu = block_qdq_weight(w_up)
        wd = block_qdq_weight(w_down)
        xq = act_qdq(x)
        up = act_qdq(jnp.einsum('bsh,ih->bsi', xq, wu))
        gate = act_qdq(jnp.einsum('bsh,ih->bsi', xq, wg))
        sig = fixed_qdq(jax.nn.sigmoid(gate), sigmoid_scale)
        gate = act_qdq(gate * sig)
        o = act_qdq(gate * up)
        return jnp.einsum('bsi,hi->bsh', o, wd)

    def _L1_attn_ref(hidden_states, Wq, Wk_down, Wv_down, Wk_up, Wv_up, Wo):
        import jax, jax.numpy as jnp
        import numpy as np
        B, S, HID = (1, 256, 512)
        H, HK, D = (32, 8, 128)
        L = D // 4
        b, s, _ = hidden_states.shape
        q = (hidden_states @ Wq.T).reshape(b, s, H, D).transpose(0, 2, 1, 3)
        kc = (hidden_states @ Wk_down.T).reshape(b, s, HK, L).transpose(0, 2, 1, 3)
        vc = (hidden_states @ Wv_down.T).reshape(b, s, HK, L).transpose(0, 2, 1, 3)
        lat = jnp.concatenate([kc, vc], axis=-1).reshape(b, s, HK * 2 * L)
        k_cmp, v_cmp = jnp.split(lat, 2, axis=-1)
        k = (k_cmp @ Wk_up.T).reshape(b, s, HK, D).transpose(0, 2, 1, 3)
        v = (v_cmp @ Wv_up.T).reshape(b, s, HK, D).transpose(0, 2, 1, 3)
        n_rep = H // HK
        k = jnp.repeat(k, n_rep, axis=1)
        v = jnp.repeat(v, n_rep, axis=1)
        scale = 1.0 / jnp.sqrt(jnp.asarray(D, hidden_states.dtype))
        scores = jnp.einsum('bhqd,bhkd->bhqk', q, k) * scale
        causal = jnp.tril(jnp.ones((s, s), dtype=bool))
        scores = jnp.where(causal, scores, jnp.asarray(-1000000000.0, scores.dtype))
        attn = jax.nn.softmax(scores, axis=-1)
        out = jnp.einsum('bhqk,bhkd->bhqd', attn, v)
        out = out.transpose(0, 2, 1, 3).reshape(b, s, H * D)
        return out @ Wo.T

    def _L1_xattn_ref(q, k, v, Wq, Wk, Wv, Wo, bo, g):
        import jax, jax.numpy as jnp
        import numpy as np
        DIM = 64
        HEADS = 8
        DIM_HEAD = 64
        HIDDEN = HEADS * DIM_HEAD
        SCALE = DIM_HEAD ** (-0.5)
        b = q.shape[0]
        qh = jnp.einsum('bcn,oc->bon', q, Wq).reshape(b, HEADS, DIM_HEAD, -1)
        kh = jnp.einsum('bcn,oc->bon', k, Wk).reshape(b, HEADS, DIM_HEAD, -1)
        vh = jnp.einsum('bcn,oc->bon', v, Wv).reshape(b, HEADS, DIM_HEAD, -1)
        qh = jax.nn.softmax(qh, axis=-2) * SCALE
        kh = jax.nn.softmax(kh, axis=-1)
        context = jnp.einsum('bhdn,bhen->bhde', kh, vh)
        out = jnp.einsum('bhde,bhdn->bhen', context, qh)
        out = out.reshape(b, HIDDEN, -1)
        out = jnp.einsum('bcn,oc->bon', out, Wo) + bo[None, :, None]
        norm = jnp.maximum(jnp.sqrt(jnp.sum(out * out, axis=1, keepdims=True)), 1e-12)
        return out / norm * g * np.sqrt(DIM)

    def _L1_ffn_ref(x, gate_qweight, gate_scales, gate_zeros, up_qweight, up_scales, up_zeros, down_qweight, down_scales, down_zeros):
        import jax, jax.numpy as jnp
        import numpy as np
        HIDDEN = 512
        INTER = 1376
        GROUPSIZE = 128
        PACK = 8

        def dequant_gptq(qweight, scales, zeros, groupsize):
            K = qweight.shape[0] * PACK
            N = qweight.shape[1]
            k = jnp.arange(K)
            q = qweight[k // PACK, :] >> (k % PACK * 4)[:, None] & 15
            n = jnp.arange(N)
            z = zeros[:, n // PACK] >> (n % PACK * 4)[None, :] & 15
            s = scales.astype(jnp.float32)
            zp = (z.astype(jnp.float32) + 1.0) * s
            g = k // groupsize
            return q.astype(jnp.float32) * s[g] - zp[g]
        B, S, H = x.shape
        x2 = x.reshape(-1, H).astype(jnp.float32)
        Wg = dequant_gptq(gate_qweight, gate_scales, gate_zeros, GROUPSIZE)
        Wu = dequant_gptq(up_qweight, up_scales, up_zeros, GROUPSIZE)
        Wd = dequant_gptq(down_qweight, down_scales, down_zeros, GROUPSIZE)
        gate = x2 @ Wg
        up = x2 @ Wu
        inter = gate * jax.nn.sigmoid(gate) * up
        out = (inter @ Wd).astype(jnp.float16)
        return out.reshape(B, S, H)
    x = _layernorm(x + _L0_attn_ref(x, L0_attn_Wq, L0_attn_Wk, L0_attn_Wv, L0_attn_Wo), axis=-1)
    x = _layernorm(x + _L0_xattn_ref(x, ctx_4096, L0_xattn_Wq, L0_xattn_bq, L0_xattn_Wk, L0_xattn_bk, L0_xattn_Wv, L0_xattn_bv, L0_xattn_Wo, L0_xattn_bo), axis=-1)
    x = _layernorm(x + _L0_ffn_ref(x, L0_ffn_w_gate, L0_ffn_w_up, L0_ffn_w_down), axis=-1)
    x = _layernorm(x + _L1_attn_ref(x, L1_attn_Wq, L1_attn_Wk_down, L1_attn_Wv_down, L1_attn_Wk_up, L1_attn_Wv_up, L1_attn_Wo), axis=-1)
    x = _layernorm(x + _L1_xattn_ref(x, ctx_4096, ctx_4096, L1_xattn_Wq, L1_xattn_Wk, L1_xattn_Wv, L1_xattn_Wo, L1_xattn_bo, L1_xattn_g), axis=-1)
    x = _layernorm(x + _L1_ffn_ref(x, L1_ffn_gate_qweight, L1_ffn_gate_scales, L1_ffn_gate_zeros, L1_ffn_up_qweight, L1_ffn_up_scales, L1_ffn_up_zeros, L1_ffn_down_qweight, L1_ffn_down_scales, L1_ffn_down_zeros), axis=-1)
    return x

_drawn_inputs = setup_inputs


def setup_inputs(seed=0):
    import zlib

    import numpy as np

    out = dict(_drawn_inputs(seed))
    spreads = {'L0_xattn_bq': (0.0, 0.8),
     'L0_xattn_bk': (0.0, 2.0),
     'L0_xattn_bv': (0.0, 0.8),
     'L0_xattn_bo': (0.0, 2.0),
     'L1_xattn_g': (1.0, 0.2)}
    factors = {'L0_xattn_Wq': 8.0,
     'L0_xattn_Wk': 8.0,
     'L0_xattn_Wv': 4.324,
     'L0_xattn_Wo': 4.279,
     'L1_attn_Wq': 8.0,
     'L1_attn_Wk_up': 8.0}
    for name, (base, spread) in spreads.items():
        noise = np.random.default_rng([zlib.crc32(name.encode()), seed]).standard_normal(out[name].shape)
        drawn = base * np.exp(spread * noise) if base else spread * noise
        out[name] = jnp.asarray(drawn.astype(out[name].dtype))
    for name, factor in factors.items():
        out[name] = (out[name] * factor).astype(out[name].dtype)
    return out
```

```python
from contextlib import ExitStack

import numpy as np

import concourse.bass as bass
from concourse import mybir

ALU = mybir.AluOpType
ACT = mybir.ActivationFunctionType
AX = mybir.AxisListType
F32 = mybir.dt.float32
F16 = mybir.dt.float16
I32 = mybir.dt.int32
RMAX = bass.bass_isa.ReduceOp.max

P = 128
B, S, D = 32, 64, 512
ROWS = B * S
NT = ROWS // P
DC = D // P
EPS = 1e-5
NEG = -1e30


class Scope:

    def __init__(self, nc, name):
        self.nc, self.name, self.stack, self.sems = nc, name, ExitStack(), []

    def __enter__(self):
        self.stack.__enter__()
        return self

    def __exit__(self, *a):
        if self.sems and a[0] is None:
            self.nc.clear_and_free_semaphores(self.sems)
            self.nc.all_engine_barrier()
        return self.stack.__exit__(*a)

    def sb(self, name, shape, dt=F32):
        return self.stack.enter_context(self.nc.sbuf_tensor(f"{self.name}_{name}", shape, dt))

    def ps(self, name, shape):
        return self.stack.enter_context(self.nc.psum_tensor(f"{self.name}_{name}", shape, F32))

    def sem(self, name):
        self.sems.append(self.nc.alloc_semaphore(f"{self.name}_{name}"))
        return self.sems[-1]

    def block(self):
        return self.nc.Block()


def wait_apart(eng, sem, turn, held):
    eng.wait_ge(sem, turn)
    eng.sem_inc(held, 1)


class Norm:

    def __init__(self, nc, s, ahead=0):
        self.nc = nc
        self.ahead = ahead
        self.y = s.sb("y", [P, D])
        self.xn = s.sb("xn", [P, D])
        self.stats = s.sb("stats", [P, 6])
        self.mv = s.sb("mv", [P, 2])
        self.ve = s.sb("ve", [P, 1])
        self.rstd = s.sb("rstd", [P, 1])
        self.y_ready = s.sem("y_ready")
        self.stats_ready = s.sem("stats_ready")
        self.held = s.sem("held")
        self.mv_ready = s.sem("mv_ready")
        self.ve_ready = s.sem("ve_ready")
        self.rstd_ready = s.sem("rstd_ready")
        self.xn_ready = s.sem("xn_ready")
        self.stored = s.sem("stored")

    def vector(self, dve, turn):
        self.moments(dve, turn)
        self.normed(dve, turn)

    def moments(self, dve, turn):
        nc = self.nc
        dve.wait_ge(self.y_ready, turn + self.ahead)
        nc.vector.bn_stats(self.stats[:, :], self.y[:, :]).then_inc(self.stats_ready, 1)
        wait_apart(dve, self.stats_ready, turn, self.held)
        nc.vector.bn_aggr(self.mv[:, :], self.stats[:, :]).then_inc(self.mv_ready, 1)
        dve.wait_ge(self.mv_ready, turn)
        nc.vector.tensor_scalar(self.ve[:, :], self.mv[:, 1:2], EPS, None, ALU.add).then_inc(self.ve_ready, 1)

    def normed(self, dve, turn):
        dve.wait_ge(self.rstd_ready, turn)
        dve.wait_ge(self.stored, turn * 16)
        self.nc.vector.tensor_scalar(self.xn[:, :], self.y[:, :], self.mv[:, 0:1], self.rstd[:, :],
                                     ALU.subtract, ALU.mult).then_inc(self.xn_ready, 1)
        dve.wait_ge(self.xn_ready, turn)

    def end(self, dve):
        dve.wait_ge(self.held, NT)

    def root(self, pool, turn, m_half):
        pool.wait_ge(self.ve_ready, turn)
        self.nc.gpsimd.tensor_tensor(self.rstd[:, :], self.ve[:, :], m_half[:, :], ALU.pow).then_inc(self.rstd_ready, 1)

    def store(self, sp, x_out, i, turn):
        sp.wait_ge(self.xn_ready, turn)
        sp.dma_start(rows(x_out, i), self.xn[:, :]).then_inc(self.stored, 16)


def rows(dram, i):
    return dram[bass.ds(i * P, P), :]



def attention0(nc, x_in, x_out, wq, wk, wv, wo, k):
    NH, HD, NKV = 32, 16, 8
    NQK = (NH + NKV) * HD
    with Scope(nc, "a0") as s:
        ident = s.sb("ident", [P, P])
        cos = s.sb("cos", [P, HD])
        sin = s.sb("sin", [P, HD])
        causal = s.sb("causal", [P, S])
        half_mask = s.sb("half_mask", [P, 2])
        m_half = s.sb("m_half", [P, 1])
        w_qkv = s.sb("w_qkv", [P, DC, D + 2 * NKV * HD])
        w_o = s.sb("w_o", [P, DC, D])
        xt = s.sb("xt", [P, D])
        xres = s.sb("xres", [P, D])
        xT = s.sb("xT", [P, DC, P])
        rot_a = s.sb("rot_a", [P, NH + NKV, HD])
        rot_b = s.sb("rot_b", [P, NH + NKV, HD])
        qk = s.sb("qk", [P, NH + NKV, HD])
        krep = s.sb("krep", [P, NKV, 4, HD])
        qT = s.sb("qT", [P, DC, P])
        kpair = s.sb("kpair", [P, DC, 2, 2, S])
        v_hold = s.sb("v_hold", [P, NKV, HD])
        vpair = s.sb("vpair", [P, 2, NKV, 2, HD])
        sc = s.sb("sc", [P, NH, S])
        pr = s.sb("pr", [P, NH, S])
        mx = s.sb("mx", [P, NH])
        sm = s.sb("sm", [P, NH])
        rs = s.sb("rs", [P, NH])
        pT = s.sb("pT", [P, 16, P])
        oT = s.sb("oT", [P, DC, P])
        norm = Norm(nc, s, ahead=1)

        ps_t = s.ps("ps_t", [P, DC, P])
        ps_qkv = s.ps("ps_qkv", [P, 2 * D])
        ps_s = s.ps("ps_s", [P, 4, DC, 2, S])
        ps_y = s.ps("ps_y", [P, D])

        consts = s.sem("consts")
        weights = s.sem("weights")
        zeroed = s.sem("zeroed")
        xt_in = s.sem("xt_in")
        xres_in = s.sem("xres_in")
        xt_turned = s.sem("xt_turned")
        xT_ready = s.sem("xT_ready")
        qkv_ready = s.sem("qkv_ready")
        rot_ready = s.sem("rot_ready")
        qk_ready = s.sem("qk_ready")
        krep_ready = s.sem("krep_ready")
        q_turned = s.sem("q_turned")
        qT_ready = s.sem("qT_ready")
        k_turned = s.sem("k_turned")
        kpair_ready = s.sem("kpair_ready")
        scores_ready = s.sem("scores_ready")
        masked = s.sem("masked")
        mx_ready = s.sem("mx_ready")
        centred = s.sem("centred")
        exp_ready = s.sem("exp_ready")
        sum_ready = s.sem("sum_ready")
        inv_ready = s.sem("inv_ready")
        probs_ready = s.sem("probs_ready")
        probs_turned = s.sem("probs_turned")
        pT_ready = s.sem("pT_ready")
        o_ready = s.sem("o_ready")
        oT_ready = s.sem("oT_ready")
        v_held = s.sem("v_held")
        v_ready = s.sem("v_ready")
        proj_ready = s.sem("proj_ready")

        N_CONST = 6 * 16
        with s.block() as block:

            @block.sync
            def _(sp):
                for dst, src in ((ident, k["ident"]), (cos, k["cos"]), (sin, k["sin"]),
                                 (causal, k["causal"]), (half_mask, k["half_mask"]), (m_half, k["m_half"])):
                    sp.dma_start(dst[:, :], src).then_inc(consts, 16)
                sp.dma_start(xt[:, :], rows(x_in, 0)).then_inc(xt_in, 16)
                n = D
                sp.dma_start(w_qkv[:, :, 0:n], wq.rearrange("(c p) n -> p c n", p=P)).then_inc(weights, 16)
                sp.dma_start(w_qkv[:, :, n:n + P], wk.rearrange("(c p) n -> p c n", p=P)).then_inc(weights, 16)
                sp.dma_start(w_qkv[:, :, n + P:n + 2 * P], wv.rearrange("(c p) n -> p c n", p=P)).then_inc(weights, 16)
                sp.dma_start(w_o[:, :, :], wo.rearrange("(c p) n -> p c n", p=P)).then_inc(weights, 16)

                def load_xt(turn):
                    sp.wait_ge(xt_turned, turn - 1)
                    sp.dma_start(xt[:, :], rows(x_in, turn - 1)).then_inc(xt_in, 16)

                def load_xres(turn):
                    sp.wait_ge(norm.y_ready, turn)
                    sp.dma_start(xres[:, :], rows(x_in, turn - 1)).then_inc(xres_in, 16)

                load_xt(2)
                load_xres(1)
                load_xt(3)
                load_xt(4)
                with sp.Fori(2, NT - 2) as t:
                    load_xt(t + 3)
                    load_xres(t)
                    norm.store(sp, x_out, t - 2, t - 1)
                for t in range(NT - 2, NT + 1):
                    load_xres(t)
                    norm.store(sp, x_out, t - 2, t - 1)
                norm.store(sp, x_out, NT - 1, NT)
                sp.wait_ge(norm.stored, 16 * (NT + 1))

            @block.tensor
            def _(pe):
                def turn_x(turn):
                    pe.wait_ge(xt_in, turn * 16)
                    for c in range(DC):
                        mm = pe.transpose(ps_t[:, c, :], xt[:, c * P:(c + 1) * P], ident[:, :])
                    mm.then_inc(xt_turned, 1)

                def project(turn, held=True):
                    pe.wait_ge(xT_ready, turn)
                    if held:
                        pe.wait_ge(v_held, turn - 1)
                    for c in range(DC):
                        pe.matmul(ps_qkv[:, 0:D], xT[:, c, :], w_qkv[:, c, 0:D], start=c == 0, stop=c == DC - 1)
                    for c in range(DC):
                        mm = pe.matmul(ps_qkv[:, D:D + 256], xT[:, c, :], w_qkv[:, c, D:D + 256],
                                       start=c == 0, stop=c == DC - 1)
                    mm.then_inc(qkv_ready, 1)

                def turn_qk(turn):
                    pe.wait_ge(qk_ready, turn)
                    for c in range(DC):
                        mm = pe.transpose(ps_t[:, c, :], qk[:, 8 * c:8 * c + 8, :].rearrange("p h d -> p (h d)"), ident[:, :])
                    mm.then_inc(q_turned, 1)
                    pe.wait_ge(qT_ready, turn)
                    pe.wait_ge(krep_ready, turn)
                    for c in range(DC):
                        mm = pe.transpose(ps_t[:, c, :], krep[:, 2 * c:2 * c + 2, :, :].rearrange("p g r d -> p (g r d)"),
                                          ident[:, :])
                    mm.then_inc(k_turned, 1)

                def scores(turn):
                    pe.wait_ge(kpair_ready, turn)
                    for a in range(DC):
                        for b in range(2):
                            for j in range(4):
                                q4 = slice(32 * j, 32 * j + 32)
                                mm = pe.matmul(ps_s[64 * b:64 * b + 64, j, a, :, :].rearrange("p e k -> p (e k)"),
                                               qT[q4, a, 64 * b:64 * b + 64],
                                               kpair[q4, a, b, :, :].rearrange("p e k -> p (e k)"),
                                               start=True, stop=True)
                    mm.then_inc(scores_ready, 1)

                def turn_probs(turn, ahead=True):
                    pe.wait_ge(probs_ready, turn)
                    if ahead:
                        pe.wait_ge(masked, turn + 1)
                    for j in range(4):
                        for a in range(DC):
                            h = 8 * a + 2 * j
                            mm = pe.transpose(ps_s[:, j, a, :, :].rearrange("p e k -> p (e k)"),
                                              pr[:, h:h + 2, :].rearrange("p e k -> p (e k)"), ident[:, :])
                    mm.then_inc(probs_turned, 1)

                def attend(turn, ahead=True):
                    pe.wait_ge(pT_ready, turn)
                    pe.wait_ge(v_ready, turn)
                    if ahead:
                        pe.wait_ge(kpair_ready, turn + 2)
                    for a in range(DC):
                        for j in range(4):
                            for b in range(2):
                                mm = pe.matmul(ps_t[32 * j:32 * j + 32, a, 64 * b:64 * b + 64],
                                               vpair[:, b, 2 * a + j // 2, :, :].rearrange("p e d -> p (e d)"),
                                               pT[:, 4 * j + a, 64 * b:64 * b + 64], start=True, stop=True,
                                               tile_position=(0, 32 * j))
                    mm.then_inc(o_ready, 1)

                def output(turn):
                    pe.wait_ge(oT_ready, turn)
                    pe.wait_ge(norm.y_ready, turn)
                    for c in range(DC):
                        mm = pe.matmul(ps_y[:, :], oT[:, c, :], w_o[:, c, :], start=c == 0, stop=c == DC - 1)
                    mm.then_inc(proj_ready, 1)

                def turn_of(t, before=True):
                    scores(t + 1)
                    if before:
                        pe.wait_ge(oT_ready, t - 1)
                    turn_x(t + 2)
                    if before:
                        output(t - 1)
                    project(t + 2)
                    turn_probs(t)
                    turn_qk(t + 2)
                    attend(t)

                pe.wait_ge(consts, N_CONST)
                pe.wait_ge(weights, 64)
                turn_x(1)
                project(1, held=False)
                turn_qk(1)
                scores(1)
                turn_x(2)
                project(2)
                turn_qk(2)
                turn_of(1, before=False)
                with pe.Fori(2, NT - 1) as t:
                    turn_of(t)
                scores(NT)
                output(NT - 2)
                turn_probs(NT - 1)
                attend(NT - 1, ahead=False)
                output(NT - 1)
                turn_probs(NT, ahead=False)
                attend(NT, ahead=False)
                output(NT)

            @block.scalar
            def _(act):
                def front_x(turn):
                    act.wait_ge(xt_turned, turn)
                    nc.scalar.copy(xT[:, :, :], ps_t[:, :, :]).then_inc(xT_ready, 1)

                def front_q(turn):
                    act.wait_ge(q_turned, turn)
                    nc.scalar.copy(qT[:, :, :], ps_t[:, :, :]).then_inc(qT_ready, 1)

                def hold_values(turn, before=True):
                    act.wait_ge(rot_ready, turn)
                    if before:
                        act.wait_ge(v_ready, turn - 1)
                    nc.scalar.copy(v_hold[:, :, :], ps_qkv[:, NQK:NQK + NKV * HD].rearrange("p (g d) -> p g d", d=HD)
                                   ).then_inc(v_held, 1)

                def values(turn):
                    act.wait_ge(v_held, turn)
                    for b in range(2):
                        for e in range(2):
                            ins = nc.scalar.copy(vpair[64 * e:64 * e + 64, b, :, e, :], v_hold[64 * b:64 * b + 64, :, :])
                    ins.then_inc(v_ready, 1)

                def exps(turn, before=True):
                    act.wait_ge(centred, turn)
                    if before:
                        act.wait_ge(probs_turned, turn - 1)
                    nc.scalar.activation(pr[:, :, :], sc[:, :, :], ACT.Exp, scale=HD ** -0.5).then_inc(exp_ready, 1)

                def keep_probs(turn):
                    act.wait_ge(probs_turned, turn)
                    nc.scalar.copy(pT[:, :, :], ps_s[:, :, :, :, :].rearrange("p j a e k -> p (j a) (e k)")).then_inc(pT_ready, 1)

                def keep_attended(turn):
                    act.wait_ge(o_ready, turn)
                    nc.scalar.copy(oT[:, :, :], ps_t[:, :, :]).then_inc(oT_ready, 1)

                def turn_of(t):
                    front_x(t + 2)
                    keep_probs(t)
                    front_q(t + 2)
                    exps(t + 1)
                    keep_attended(t)
                    values(t + 1)
                    hold_values(t + 2)

                act.wait_ge(zeroed, 1)
                front_x(1)
                hold_values(1, before=False)
                values(1)
                front_q(1)
                front_x(2)
                exps(1, before=False)
                hold_values(2)
                front_q(2)
                with act.Fori(1, NT - 1) as t:
                    turn_of(t)
                keep_probs(NT - 1)
                exps(NT)
                keep_attended(NT - 1)
                values(NT)
                keep_probs(NT)
                keep_attended(NT)

            @block.vector
            def _(dve):
                def rotate(turn):
                    dve.wait_ge(qkv_ready, turn)
                    src = ps_qkv[:, 0:NQK].rearrange("p (h d) -> p h d", d=HD)
                    n = NH + NKV
                    nc.vector.tensor_tensor(rot_a[:, :, :], src, cos[:, :].unsqueeze(1).broadcast_to([P, n, HD]), ALU.mult)
                    for e in range(2):
                        ins = nc.vector.tensor_tensor(rot_b[:, :, e::2], src[:, :, 1 - e::2],
                                                      sin[:, e::2].unsqueeze(1).broadcast_to([P, n, HD // 2]), ALU.mult)
                    ins.then_inc(rot_ready, 1)
                    dve.wait_ge(rot_ready, turn)
                    nc.vector.tensor_tensor(qk[:, :, :], rot_a[:, :, :], rot_b[:, :, :], ALU.add).then_inc(qk_ready, 1)

                def pairs(turn):
                    dve.wait_ge(k_turned, turn)
                    for a in range(DC):
                        for b in range(2):
                            ins = nc.vector.tensor_tensor(
                                kpair[:, a, b, :, :],
                                ps_t[:, a, 64 * b:64 * b + 64].unsqueeze(1).broadcast_to([P, 2, S]),
                                half_mask[:, :].unsqueeze(2).broadcast_to([P, 2, S]), ALU.mult)
                    ins.then_inc(kpair_ready, 1)

                def softmax_a(turn):
                    dve.wait_ge(scores_ready, turn)
                    for j in range(4):
                        for a in range(DC):
                            h = 8 * a + 2 * j
                            ins = nc.vector.tensor_tensor(sc[:, h:h + 2, :], ps_s[:, j, a, :, :],
                                                          causal[:, :].unsqueeze(1).broadcast_to([P, 2, S]), ALU.add)
                    ins.then_inc(masked, 1)
                    dve.wait_ge(masked, turn)
                    nc.vector.tensor_reduce(mx[:, :], sc[:, :, :], AX.X, ALU.max).then_inc(mx_ready, 1)
                    dve.wait_ge(mx_ready, turn)
                    nc.vector.tensor_tensor(sc[:, :, :], sc[:, :, :], mx[:, :].unsqueeze(2).broadcast_to([P, NH, S]),
                                            ALU.subtract).then_inc(centred, 1)

                def softmax_b(turn):
                    dve.wait_ge(exp_ready, turn)
                    nc.vector.tensor_reduce(sm[:, :], pr[:, :, :], AX.X, ALU.add).then_inc(sum_ready, 1)
                    dve.wait_ge(sum_ready, turn)
                    nc.vector.reciprocal(rs[:, :], sm[:, :]).then_inc(inv_ready, 1)
                    dve.wait_ge(inv_ready, turn)
                    nc.vector.tensor_tensor(pr[:, :, :], pr[:, :, :], rs[:, :].unsqueeze(2).broadcast_to([P, NH, S]),
                                            ALU.mult).then_inc(probs_ready, 1)

                def normalise(turn):
                    dve.wait_ge(xres_in, turn * 16)
                    dve.wait_ge(proj_ready, turn)
                    nc.vector.tensor_tensor(norm.y[:, :], ps_y[:, :], xres[:, :], ALU.add).then_inc(norm.y_ready, 1)
                    norm.vector(dve, turn)

                nc.vector.memset(vpair[:, :, :, :, :], 0.0).then_inc(zeroed, 1)
                dve.sem_inc(norm.stored, 16)
                dve.sem_inc(norm.y_ready, 1)
                dve.wait_ge(consts, N_CONST)
                rotate(1)
                pairs(1)
                softmax_a(1)
                rotate(2)
                pairs(2)
                softmax_b(1)
                softmax_a(2)
                rotate(3)
                pairs(3)
                softmax_b(2)
                with dve.Fori(2, NT - 1) as t:
                    softmax_a(t + 1)
                    normalise(t - 1)
                    rotate(t + 2)
                    pairs(t + 2)
                    softmax_b(t + 1)
                softmax_a(NT)
                normalise(NT - 2)
                softmax_b(NT)
                normalise(NT - 1)
                normalise(NT)
                norm.end(dve)

            @block.gpsimd
            def _(pool):
                def copies(turn):
                    pool.wait_ge(rot_ready, turn)
                    nc.gpsimd.tensor_tensor(krep[:, :, :, :],
                                            rot_a[:, NH:NH + NKV, :].unsqueeze(2).broadcast_to([P, NKV, 4, HD]),
                                            rot_b[:, NH:NH + NKV, :].unsqueeze(2).broadcast_to([P, NKV, 4, HD]),
                                            ALU.add).then_inc(krep_ready, 1)

                pool.wait_ge(consts, N_CONST)
                for t in range(1, 4):
                    copies(t)
                with pool.Fori(2, NT - 1) as t:
                    norm.root(pool, t - 1, m_half)
                    copies(t + 2)
                norm.root(pool, NT - 2, m_half)
                norm.root(pool, NT - 1, m_half)
                norm.root(pool, NT, m_half)



MAGIC = 12582912.0
QMAX = 65535.0


class Quant:

    SCALE, INV, LO, HI = range(4)

    def __init__(self, s, keep, name, parts):
        self.ends = s.sb(f"{name}_ends", [P, 2, parts])
        self.mine = s.sb(f"{name}_mine", [P, 2])
        self.all = s.sb(f"{name}_all", [P, 2])
        self.tmp = s.sb(f"{name}_tmp", [P, 4])
        self.par = keep.sb(f"{name}_par", [P, 4])
        self.step = s.sem(f"{name}_step")

    def get(self, n):
        return self.par[:, n:n + 1]

    def vector(self, nc, dve):
        step, t = self.step, self.tmp
        nc.vector.tensor_reduce(self.mine[:, :], self.ends[:, :, :], AX.X, ALU.max).then_inc(step, 1)
        dve.wait_ge(step, 2)
        nc.vector.tensor_scalar(self.all[:, :], self.all[:, :], 0.0, None, ALU.max).then_inc(step, 1)
        dve.wait_ge(step, 3)
        nc.vector.tensor_tensor(t[:, 0:1], self.all[:, 0:1], self.all[:, 1:2], ALU.add).then_inc(step, 1)
        dve.wait_ge(step, 4)
        nc.vector.tensor_scalar(self.get(self.SCALE), t[:, 0:1], 1.0 / QMAX, 1e-12, ALU.mult, ALU.max).then_inc(step, 1)
        dve.wait_ge(step, 5)
        nc.vector.reciprocal(self.get(self.INV), self.get(self.SCALE)).then_inc(step, 1)
        dve.wait_ge(step, 6)
        nc.vector.tensor_scalar(t[:, 1:2], self.all[:, 1:2], self.get(self.INV), MAGIC, ALU.mult, ALU.add).then_inc(step, 1)
        dve.wait_ge(step, 7)
        nc.vector.tensor_scalar(t[:, 2:3], t[:, 1:2], MAGIC, QMAX, ALU.subtract, ALU.min).then_inc(step, 1)
        dve.wait_ge(step, 8)
        nc.vector.tensor_scalar(self.get(self.LO), t[:, 2:3], -1.0, MAGIC, ALU.mult, ALU.add).then_inc(step, 1)
        dve.wait_ge(step, 9)
        nc.vector.tensor_scalar(self.get(self.HI), self.get(self.LO), QMAX, None, ALU.add).then_inc(step, 1)

    DONE = 10

    def pool(self, nc, pool):
        pool.wait_ge(self.step, 1)
        nc.gpsimd.partition_all_reduce(self.all[:, :], self.mine[:, :], P, RMAX).then_inc(self.step, 1)



def cross0(nc, x_in, ctx, x_out, w, k, xq):
    H, HD, W, LEFT = 8, 8, 16, 8
    BH = 2 * H
    ON_POOL = (3, 7, 11, 15)
    ON_DVE = tuple(p for p in range(W) if p not in ON_POOL)
    NV, NP_, RV, RP = len(ON_DVE), len(ON_POOL), 4, 2
    SUM = 8
    SUMS, ADDS = W // SUM, SUM - 1
    with Scope(nc, "c0") as s:
        ident = s.sb("ident", [P, P])
        heads = s.sb("heads", [P, BH])
        m_half = s.sb("m_half", [P, 1])
        wts = s.sb("wts", [P, 4, P])
        bias = s.sb("bias", [P, 4])
        xt = s.sb("xt", [P, D])
        ct = s.sb("ct", [P, 2, D])
        xres = s.sb("xres", [P, D])
        q = s.sb("q", [P, D])
        kp = s.sb("kp", [P, D + W])
        vp = s.sb("vp", [P, 2, D + W])
        prod_v = s.sb("prod_v", [P, RV, D])
        prod_p = s.sb("prod_p", [P, RP, D])
        dots = s.sb("dots", [P, 4, W, BH])
        pr = s.sb("pr", [P, 4, W, BH])
        wide = s.sb("wide", [P, 2, 4, W, BH * HD])
        mx = s.sb("mx", [P, 4, BH])
        sm = s.sb("sm", [P, 4, BH])
        rs = s.sb("rs", [P, 4, BH])
        pv = s.sb("pv", [P, SUM, D])
        summed = s.sb("summed", [P, SUMS, D])
        norm = Norm(nc, s, ahead=1)

        ps_q = s.ps("ps_q", [P, D])
        ps_k = s.ps("ps_k", [P, D])
        ps_v = s.ps("ps_v", [P, D])
        ps_dots = s.ps("ps_dots", [P, 4, W, BH])
        ps_e = s.ps("ps_e", [P, 2, D])
        ps_y = s.ps("ps_y", [P, D])

        consts = s.sem("consts")
        padded = s.sem("padded")
        xt_in = s.sem("xt_in")
        ct_in = [s.sem(f"ct_in{n}") for n in range(2)]
        xres_in = s.sem("xres_in")
        q_done = s.sem("q_done")
        k_done = s.sem("k_done")
        v_done = s.sem("v_done")
        q_ready = s.sem("q_ready")
        k_ready = s.sem("k_ready")
        v_ready = s.sem("v_ready")
        prod_v_ready = s.sem("prod_v_ready")
        prod_p_ready = s.sem("prod_p_ready")
        prod_used = s.sem("prod_used")
        dots_ready = s.sem("dots_ready")
        mx_ready = s.sem("mx_ready")
        centred = s.sem("centred")
        exp_ready = s.sem("exp_ready")
        sum_ready = s.sem("sum_ready")
        inv_ready = s.sem("inv_ready")
        probs_ready = s.sem("probs_ready")
        wide_ready = s.sem("wide_ready")
        spread = s.sem("spread")
        pv_ready = s.sem("pv_ready")
        added = s.sem("added")
        sum_used = s.sem("sum_used")
        ends_ready = s.sem("ends_ready")

        N_CONST = 16 * 5

        with s.block() as block:

            @block.sync
            def _(sp):
                for dst, src in ((ident[:, :], k["ident"]), (heads[:, :], k["heads"]), (m_half[:, :], k["m_half"]),
                                 (wts[:, :, :], w["wts"]), (bias[:, :], w["bias"])):
                    sp.dma_start(dst, src).then_inc(consts, 16)

                def load_xt(turn):
                    if not (isinstance(turn, int) and turn == 1):
                        sp.wait_ge(q_done, turn - 1)
                    sp.dma_start(xt[:, :], rows(x_in, turn - 1)).then_inc(xt_in, 16)

                def load_ct(turn, n, free=True):
                    if free:
                        sp.wait_ge(v_done, turn - 2)
                    sp.dma_start(ct[:, n, :], rows(ctx, turn - 1)).then_inc(ct_in[n], 16)

                def load_xres(turn):
                    sp.wait_ge(norm.y_ready, turn)
                    sp.dma_start(xres[:, :], rows(x_in, turn - 1)).then_inc(xres_in, 16)

                load_xt(1)
                load_ct(1, 0, free=False)
                load_xt(2)
                load_ct(2, 1, free=False)
                load_xt(3)
                load_ct(3, 0)
                load_xres(1)
                with sp.Fori(0, NT // 2 - 2) as j:
                    for n in range(2):
                        t = 2 * j + n + 1
                        load_xt(t + 3)
                        load_ct(t + 3, 1 - n)
                        load_xres(t + 1)
                        norm.store(sp, x_out, t - 1, t)
                load_xt(NT)
                load_ct(NT, 1)
                for t in range(NT - 3, NT):
                    load_xres(t + 1)
                    norm.store(sp, x_out, t - 1, t)
                norm.store(sp, x_out, NT - 1, NT)
                sp.wait_ge(norm.stored, 16 * (NT + 1))

            @block.tensor
            def _(pe):
                def project_qk(turn, n, j):
                    pe.wait_ge(xt_in, turn * 16)
                    pe.matmul(ps_q[:, :], wts[:, 0, :], xt[:, :], start=True, stop=True).then_inc(q_done, 1)
                    pe.wait_ge(ct_in[n], j * 16)
                    pe.matmul(ps_k[:, :], wts[:, 1, :], ct[:, n, :], start=True, stop=True).then_inc(k_done, 1)

                def project_v(turn, n):
                    pe.wait_ge(v_ready, turn)
                    pe.matmul(ps_v[:, :], wts[:, 2, :], ct[:, n, :], start=True, stop=True).then_inc(v_done, 1)

                def score(turn, p):
                    if p == 0:
                        pe.wait_ge(centred, turn)
                    if p in ON_POOL:
                        m = ON_POOL.index(p)
                        src = prod_p[:, m % RP, :]
                        pe.wait_ge(prod_p_ready, (turn - 1) * NP_ + m + 1)
                    else:
                        m = ON_DVE.index(p)
                        src = prod_v[:, m % RV, :]
                        pe.wait_ge(prod_v_ready, (turn - 1) * NV + m + 1)
                    for t in range(4):
                        mm = pe.matmul(ps_dots[:, t, p, :], src[:, t * P:(t + 1) * P], heads[:, :], start=True, stop=True)
                    mm.then_inc(prod_used if p < W - 1 else dots_ready, 1)

                def out(turn, m):
                    if m == 0:
                        pe.wait_ge(norm.y_ready, turn)
                    pe.wait_ge(added, ((turn - 1) * SUMS + m + 2) * ADDS)
                    pe.matmul(ps_y[:, :], wts[:, 3, :], summed[:, m, :], start=m == 0, stop=m == SUMS - 1
                              ).then_inc(sum_used, 1)

                def attend(turn, n, scored=None, before=True):
                    for p in range(W):
                        if p % 4 == 0:
                            pe.wait_ge(wide_ready, turn * 4 + p // 4 + 1)
                        pe.wait_ge(pv_ready, turn * W + W - 1 + p)
                        for t in range(4):
                            mm = pe.transpose(ps_e[:, p % 2, t * P:(t + 1) * P], wide[:, n, t, p, :], ident[:, :])
                        mm.then_inc(spread, 1)
                        if scored is not None:
                            score(scored, p)
                        if p == 1 and before:
                            out(turn - 1, SUMS - 1)
                        if p == SUM + 3:
                            out(turn, 0)

                pe.wait_ge(consts, N_CONST)
                project_qk(1, 0, 1)
                project_v(1, 0)
                for p in range(W):
                    score(1, p)
                project_qk(2, 1, 1)
                for p in range(W):
                    score(2, p)
                def turn_of(t, n, j, before=True):
                    project_qk(t + 2, n, j + 2)
                    project_v(t + 1, 1 - n)
                    attend(t, n, t + 2, before)

                turn_of(1, 0, 0, before=False)
                turn_of(2, 1, 0)
                with pe.Fori(1, NT // 2 - 1) as j:
                    for n in range(2):
                        turn_of(2 * j + n + 1, n, j)
                project_v(NT, 1)
                attend(NT - 1, 0)
                attend(NT, 1)
                out(NT, SUMS - 1)

            @block.scalar
            def _(act):
                def evacuate_qk(turn):
                    act.wait_ge(q_done, turn)
                    act.wait_ge(dots_ready, turn)
                    nc.scalar.activation(q[:, :], ps_q[:, :], ACT.Identity, bias=bias[:, 0:1]).then_inc(q_ready, 1)
                    act.wait_ge(k_done, turn)
                    nc.scalar.activation(kp[:, LEFT:LEFT + D], ps_k[:, :], ACT.Identity, bias=bias[:, 1:2]).then_inc(k_ready, 1)

                def evacuate_v(turn, n):
                    act.wait_ge(v_done, turn)
                    act.wait_ge(pv_ready, turn * W)
                    nc.scalar.activation(vp[:, n, LEFT:LEFT + D], ps_v[:, :], ACT.Identity, bias=bias[:, 2:3]).then_inc(v_ready, 1)

                def exps(turn, n):
                    act.wait_ge(centred, turn + 1)
                    act.wait_ge(wide_ready, turn * 4)
                    nc.scalar.activation(pr[:, :, :, :], dots[:, :, :, :], ACT.Exp, scale=HD ** -0.5).then_inc(exp_ready, 1)
                    act.wait_ge(probs_ready, turn)
                    act.wait_ge(spread, turn * W)
                    for g in range(4):
                        nc.scalar.copy(
                            wide[:, n, :, 4 * g:4 * g + 4, :].rearrange("p t w (h d) -> p t (w h) d", d=HD),
                            pr[:, :, 4 * g:4 * g + 4, :].rearrange("p t w h -> p t (w h)").unsqueeze(3).broadcast_to(
                                [P, 4, 4 * BH, HD])).then_inc(wide_ready, 1)

                act.wait_ge(consts, N_CONST)
                act.wait_ge(padded, 1)
                evacuate_qk(1)
                evacuate_v(1, 0)
                evacuate_qk(2)
                exps(1, 0)
                with act.Fori(0, NT // 2 - 1) as j:
                    for n in range(2):
                        t = 2 * j + n + 1
                        evacuate_qk(t + 2)
                        evacuate_v(t + 1, 1 - n)
                        exps(t + 1, 1 - n)
                evacuate_v(NT, 1)
                exps(NT, 1)

            @block.vector
            def _(dve):
                def product(turn, p):
                    if p in ON_POOL or p >= W:
                        return
                    if p == 0:
                        dve.wait_ge(q_ready, turn)
                        dve.wait_ge(k_ready, turn)
                    m = ON_DVE.index(p)
                    if m >= RV:
                        dve.wait_ge(prod_used, (turn - 1) * (W - 1) + ON_DVE[m - RV] + 1)
                    nc.vector.tensor_tensor(prod_v[:, m % RV, :], q[:, :], kp[:, p:p + D], ALU.mult).then_inc(prod_v_ready, 1)

                def softmax_a(turn):
                    dve.wait_ge(dots_ready, turn + 1)
                    nc.vector.tensor_reduce(mx[:, :, :], ps_dots[:, :, :, :].rearrange("p t w h -> p t h w"), AX.X,
                                            ALU.max).then_inc(mx_ready, 1)
                    dve.wait_ge(mx_ready, turn)
                    nc.vector.tensor_tensor(dots[:, :, :, :], ps_dots[:, :, :, :],
                                            mx[:, :, :].unsqueeze(2).broadcast_to([P, 4, W, BH]), ALU.subtract
                                            ).then_inc(centred, 1)

                def softmax_b(turn):
                    dve.wait_ge(exp_ready, turn)
                    nc.vector.tensor_reduce(sm[:, :, :], pr[:, :, :, :].rearrange("p t w h -> p t h w"), AX.X,
                                            ALU.add).then_inc(sum_ready, 1)
                    dve.wait_ge(sum_ready, turn)
                    nc.vector.reciprocal(rs[:, :, :], sm[:, :, :]).then_inc(inv_ready, 1)
                    dve.wait_ge(inv_ready, turn)
                    nc.vector.tensor_tensor(pr[:, :, :, :], pr[:, :, :, :],
                                            rs[:, :, :].unsqueeze(2).broadcast_to([P, 4, W, BH]), ALU.mult
                                            ).then_inc(probs_ready, 1)

                def value(turn, n, p):
                    dve.wait_ge(spread, (turn + 1) * W + p + 1)
                    dve.wait_ge(added, ((turn - 1) * SUMS + p // SUM) * ADDS + max(p % SUM, 1))
                    nc.vector.tensor_tensor(pv[:, p % SUM, :], ps_e[:, p % 2, :], vp[:, n, p:p + D], ALU.mult).then_inc(pv_ready, 1)

                def residual(turn):
                    dve.wait_ge(sum_used, turn * SUMS + SUMS)
                    dve.wait_ge(xres_in, turn * 16)
                    nc.vector.scalar_tensor_tensor(norm.y[:, :], ps_y[:, :], bias[:, 3:4], xres[:, :], ALU.add, ALU.add
                                                   ).then_inc(norm.y_ready, 1)

                def ends(turn):
                    nc.vector.tensor_reduce(xq.ends[:, 0, bass.ds(turn - 1, 1)], norm.xn[:, :], AX.X, ALU.max)
                    nc.vector.tensor_reduce(xq.ends[:, 1, bass.ds(turn - 1, 1)], norm.xn[:, :], AX.X, ALU.min, negate=True
                                            ).then_inc(ends_ready, 1)

                def turn_of(t, n, before=True, soft=True, scored=True):
                    if soft:
                        softmax_a(t + 1)
                    if scored:
                        product(t + 2, 0)
                        product(t + 2, 1)
                    dve.wait_ge(v_ready, t + 1)
                    for p in range(W):
                        if scored:
                            product(t + 2, p + 2)
                        value(t, n, p)
                        if p == 2 and before:
                            residual(t - 1)
                        if p == 3 and before:
                            norm.moments(dve, t - 1)
                        if p == 5 and before:
                            norm.normed(dve, t - 1)
                            ends(t - 1)
                        if p == 7 and soft:
                            softmax_b(t + 1)

                nc.vector.memset(xq.ends[:, :, :], 0.0)
                nc.vector.memset(kp[:, :], 0.0)
                nc.vector.memset(vp[:, :, :], 0.0).then_inc(padded, 1)
                dve.sem_inc(norm.stored, 16)
                dve.sem_inc(norm.y_ready, 1)
                dve.sem_inc(centred, 1)
                dve.sem_inc(dots_ready, 1)
                dve.sem_inc(v_ready, 1)
                dve.sem_inc(wide_ready, 4)
                dve.sem_inc(spread, 2 * W)
                dve.sem_inc(pv_ready, 2 * W)
                dve.sem_inc(added, ADDS)
                dve.sem_inc(sum_used, SUMS)
                dve.wait_ge(padded, 1)
                for p in range(W):
                    product(1, p)
                softmax_a(1)
                for p in range(W):
                    product(2, p)
                    if p == 5:
                        softmax_b(1)
                turn_of(1, 0, before=False)
                turn_of(2, 1)
                with dve.Fori(1, NT // 2 - 1) as j:
                    for n in range(2):
                        turn_of(2 * j + n + 1, n)
                turn_of(NT - 1, 0, scored=False)
                turn_of(NT, 1, soft=False, scored=False)
                residual(NT)
                norm.vector(dve, NT)
                ends(NT)
                norm.end(dve)
                dve.wait_ge(ends_ready, NT)
                xq.vector(nc, dve)
                dve.wait_ge(xq.step, Quant.DONE)

            @block.gpsimd
            def _(pool):
                def product(turn, m):
                    if m == 0:
                        pool.wait_ge(q_ready, turn)
                        pool.wait_ge(k_ready, turn)
                    if m >= RP:
                        pool.wait_ge(prod_used, (turn - 1) * (W - 1) + ON_POOL[m - RP] + 1)
                    p = ON_POOL[m]
                    nc.gpsimd.tensor_tensor(prod_p[:, m % RP, :], q[:, :], kp[:, p:p + D], ALU.mult).then_inc(prod_p_ready, 1)

                def add(turn, p):
                    m, e = divmod(p, SUM)
                    pool.wait_ge(pv_ready, (turn + 1) * W + p + 1)
                    if e == 1:
                        pool.wait_ge(sum_used, (turn - 1) * SUMS + m + 1)
                    else:
                        pool.wait_ge(added, ((turn - 1) * SUMS + m + 1) * ADDS + e - 1)
                    a = pv[:, 0, :] if e == 1 else summed[:, m, :]
                    nc.gpsimd.tensor_tensor(summed[:, m, :], a, pv[:, e, :], ALU.add).then_inc(added, 1)

                def turn_of(t, before=True, scored=True):
                    for p in range(W):
                        if scored and p % 4 == 0:
                            product(t + 2, p // 4)
                        if p % SUM:
                            add(t, p)
                        if p == 3 and before:
                            norm.root(pool, t - 1, m_half)

                pool.wait_ge(consts, N_CONST)
                for turn in (1, 2):
                    for m in range(NP_):
                        product(turn, m)
                turn_of(1, before=False)
                turn_of(2)
                with pool.Fori(1, NT // 2 - 1) as j:
                    for n in range(2):
                        turn_of(2 * j + n + 1)
                turn_of(NT - 1, scored=False)
                turn_of(NT, scored=False)
                norm.root(pool, NT, m_half)
                xq.pool(nc, pool)



INTER = 1376
IT = (INTER + P - 1) // P
LAST = INTER - (IT - 1) * P
NG = ROWS // D


def tile_rows(it):
    return LAST if it == IT - 1 else P


def ffn0(nc, x_in, x_out, w_gate, w_up, w_down, up_scratch, k, xq):
    with Scope(nc, "f0") as s:
        ident = s.sb("ident", [P, P])
        m_half = s.sb("m_half", [P, 1])
        inner = s.sb("inner", [P, IT, ROWS])
        wd = s.sb("wd", [P, IT, D])
        gq, uq, sq, oq = (Quant(s, s, n, NG * IT) for n in ("gate", "up", "silu", "prod"))
        with Scope(nc, "f0w") as sw:
            wgu = sw.sb("wgu", [P, 2, DC, INTER])
            quantise_weights(nc, w_gate, w_up, w_down, k, ident, m_half, inner, wgu, wd, (gq, uq, sq, oq))
            gate_up(nc, x_in, up_scratch, ident, xq, wgu, inner, gq, uq, sq)
        product(nc, up_scratch, inner, uq, sq, oq)
        down0(nc, x_in, x_out, inner, wd, oq, m_half)


def quantise_weights(nc, w_gate, w_up, w_down, k, ident, m_half, inner, wgu, wd, quants):
    BLK = 32
    with Scope(nc, "f0q") as s:
        nat = s.sb("nat", [P, 2, INTER])
        rnd = s.sb("rnd", [P, 2, INTER])
        nb = 2 * DC * P // BLK
        big = s.sb("big", [P, 64])
        scale = s.sb("scale", [P, 64])
        inv = s.sb("inv", [P, 64])
        ps = s.ps("ps", [P, 2, 3 * D])
        consts = s.sem("consts")
        nat_in = [s.sem(f"nat_loaded{n}") for n in range(2)]
        step = s.sem("step")
        nat_used = s.sem("nat_used")
        rounded = s.sem("rounded")
        turned = s.sem("turned")
        kept = s.sem("kept")
        zeroed = s.sem("zeroed")
        GU, DN = IT, DC
        STEPS = 5

        with s.block() as block:

            @block.sync
            def _(sp):
                sp.dma_start(ident[:, :], k["ident"]).then_inc(consts, 16)
                sp.dma_start(m_half[:, :], k["m_half"]).then_inc(consts, 16)

                def load(n, r0, rows_, turn, down=False):
                    if down:
                        sp.dma_start(nat[0:rows_, n, :], w_down[r0:r0 + rows_, :] if isinstance(r0, int) else
                                     w_down[bass.ds(r0, rows_), :]).then_inc(nat_in[n], 16)
                    else:
                        for m, src in enumerate((w_gate, w_up)):
                            sp.dma_start(nat[0:rows_, n, m * D:m * D + D], src[bass.ds(r0, rows_), :]
                                         ).then_inc(nat_in[n], 16)

                load(0, 0, P, 1)
                load(1, P, P, 2)
                with sp.Fori(0, GU // 2 - 1) as j:
                    for n in range(2):
                        sp.wait_ge(nat_used, 2 * j + n + 1)
                        load(n, (2 * j + n + 2) * P, P, 0)
                sp.wait_ge(nat_used, GU - 2)
                load(0, (IT - 1) * P, LAST, GU)
                for d in range(DN):
                    sp.wait_ge(nat_used, GU - 1 + d)
                    load((GU + d) % 2, d * P, P, 0, down=True)

            def piece_counts(t):
                return sum(16 * (2 if u < GU else 1) for u in range(t % 2, t + 1, 2))

            @block.vector
            def _(dve):
                def piece(n, rows_, width, base, loaded):
                    nbk = width // BLK
                    src = nat[0:rows_, n, 0:width].rearrange("p (b e) -> p b e", e=BLK)
                    dst = rnd[0:rows_, n, 0:width].rearrange("p (b e) -> p b e", e=BLK)
                    flat = rnd[0:rows_, n, 0:width]
                    dve.wait_ge(nat_in[n], loaded)
                    nc.vector.tensor_reduce(big[0:rows_, 0:nbk], src, AX.X, ALU.max, apply_absolute_value=True).then_inc(step, 1)
                    dve.wait_ge(step, base + 1)
                    nc.vector.tensor_scalar(scale[0:rows_, 0:nbk], big[0:rows_, 0:nbk], 1.0 / 7.0, 1e-12, ALU.mult,
                                            ALU.max).then_inc(step, 1)
                    dve.wait_ge(step, base + 2)
                    nc.vector.reciprocal(inv[0:rows_, 0:nbk], scale[0:rows_, 0:nbk]).then_inc(step, 1)
                    dve.wait_ge(step, base + 3)
                    return src, dst, flat, nbk

                def rest(n, rows_, base, turn, src, dst, flat, nbk):
                    dve.wait_ge(turned, turn)
                    nc.vector.tensor_tensor(dst, src, inv[0:rows_, 0:nbk].unsqueeze(2).broadcast_to([rows_, nbk, BLK]),
                                            ALU.mult).then_inc(nat_used, 1)
                    dve.wait_ge(nat_used, turn)
                    nc.vector.tensor_scalar(flat, flat, MAGIC, MAGIC + 7.0, ALU.add, ALU.min).then_inc(step, 1)
                    dve.wait_ge(step, base + 4)
                    nc.vector.tensor_scalar(flat, flat, MAGIC - 8.0, MAGIC, ALU.max, ALU.subtract).then_inc(step, 1)
                    dve.wait_ge(step, base + 5)
                    nc.vector.tensor_tensor(dst, dst, scale[0:rows_, 0:nbk].unsqueeze(2).broadcast_to([rows_, nbk, BLK]),
                                            ALU.mult).then_inc(rounded, 1)

                for q in quants:
                    nc.vector.memset(q.ends[:, :, :], 0.0)
                nc.vector.memset(inner[96:P, IT - 1, :], 0.0).then_inc(zeroed, 1)
                dve.sem_inc(turned, 2)
                with dve.Fori(0, GU // 2) as j:
                    for n in range(2):
                        base = (2 * j + n) * STEPS
                        a = piece(n, P, 2 * D, base, 32 * j + 32)
                        rest(n, P, base, 2 * j + n + 1, *a)
                for t in range(GU - 1, GU + DN):
                    r, width = (LAST, 2 * D) if t < GU else (P, INTER)
                    a = piece(t % 2, r, width, t * STEPS, piece_counts(t))
                    rest(t % 2, r, t * STEPS, t + 1, *a)
                dve.wait_ge(zeroed, 1)

            @block.tensor
            def _(pe):
                def gate_up_piece(n, rows_, turn):
                    pe.wait_ge(rounded, turn)
                    pe.wait_ge(kept, turn)
                    for c in range(2 * DC):
                        mm = pe.transpose(ps[:, n, c * P:c * P + rows_], rnd[0:rows_, n, c * P:(c + 1) * P],
                                          ident[0:rows_, 0:rows_])
                    mm.then_inc(turned, 1)

                def down_piece(n, turn):
                    pe.wait_ge(rounded, turn)
                    pe.wait_ge(kept, turn)
                    for it in range(IT):
                        r = tile_rows(it)
                        mm = pe.transpose(ps[0:r, n, it * P:(it + 1) * P], rnd[:, n, it * P:it * P + r], ident[:, :])
                    mm.then_inc(turned, 1)

                pe.wait_ge(consts, 32)
                with pe.Fori(0, GU // 2) as j:
                    for n in range(2):
                        gate_up_piece(n, P, 2 * j + n + 1)
                gate_up_piece(0, LAST, GU)
                for t in range(GU, GU + DN):
                    down_piece(t % 2, t + 1)

            @block.scalar
            def _(act):
                def gate_up_piece(n, r0, rows_, turn):
                    act.wait_ge(turned, turn + 2)
                    nc.scalar.copy(wgu[:, :, :, bass.ds(r0, rows_)].rearrange("p m c r -> p (m c) r"),
                                   ps[:, n, 0:2 * DC * P].rearrange("p (c r) -> p c r", r=P)[:, :, 0:rows_]).then_inc(kept, 1)

                act.sem_inc(kept, 2)
                with act.Fori(0, GU // 2) as j:
                    for n in range(2):
                        gate_up_piece(n, (2 * j + n) * P, P, 2 * j + n + 1)
                gate_up_piece(0, (IT - 1) * P, LAST, GU)
                for d in range(DN):
                    t = GU + d
                    act.wait_ge(turned, t + 3)
                    nc.scalar.copy(wd[:, 0:IT - 1, d * P:(d + 1) * P],
                                   ps[:, t % 2, 0:(IT - 1) * P].rearrange("p (i r) -> p i r", r=P))
                    nc.scalar.copy(wd[0:LAST, IT - 1, d * P:(d + 1) * P],
                                   ps[0:LAST, t % 2, (IT - 1) * P:IT * P]).then_inc(kept, 1)
                act.wait_ge(kept, GU + DN + 2)


def gate_up(nc, x_in, up_scratch, ident, xq, wgu, inner, gq, uq, sq):
    SIG = 65536.0
    RU = 4
    with Scope(nc, "f0g") as s:
        xg = s.sb("xg", [P, 2, D])
        xr = s.sb("xr", [P, 2, D])
        xqT = s.sb("xqT", [P, DC, ROWS])
        up = s.sb("up", [P, RU, D])
        th = s.sb("th", [P, 2, D])
        ps_t = s.ps("ps_t", [P, 2, DC, P])
        ps_w = s.ps("ps_w", [P, 4, D])
        x_loaded = [s.sem(f"x_loaded{n}") for n in range(2)]
        x_step = s.sem("x_step")
        x_read = s.sem("x_read")
        x_rounded = s.sem("x_rounded")
        x_turned = s.sem("x_turned")
        xqT_ready = s.sem("xqT_ready")
        gate_done = s.sem("gate_done")
        gate_kept = s.sem("gate_kept")
        gate_ends = s.sem("gate_ends")
        up_done = s.sem("up_done")
        up_kept = s.sem("up_kept")
        up_ends = s.sem("up_ends")
        up_stored = [s.sem(f"up_stored{n}") for n in range(RU)]
        g_step = s.sem("g_step")
        g_ready = s.sem("g_ready")
        th_ready = s.sem("th_ready")
        silu_ready = s.sem("silu_ready")
        silu_ends = s.sem("silu_ends")
        N = NG * IT

        with s.block() as block:

            @block.sync
            def _(sp):
                for n in range(2):
                    sp.dma_start(xg[:, n, :], rows(x_in, n)).then_inc(x_loaded[n], 16)
                with sp.Fori(0, NT // 2 - 1) as j:
                    for n in range(2):
                        sp.wait_ge(x_read, 2 * j + n + 1)
                        sp.dma_start(xg[:, n, :], rows(x_in, 2 * j + n + 2)).then_inc(x_loaded[n], 16)
                with sp.Fori(0, NG) as g:
                    for it in range(IT):
                        r = tile_rows(it)
                        sp.wait_ge(up_kept, g * IT + it + 3)
                        sp.dma_start(up_scratch[it, 0:r, bass.ds(g * D, D)], up[0:r, it % RU, :]).then_inc(up_stored[it % RU], 16)
                for n in range(RU):
                    sp.wait_ge(up_stored[n], 16 * (NG * len(range(n, IT, RU)) + 1))

            @block.tensor
            def _(pe):
                with pe.Fori(0, NT // 2) as j:
                    for n in range(2):
                        turn = 2 * j + n + 1
                        pe.wait_ge(x_rounded, turn)
                        pe.wait_ge(xqT_ready, turn)
                        for c in range(DC):
                            mm = pe.transpose(ps_t[:, n, c, :], xr[:, n, c * P:(c + 1) * P], ident[:, :])
                        mm.then_inc(x_turned, 1)
                pe.wait_ge(xqT_ready, NT + 2)
                for m, done, kept in ((0, gate_done, gate_kept), (1, up_done, up_kept)):
                    with pe.Fori(0, NG) as g:
                        for it in range(IT):
                            r = tile_rows(it)
                            bank = 2 * m + it % 2
                            pe.wait_ge(kept, g * IT + it + (2 if it == 0 else 1))
                            for c in range(DC):
                                mm = pe.matmul(ps_w[0:r, bank, :], wgu[:, m, c, it * P:it * P + r],
                                               xqT[:, c, bass.ds(g * D, D)], start=c == 0, stop=c == DC - 1)
                            mm.then_inc(done, 1)

            @block.scalar
            def _(act):
                act.sem_inc(xqT_ready, 2)
                with act.Fori(0, NT // 2) as j:
                    for n in range(2):
                        turn = 2 * j + n + 1
                        act.wait_ge(x_turned, turn + 2)
                        nc.scalar.copy(xqT[:, :, bass.ds((turn - 1) * P, P)], ps_t[:, n, :, :]).then_inc(xqT_ready, 1)
                with act.Fori(0, NG) as g:
                    for it in range(IT):
                        r = tile_rows(it)
                        act.wait_ge(gate_done, g * IT + it + 1)
                        nc.scalar.copy(inner[0:r, it, bass.ds(g * D, D)], ps_w[0:r, it % 2, :]).then_inc(gate_kept, 1)
                with act.Fori(0, NG) as g:
                    for it in range(IT):
                        r = tile_rows(it)
                        u = g * IT + it
                        act.wait_ge(up_done, u + 1)
                        act.wait_ge(up_ends, u + 1 + (it < RU - 1))
                        act.wait_ge(up_stored[it % RU], 16 * (g * len(range(it % RU, IT, RU)) + it // RU + 1))
                        nc.scalar.copy(up[0:r, it % RU, :], ps_w[0:r, 2 + it % 2, :]).then_inc(up_kept, 1)
                        act.wait_ge(g_ready, u + 1)
                        act.wait_ge(silu_ready, u + 1 + (it == 0))
                        nc.scalar.activation(th[0:r, it % 2, :], inner[0:r, it, bass.ds(g * D, D)], ACT.Tanh,
                                             scale=0.5).then_inc(th_ready, 1)

            @block.vector
            def _(dve):
                with dve.Fori(0, NT // 2) as j:
                    for n in range(2):
                        turn = 2 * j + n + 1
                        dve.wait_ge(x_loaded[n], 16 * j + 16)
                        dve.wait_ge(x_turned, turn)
                        nc.vector.tensor_scalar(xr[:, n, :], xg[:, n, :], xq.get(1), MAGIC, ALU.mult, ALU.add).then_inc(x_read, 1)
                        dve.wait_ge(x_read, turn)
                        nc.vector.tensor_scalar(xr[:, n, :], xr[:, n, :], xq.get(2), xq.get(3), ALU.max, ALU.min).then_inc(x_step, 1)
                        dve.wait_ge(x_step, turn)
                        nc.vector.tensor_scalar(xr[:, n, :], xr[:, n, :], MAGIC, xq.get(0), ALU.subtract, ALU.mult
                                                ).then_inc(x_rounded, 1)
                with dve.Fori(0, NG) as g:
                    for it in range(IT):
                        r = tile_rows(it)
                        u = g * IT + it
                        dve.wait_ge(gate_kept, u + 3)
                        part = inner[0:r, it, bass.ds(g * D, D)]
                        nc.vector.tensor_reduce(gq.ends[0:r, 0, bass.ds(u, 1)], part, AX.X, ALU.max)
                        nc.vector.tensor_reduce(gq.ends[0:r, 1, bass.ds(u, 1)], part, AX.X, ALU.min, negate=True).then_inc(gate_ends, 1)
                dve.wait_ge(gate_ends, N)
                gq.vector(nc, dve)
                dve.wait_ge(gq.step, Quant.DONE)

                with dve.Fori(0, NG) as g:
                    def first(it):
                        r = tile_rows(it)
                        u = g * IT + it
                        part = inner[0:r, it, bass.ds(g * D, D)]
                        nc.vector.tensor_scalar(part, part, gq.get(1)[0:r], MAGIC, ALU.mult, ALU.add).then_inc(g_step, 1)
                        dve.wait_ge(g_step, 5 * u + 1)
                        nc.vector.tensor_scalar(part, part, gq.get(2)[0:r], gq.get(3)[0:r], ALU.max, ALU.min).then_inc(g_step, 1)
                        dve.wait_ge(g_step, 5 * u + 2)
                        nc.vector.tensor_scalar(part, part, MAGIC, gq.get(0)[0:r], ALU.subtract, ALU.mult).then_inc(g_ready, 1)
                        dve.wait_ge(g_ready, u + 1)
                        dve.wait_ge(up_kept, u + 3)
                        nc.vector.tensor_reduce(uq.ends[0:r, 0, bass.ds(u, 1)], up[0:r, it % RU, :], AX.X, ALU.max)
                        nc.vector.tensor_reduce(uq.ends[0:r, 1, bass.ds(u, 1)], up[0:r, it % RU, :], AX.X, ALU.min,
                                                negate=True).then_inc(up_ends, 1)

                    def second(it):
                        r = tile_rows(it)
                        u = g * IT + it
                        part = inner[0:r, it, bass.ds(g * D, D)]
                        t = th[0:r, it % 2, :]
                        dve.wait_ge(th_ready, u + 1)
                        nc.vector.tensor_scalar(t, t, SIG / 2, SIG / 2 + MAGIC, ALU.mult, ALU.add).then_inc(g_step, 1)
                        dve.wait_ge(g_step, 5 * u + 3)
                        nc.vector.tensor_scalar(t, t, MAGIC + QMAX, MAGIC, ALU.min, ALU.subtract).then_inc(g_step, 1)
                        dve.wait_ge(g_step, 5 * u + 4)
                        nc.vector.scalar_tensor_tensor(part, t, 1.0 / SIG, part, ALU.mult, ALU.mult).then_inc(silu_ready, 1)
                        dve.wait_ge(silu_ready, u + 3)
                        nc.vector.tensor_reduce(sq.ends[0:r, 0, bass.ds(u, 1)], part, AX.X, ALU.max)
                        nc.vector.tensor_reduce(sq.ends[0:r, 1, bass.ds(u, 1)], part, AX.X, ALU.min, negate=True).then_inc(g_step, 1)

                    for it in range(IT):
                        first(it)
                        second(it)
                dve.wait_ge(g_step, 5 * N)
                uq.vector(nc, dve)
                sq.vector(nc, dve)
                dve.wait_ge(uq.step, Quant.DONE)
                dve.wait_ge(sq.step, Quant.DONE)

            @block.gpsimd
            def _(pool):
                pool.sem_inc(x_turned, 2)
                pool.sem_inc(gate_kept, 2)
                pool.sem_inc(up_kept, 2)
                pool.sem_inc(up_ends, RU)
                pool.sem_inc(silu_ready, 2)
                for n in range(RU):
                    pool.sem_inc(up_stored[n], 16)
                gq.pool(nc, pool)
                uq.pool(nc, pool)
                sq.pool(nc, pool)


def product(nc, up_scratch, inner, uq, sq, oq):
    C = 1024
    PER = ROWS // C
    with Scope(nc, "f0p") as s:
        up = s.sb("up", [P, 2, PER, C])
        up_in = [s.sem(f"up_in{n}") for n in range(2)]
        up_read = s.sem("up_read")
        u_step = s.sem("u_step")
        held = s.sem("held")
        u_ready = s.sem("u_ready")
        g_step = s.sem("g_step")
        ends = s.sem("ends")
        done = s.sem("done")

        with s.block() as block:

            @block.sync
            def _(sp):
                def load(n, it, r):
                    sp.dma_start(up[0:r, n, :, :].rearrange("p h c -> p (h c)"),
                                 up_scratch[bass.ds(it, 1), 0:r, :].rearrange("o p c -> (o p) c")).then_inc(up_in[n], 16)

                load(0, 0, P)
                load(1, 1, P)
                with sp.Fori(0, (IT - 1) // 2 - 1) as j:
                    for n in range(2):
                        sp.wait_ge(done, PER * (2 * j + n + 1))
                        load(n, 2 * j + n + 2, P)
                sp.wait_ge(done, PER * (IT - 2))
                load(0, IT - 1, LAST)

            def each(loop_engine, body):
                with loop_engine.Fori(0, (IT - 1) // 2) as j:
                    for n in range(2):
                        for h in range(PER):
                            body(n, 2 * j + n, P, h, (2 * j + n) * PER + h, j + 1)
                for h in range(PER):
                    body(0, IT - 1, LAST, h, (IT - 1) * PER + h, (IT - 1) // 2 + 1)

            @block.gpsimd
            def _(pool):
                def body(n, it, r, h, u, loads):
                    part = up[0:r, n, h, :]
                    wait_apart(pool, up_in[n], loads * 16, held)
                    nc.gpsimd.tensor_scalar(part, part, uq.get(1)[0:r], MAGIC, ALU.mult, ALU.add).then_inc(u_step, 1)
                    wait_apart(pool, u_step, 2 * u + 1, held)
                    nc.gpsimd.tensor_scalar(part, part, uq.get(3)[0:r], uq.get(2)[0:r], ALU.min, ALU.max).then_inc(u_step, 1)
                    wait_apart(pool, u_step, 2 * u + 2, held)
                    nc.gpsimd.tensor_scalar(part, part, -MAGIC, uq.get(0)[0:r], ALU.add, ALU.mult).then_inc(u_ready, 1)
                each(pool, body)
                pool.wait_ge(held, 3 * IT * PER)
                oq.pool(nc, pool)

            @block.vector
            def _(dve):
                def body(n, it, r, h, u, loads):
                    part = inner[0:r, bass.ds(it, 1), h * C:(h + 1) * C].rearrange("p o c -> p (o c)")
                    nc.vector.tensor_scalar(part, part, sq.get(1)[0:r], MAGIC, ALU.mult, ALU.add).then_inc(g_step, 1)
                    dve.wait_ge(g_step, 3 * u + 1)
                    nc.vector.tensor_scalar(part, part, sq.get(2)[0:r], sq.get(3)[0:r], ALU.max, ALU.min).then_inc(g_step, 1)
                    dve.wait_ge(g_step, 3 * u + 2)
                    nc.vector.tensor_scalar(part, part, MAGIC, sq.get(0)[0:r], ALU.subtract, ALU.mult).then_inc(g_step, 1)
                    dve.wait_ge(g_step, 3 * u + 3)
                    dve.wait_ge(u_ready, u + 1)
                    nc.vector.tensor_tensor(part, part, up[0:r, n, h, :], ALU.mult).then_inc(done, 1)
                    dve.wait_ge(done, u + 1)
                    nc.vector.tensor_reduce(oq.ends[0:r, 0, bass.ds(u, 1)], part, AX.X, ALU.max)
                    nc.vector.tensor_reduce(oq.ends[0:r, 1, bass.ds(u, 1)], part, AX.X, ALU.min, negate=True).then_inc(ends, 1)
                each(dve, body)
                dve.wait_ge(ends, IT * PER)
                oq.vector(nc, dve)
                dve.wait_ge(oq.step, Quant.DONE)


def down0(nc, x_in, x_out, inner, wd, oq, m_half):
    with Scope(nc, "f0d") as s:
        xres = s.sb("xres", [P, D])
        o = s.sb("o", [P, 2, IT, P])
        norm = Norm(nc, s, ahead=2)
        ps_y = s.ps("ps_y", [P, 2, D])
        xres_in = s.sem("xres_in")
        o_step = s.sem("o_step")
        o_ready = s.sem("o_ready")
        y_done = s.sem("y_done")

        with s.block() as block:

            @block.sync
            def _(sp):
                sp.dma_start(xres[:, :], rows(x_in, 0)).then_inc(xres_in, 16)
                with sp.Fori(0, NT - 1) as i:
                    sp.wait_ge(norm.y_ready, i + 3)
                    sp.dma_start(xres[:, :], rows(x_in, i + 1)).then_inc(xres_in, 16)
                    norm.store(sp, x_out, i, i + 1)
                norm.store(sp, x_out, NT - 1, NT)
                sp.wait_ge(norm.stored, 16 * (NT + 1))

            @block.tensor
            def _(pe):
                with pe.Fori(0, NT // 2) as j:
                    for n in range(2):
                        turn = 2 * j + n + 1
                        pe.wait_ge(o_ready, turn)
                        pe.wait_ge(norm.y_ready, turn)
                        for it in range(IT):
                            r = tile_rows(it)
                            mm = pe.matmul(ps_y[:, n, :], o[0:r, n, it, :], wd[0:r, it, :], start=it == 0, stop=it == IT - 1)
                        mm.then_inc(y_done, 1)

            @block.vector
            def _(dve):
                def round_(turn, n):
                    part = inner[:, :, bass.ds((turn - 1) * P, P)]
                    dve.wait_ge(y_done, turn)
                    nc.vector.tensor_scalar(o[:, n, :, :], part, oq.get(1), MAGIC, ALU.mult, ALU.add).then_inc(o_step, 1)
                    dve.wait_ge(o_step, 2 * turn - 1)
                    nc.vector.tensor_scalar(o[:, n, :, :], o[:, n, :, :], oq.get(2), oq.get(3), ALU.max, ALU.min).then_inc(o_step, 1)
                    dve.wait_ge(o_step, 2 * turn)
                    nc.vector.tensor_scalar(o[:, n, :, :], o[:, n, :, :], MAGIC, oq.get(0), ALU.subtract, ALU.mult
                                            ).then_inc(o_ready, 1)

                def finish(turn, n):
                    dve.wait_ge(xres_in, turn * 16)
                    dve.wait_ge(y_done, turn + 2)
                    nc.vector.tensor_tensor(norm.y[:, :], ps_y[:, n, :], xres[:, :], ALU.add).then_inc(norm.y_ready, 1)
                    norm.vector(dve, turn)

                dve.sem_inc(norm.stored, 16)
                dve.sem_inc(y_done, 2)
                dve.sem_inc(norm.y_ready, 2)
                round_(1, 0)
                with dve.Fori(0, NT // 2 - 1) as j:
                    round_(2 * j + 2, 1)
                    finish(2 * j + 1, 0)
                    round_(2 * j + 3, 0)
                    finish(2 * j + 2, 1)
                round_(NT, 1)
                finish(NT - 1, 0)
                finish(NT, 1)
                norm.end(dve)

            @block.gpsimd
            def _(pool):
                with pool.Fori(0, NT) as i:
                    norm.root(pool, i + 1, m_half)



NH1, NKV1, HD1, LAT = 32, 8, 128, 32
STEP = 256
NS = ROWS // STEP


def latent1(nc, x_in, x_out, w, lat_scratch, k):
    with Scope(nc, "a1") as s:
        ident = s.sb("ident", [P, P])
        wq = s.sb("wq", [P, DC, NH1 * HD1])
        wo = s.sb("wo", [P, NH1, D])
        wku = s.sb("wku", [P, 2, NKV1 * HD1])
        wvu = s.sb("wvu", [P, 2, NKV1 * HD1])
        wq_in = s.sem("wq_in")
        wo_in = s.sem("wo_in")
        latents(nc, x_in, w, lat_scratch, k, ident, (wq, wo, wku, wvu), (wq_in, wo_in))
        attend1(nc, x_in, x_out, lat_scratch, k, ident, (wq, wo, wku, wvu), (wq_in, wo_in))


def latents(nc, x_in, w, lat_scratch, k, ident, weights, loaded):
    with Scope(nc, "l1") as s:
        wdn = s.sb("wdn", [P, DC, 2 * NKV1 * LAT])
        xt = s.sb("xt", [P, 4, D])
        xT = s.sb("xT", [P, DC, D])
        lat = s.sb("lat", [P, 2, 4, D])
        ps_t = s.ps("ps_t", [P, 2, DC, P])
        ps_c = s.ps("ps_c", [P, 4, D])
        small_in = s.sem("small_in")
        xt_in = s.sem("xt_in")
        x_turned = s.sem("x_turned")
        xT_ready = s.sem("xT_ready")
        c_done = s.sem("c_done")
        moved_act = s.sem("moved_act")
        moved_dve = s.sem("moved_dve")
        stored = [s.sem(f"stored{n}") for n in range(2)]
        wq, wo, wku, wvu = weights

        def move(copy, t, n):
            kv = t // 2
            for quad in range(4):
                h = 4 * (t % 2) + quad
                for j in range(8):
                    to = 32 * (2 * (j % 2) + kv)
                    ins = copy(
                        lat[to:to + 32, n, j // 2, :].rearrange("p (b h m) -> p b h m", h=8, m=8)[:, :, h, :],
                        ps_c[32 * quad:32 * quad + 32, t, :].rearrange("p (b m j) -> p b m j", m=8, j=8)[:, :, :, j])
            return ins

        with s.block() as block:

            @block.sync
            def _(sp):
                sp.dma_start(ident[:, :], k["ident"]).then_inc(small_in, 16)
                sp.dma_start(wdn[:, :, :], w["down"].rearrange("(c p) n -> p c n", p=P)).then_inc(small_in, 16)

                def load(g):
                    sp.dma_start(xt[:, :, :], x_in[bass.ds(g * D, D), :].rearrange("(t p) n -> p t n", p=P)).then_inc(xt_in, 16)

                load(0)
                sp.dma_start(wku[:, :, :], w["k_up"].rearrange("(c p) n -> p c n", p=P)).then_inc(loaded[0], 16)
                sp.dma_start(wvu[:, :, :], w["v_up"].rearrange("(c p) n -> p c n", p=P)).then_inc(loaded[0], 16)
                for c in range(DC):
                    sp.dma_start(wq[:, c, :], w["q"][c * P:(c + 1) * P, :]).then_inc(loaded[0], 16)
                for c in range(4):
                    sp.dma_start(wo[:, 8 * c:8 * c + 8, :], w["o"].rearrange("(h p) n -> p h n", p=P)[:, 8 * c:8 * c + 8, :]
                                 ).then_inc(loaded[1], 16)
                for g in range(NG):
                    if g + 1 < NG:
                        sp.wait_ge(x_turned, 4 * g + 4)
                        load(g + 1)
                    sp.wait_ge(moved_act, g + 1)
                    sp.wait_ge(moved_dve, g + 1)
                    sp.dma_start(lat_scratch[:, :, g * D:(g + 1) * D], lat[:, g % 2, :, :]).then_inc(stored[g % 2], 16)
                for n in range(2):
                    sp.wait_ge(stored[n], 16 * NG // 2)

            @block.tensor
            def _(pe):
                pe.wait_ge(small_in, 32)
                with pe.Fori(0, NG) as g:
                    pe.wait_ge(xt_in, 16 * g + 16)
                    for t in range(4):
                        pe.wait_ge(xT_ready, 4 * g + t + 1)
                        for c in range(DC):
                            mm = pe.transpose(ps_t[:, t % 2, c, :], xt[:, t, c * P:(c + 1) * P], ident[:, :])
                        mm.then_inc(x_turned, 1)
                    pe.wait_ge(xT_ready, 4 * g + 6)
                    pe.wait_ge(moved_act, g)
                    pe.wait_ge(moved_dve, g)
                    for t in range(4):
                        for c in range(DC):
                            mm = pe.matmul(ps_c[:, t, :], wdn[:, c, t * P:(t + 1) * P], xT[:, c, :],
                                           start=c == 0, stop=c == DC - 1)
                        mm.then_inc(c_done, 1)

            @block.scalar
            def _(act):
                act.sem_inc(xT_ready, 2)
                for g in range(NG):
                    for t in range(4):
                        act.wait_ge(x_turned, 4 * g + t + 1)
                        act.wait_ge(c_done, 4 * g)
                        nc.scalar.copy(xT[:, :, t * P:(t + 1) * P], ps_t[:, t % 2, :, :]).then_inc(xT_ready, 1)
                    if g >= 2:
                        act.wait_ge(stored[g % 2], 16 * (g // 2))
                    for t in (0, 2):
                        act.wait_ge(c_done, 4 * g + t + 1)
                        ins = move(nc.scalar.copy, t, g % 2)
                    ins.then_inc(moved_act, 1)

            @block.vector
            def _(dve):
                for g in range(NG):
                    if g >= 2:
                        dve.wait_ge(stored[g % 2], 16 * (g // 2))
                    for t in (1, 3):
                        dve.wait_ge(c_done, 4 * g + t + 1)
                        ins = move(nc.vector.tensor_copy, t, g % 2)
                    ins.then_inc(moved_dve, 1)


def attend1(nc, x_in, x_out, lat_scratch, k, ident, weights, loaded):
    G, R = NKV1, NH1 // NKV1
    BB = STEP // S
    USES = 2 + 4 + 3 * G
    with Scope(nc, "m1") as s:
        causal = s.sb("causal", [P, S])
        m_half = s.sb("m_half", [P, 1])
        xt = s.sb("xt", [P, 2, D])
        xres = s.sb("xres", [P, 2, D])
        xT = s.sb("xT", [P, DC, STEP])
        lat = s.sb("lat", [P, 4, STEP])
        qT = s.sb("qT", [P, 2, BB, R, S])
        kT = s.sb("kT", [P, 2, STEP])
        v = s.sb("v", [P, 2, G * HD1])
        sc = s.sb("sc", [P, 2 * BB, S])
        pr = s.sb("pr", [P, 2 * BB, S])
        mx = s.sb("mx", [P, 2 * BB])
        sm = s.sb("sm", [P, 2 * BB])
        rs = s.sb("rs", [P, 2 * BB])
        pT = s.sb("pT", [P, 2, 2, P])
        aT = s.sb("aT", [P, R, BB, S])
        norm = Norm(nc, s, ahead=2)
        ps_w = s.ps("ps_w", [P, 2, D])
        ps_s = s.ps("ps_s", [P, 2, BB, S])
        ps_p = s.ps("ps_p", [P, 2, 2, P])
        ps_o = s.ps("ps_o", [P, 2, BB // 2, R * S])
        ps_y = s.ps("ps_y", [P, 2, D])
        consts = s.sem("consts")
        xt_in = s.sem("xt_in")
        xres_in = s.sem("xres_in")
        lat_in = s.sem("lat_in")
        w_done = s.sem("w_done")
        w_kept = s.sem("w_kept")
        scores_ready = s.sem("scores_ready")
        masked = s.sem("masked")
        mx_ready = s.sem("mx_ready")
        centred = s.sem("centred")
        exp_ready = s.sem("exp_ready")
        sum_ready = s.sem("sum_ready")
        inv_ready = s.sem("inv_ready")
        probs_ready = s.sem("probs_ready")
        turned = s.sem("turned")
        pT_ready = s.sem("pT_ready")
        o_done = s.sem("o_done")
        aT_ready = s.sem("aT_ready")
        used = s.sem("used")
        wq, wo, wku, wvu = weights

        with s.block() as block:

            @block.sync
            def _(sp):
                sp.dma_start(causal[:, :], k["causal"]).then_inc(consts, 16)
                sp.dma_start(m_half[:, :], k["m_half"]).then_inc(consts, 16)

                def pair(dram, i):
                    return dram[bass.ds(i * STEP, STEP), :].rearrange("(t p) n -> p t n", p=P)

                sp.dma_start(xt[:, :, :], pair(x_in, 0)).then_inc(xt_in, 16)
                sp.dma_start(lat[:, :, :], lat_scratch[:, :, 0:STEP]).then_inc(lat_in, 16)
                sp.dma_start(xres[:, :, :], pair(x_in, 0)).then_inc(xres_in, 16)

                def stores(i):
                    for t in range(2):
                        norm.store(sp, x_out, 2 * i + t, 2 * i + t + 1)

                with sp.Fori(0, NS - 1) as i:
                    sp.wait_ge(w_done, i * USES + USES)
                    sp.dma_start(xt[:, :, :], pair(x_in, i + 1)).then_inc(xt_in, 16)
                    sp.dma_start(lat[:, :, :], lat_scratch[:, :, bass.ds((i + 1) * STEP, STEP)]).then_inc(lat_in, 16)
                    stores(i)
                    sp.dma_start(xres[:, :, :], pair(x_in, i + 1)).then_inc(xres_in, 16)
                stores(NS - 1)
                sp.wait_ge(norm.stored, 16 * (NT + 1))

            @block.tensor
            def _(pe):
                with pe.Fori(0, NS) as i:
                    use = [0]

                    def bank():
                        n = use[0]
                        use[0] += 1
                        pe.wait_ge(w_kept, i * USES + n + 1)
                        return ps_w[:, n % 2, :]

                    pe.wait_ge(xt_in, 16 * i + 16)
                    for t in range(2):
                        b = bank()
                        for c in range(DC):
                            mm = pe.transpose(b[:, c * P:(c + 1) * P], xt[:, t, c * P:(c + 1) * P], ident[:, :])
                        mm.then_inc(w_done, 1)
                    pe.wait_ge(lat_in, 16 * i + 16)
                    for t in range(2):
                        for h in range(2):
                            b = bank()
                            for f in range(2):
                                mm = pe.matmul(b, lat[:, 2 + f, t * P:(t + 1) * P], wvu[:, f, h * D:(h + 1) * D],
                                               start=f == 0, stop=f == 1)
                            mm.then_inc(w_done, 1)

                    def prepare(g):
                        for rp in range(2):
                            b = bank()
                            for r in range(2):
                                h = R * g + 2 * rp + r
                                for c in range(DC):
                                    mm = pe.matmul(b[:, r * STEP:(r + 1) * STEP], wq[:, c, h * HD1:(h + 1) * HD1],
                                                   xT[:, c, :], start=c == 0, stop=c == DC - 1)
                            mm.then_inc(w_done, 1)
                        b = bank()
                        for f in range(2):
                            mm = pe.matmul(b[:, 0:STEP], wku[:, f, g * HD1:(g + 1) * HD1], lat[:, f, :],
                                           start=f == 0, stop=f == 1)
                        mm.then_inc(w_done, 1)

                    pe.wait_ge(w_kept, i * USES + 4)
                    prepare(0)
                    for g in range(G):
                        unit = i * G + g + 1
                        pe.wait_ge(w_kept, i * USES + 6 + 3 * (g + 1) + 2)
                        for bb in range(BB):
                            for rp in range(2):
                                mm = pe.matmul(ps_s[:, rp, bb, :],
                                               qT[:, g % 2, bb, 2 * rp:2 * rp + 2, :].rearrange("p r q -> p (r q)"),
                                               kT[:, g % 2, bb * S:(bb + 1) * S], start=True, stop=True)
                        mm.then_inc(scores_ready, 1)
                        if g + 1 < G:
                            prepare(g + 1)
                        pe.wait_ge(probs_ready, unit)
                        for t in range(2):
                            for rp in range(2):
                                mm = pe.transpose(ps_p[:, t, rp, :],
                                                  pr[:, BB * rp + 2 * t:BB * rp + 2 * t + 2, :].rearrange("p b k -> p (b k)"),
                                                  ident[:, :])
                        mm.then_inc(turned, 1)
                        pe.wait_ge(pT_ready, unit)
                        for bb in range(BB):
                            at = slice(64 * (bb % 2), 64 * (bb % 2) + 64)
                            mm = pe.matmul(ps_o[:, bb % 2, bb // 2, :], v[at, bb // 2, g * HD1:(g + 1) * HD1],
                                           pT[at, bb // 2, :, :].rearrange("p r q -> p (r q)"), start=True, stop=True)
                        mm.then_inc(o_done, 1)
                        pe.wait_ge(aT_ready, unit)
                        if g == 0:
                            pe.wait_ge(norm.y_ready, 2 * i + 2)
                        for t in range(2):
                            for r in range(R):
                                mm = pe.matmul(ps_y[:, t, :], aT[:, r, 2 * t:2 * t + 2, :].rearrange("p b q -> p (b q)"),
                                               wo[:, R * g + r, :], start=g == 0 and r == 0, stop=g == G - 1 and r == R - 1)
                        mm.then_inc(used, 1)

            @block.scalar
            def _(act):
                act.sem_inc(w_kept, 2)
                with act.Fori(0, NS) as i:
                    use = [0]

                    def keep(dst, src):
                        n = use[0]
                        use[0] += 1
                        act.wait_ge(w_done, i * USES + n + 1)
                        nc.scalar.copy(dst, src(ps_w[:, n % 2, :])).then_inc(w_kept, 1)

                    for t in range(2):
                        keep(xT[:, :, t * P:(t + 1) * P], lambda b: b.rearrange("p (c r) -> p c r", c=DC))
                    for t in range(2):
                        for h in range(2):
                            keep(v[:, t, h * D:(h + 1) * D], lambda b: b)

                    def prepare(g):
                        for rp in range(2):
                            keep(qT[:, g % 2, :, 2 * rp:2 * rp + 2, :].rearrange("p b r q -> p r b q"),
                                 lambda b: b.rearrange("p (r b q) -> p r b q", r=2, q=S))
                        keep(kT[:, g % 2, :], lambda b: b[:, 0:STEP])

                    prepare(0)
                    for g in range(G):
                        unit = i * G + g + 1
                        act.wait_ge(centred, unit)
                        nc.scalar.activation(pr[:, :, :], sc[:, :, :], ACT.Exp, scale=HD1 ** -0.5).then_inc(exp_ready, 1)
                        if g + 1 < G:
                            prepare(g + 1)
                        act.wait_ge(turned, unit)
                        nc.scalar.copy(pT[:, :, :, :], ps_p[:, :, :, :]).then_inc(pT_ready, 1)
                        act.wait_ge(o_done, unit)
                        act.wait_ge(used, unit)
                        for e in range(2):
                            ins = nc.scalar.copy(aT[:, :, e::2, :].rearrange("p r t q -> p t r q"),
                                                 ps_o[:, e, :, :].rearrange("p t (r q) -> p t r q", r=R))
                        ins.then_inc(aT_ready, 1)

            @block.vector
            def _(dve):
                dve.sem_inc(norm.stored, 16)
                dve.sem_inc(norm.y_ready, 2)
                dve.sem_inc(used, 1)
                dve.wait_ge(consts, 32)
                n = 2 * BB
                with dve.Fori(0, NS) as i:
                    for g in range(G):
                        unit = i * G + g + 1
                        dve.wait_ge(scores_ready, unit)
                        nc.vector.tensor_tensor(sc[:, :, :], ps_s[:, :, :, :].rearrange("p r b k -> p (r b) k"),
                                                causal[:, :].unsqueeze(1).broadcast_to([P, n, S]), ALU.add).then_inc(masked, 1)
                        dve.wait_ge(masked, unit)
                        nc.vector.tensor_reduce(mx[:, :], sc[:, :, :], AX.X, ALU.max).then_inc(mx_ready, 1)
                        dve.wait_ge(mx_ready, unit)
                        nc.vector.tensor_tensor(sc[:, :, :], sc[:, :, :], mx[:, :].unsqueeze(2).broadcast_to([P, n, S]),
                                                ALU.subtract).then_inc(centred, 1)
                        dve.wait_ge(exp_ready, unit)
                        nc.vector.tensor_reduce(sm[:, :], pr[:, :, :], AX.X, ALU.add).then_inc(sum_ready, 1)
                        dve.wait_ge(sum_ready, unit)
                        nc.vector.reciprocal(rs[:, :], sm[:, :]).then_inc(inv_ready, 1)
                        dve.wait_ge(inv_ready, unit)
                        nc.vector.tensor_tensor(pr[:, :, :], pr[:, :, :], rs[:, :].unsqueeze(2).broadcast_to([P, n, S]),
                                                ALU.mult).then_inc(probs_ready, 1)
                    dve.wait_ge(xres_in, 16 * i + 16)
                    dve.wait_ge(used, i * G + G + 1)
                    for t in range(2):
                        nc.vector.tensor_tensor(norm.y[:, :], ps_y[:, t, :], xres[:, t, :], ALU.add).then_inc(norm.y_ready, 1)
                        norm.vector(dve, 2 * i + t + 1)
                norm.end(dve)

            @block.gpsimd
            def _(pool):
                pool.wait_ge(consts, 32)
                with pool.Fori(0, NT) as i:
                    norm.root(pool, i + 1, m_half)



def cross1(nc, x_in, ctx, x_out, w, k):
    NP2 = 4
    NB = D // P
    with Scope(nc, "c1") as s:
        ident = s.sb("ident", [P, P])
        m_half = s.sb("m_half", [P, 1])
        same_head = s.sb("same_head", [P, P])
        seqs = s.sb("seqs", [P, 2])
        w3 = s.sb("w3", [P, 3, D])
        wo = s.sb("wo", [P, NP2, S])
        bo_g = s.sb("bo_g", [P, 2])
        xt = s.sb("xt", [P, D])
        ct = s.sb("ct", [P, D])
        xres = s.sb("xres", [P, D])
        qd = s.sb("qd", [P, NB, D])
        qs = s.sb("qs", [P, NB, D])
        qmx = s.sb("qmx", [P, NB, 8])
        qsm = s.sb("qsm", [P, NB, 8])
        qrs = s.sb("qrs", [P, NB, 8])
        kmx = s.sb("kmx", [P, NP2])
        ksm = s.sb("ksm", [P, NP2])
        krs = s.sb("krs", [P, NP2])
        ek = s.sb("ek", [P, NP2, D])
        ekT = s.sb("ekT", [P, NB, D])
        vT = s.sb("vT", [P, NB, D])
        cT = s.sb("cT", [P, NP2, P])
        m = s.sb("m", [P, NP2, S])
        qT = s.sb("qT", [P, NP2, D])
        fo = s.sb("fo", [P, D])
        gf = s.sb("gf", [P, D])
        sq = s.sb("sq", [P, D])
        nn = s.sb("nn", [P, NB * 2])
        rn = s.sb("rn", [P, NB * 2])
        rw = s.sb("rw", [P, NB, 2, S])
        m_half8 = s.sb("m_half8", [P, NB * 2])
        norm = Norm(nc, s)
        ps_w = s.ps("ps_w", [P, 4, D])
        ps_c = s.ps("ps_c", [P, NP2, P])
        ps_m = s.ps("ps_m", [P, D])
        ps_f = s.ps("ps_f", [P, D])
        ps_n = s.ps("ps_n", [P, D])
        consts = s.sem("consts")
        xt_in = s.sem("xt_in")
        ct_in = s.sem("ct_in")
        xres_in = s.sem("xres_in")
        q_done = s.sem("q_done")
        qmx_ready = s.sem("qmx_ready")
        q_centred = s.sem("q_centred")
        q_exp = s.sem("q_exp")
        q_sum = s.sem("q_sum")
        q_inv = s.sem("q_inv")
        q_ready = s.sem("q_ready")
        k_done = s.sem("k_done")
        kmx_ready = s.sem("kmx_ready")
        ek_ready = s.sem("ek_ready")
        k_inv = s.sem("k_inv")
        v_done = s.sem("v_done")
        v_kept = s.sem("v_kept")
        k_turned = s.sem("k_turned")
        ekT_ready = s.sem("ekT_ready")
        c_done = s.sem("c_done")
        cT_ready = s.sem("cT_ready")
        m_done = s.sem("m_done")
        m_ready = s.sem("m_ready")
        q_turned = s.sem("q_turned")
        qT_ready = s.sem("qT_ready")
        f_done = s.sem("f_done")
        fo_ready = s.sem("fo_ready")
        sq_ready = s.sem("sq_ready")
        n_done = s.sem("n_done")
        nn_ready = s.sem("nn_ready")
        rn_ready = s.sem("rn_ready")
        rw_ready = s.sem("rw_ready")
        r_turned = s.sem("r_turned")
        gf_ready = s.sem("gf_ready")
        scaled = s.sem("scaled")
        CONSTS = (("ident", ident), ("m_half", m_half), ("same_head", same_head), ("seqs", seqs), ("m_half8", m_half8))
        N_CONST = 16 * (len(CONSTS) + 3)

        with s.block() as block:

            @block.sync
            def _(sp):
                for name, dst in CONSTS:
                    sp.dma_start(dst[:, :], k[name]).then_inc(consts, 16)
                sp.dma_start(w3[:, :, :], w["qkv"]).then_inc(consts, 16)
                sp.dma_start(wo[:, :, :], w["o"]).then_inc(consts, 16)
                sp.dma_start(bo_g[:, :], w["bo_g"]).then_inc(consts, 16)
                sp.dma_start(xt[:, :], rows(x_in, 0)).then_inc(xt_in, 16)
                sp.dma_start(ct[:, :], rows(ctx, 0)).then_inc(ct_in, 16)
                sp.dma_start(xres[:, :], rows(x_in, 0)).then_inc(xres_in, 16)
                with sp.Fori(0, NT - 1) as i:
                    sp.wait_ge(q_done, 8 * i + 8)
                    sp.dma_start(xt[:, :], rows(x_in, i + 1)).then_inc(xt_in, 16)
                    sp.wait_ge(v_done, 8 * i + 8)
                    sp.dma_start(ct[:, :], rows(ctx, i + 1)).then_inc(ct_in, 16)
                    sp.wait_ge(norm.y_ready, i + 1)
                    sp.dma_start(xres[:, :], rows(x_in, i + 1)).then_inc(xres_in, 16)
                    norm.store(sp, x_out, i, i + 1)
                norm.store(sp, x_out, NT - 1, NT)
                sp.wait_ge(norm.stored, 16 * (NT + 1))

            @block.tensor
            def _(pe):
                pe.wait_ge(consts, N_CONST)
                with pe.Fori(0, NT) as i:
                    for b in range(2):
                        at = slice(64 * b, 64 * b + 64)
                        seq = 2 * i + b
                        if b == 0:
                            pe.wait_ge(xt_in, 16 * i + 16)
                        for n in range(NB):
                            pe.wait_ge(qT_ready, 4 * seq + n + 1)
                            pe.matmul(ps_w[:, n, :], xt[at, n * P:(n + 1) * P], w3[at, 0, :], start=True, stop=True
                                      ).then_inc(q_done, 1)
                        if b == 0:
                            pe.wait_ge(ct_in, 16 * i + 16)
                        for n in range(NP2):
                            pe.wait_ge(q_centred, 4 * seq + n + 1)
                            pe.matmul(ps_w[:, n, :], w3[at, 1, n * P:(n + 1) * P], ct[at, :], start=True, stop=True
                                      ).then_inc(k_done, 1)
                        for n in range(NB):
                            pe.wait_ge(ek_ready, 4 * seq + n + 1)
                            pe.matmul(ps_w[:, n, :], ct[at, n * P:(n + 1) * P], w3[at, 2, :], start=True, stop=True
                                      ).then_inc(v_done, 1)
                        for n in range(NP2):
                            pe.wait_ge(v_kept, 4 * seq + n + 1)
                            for t in range(NB):
                                mm = pe.transpose(ps_w[:, n, t * P:(t + 1) * P], ek[:, n, t * P:(t + 1) * P], ident[:, :])
                            mm.then_inc(k_turned, 1)
                        for n in range(NP2):
                            pe.wait_ge(ekT_ready, 4 * seq + n + 1)
                            if n == 0:
                                pe.wait_ge(cT_ready, seq + 1)
                            for t in range(NB):
                                mm = pe.matmul(ps_c[:, n, :], vT[:, t, n * P:(n + 1) * P], ekT[:, t, n * P:(n + 1) * P],
                                               start=t == 0, stop=t == NB - 1)
                        mm.then_inc(c_done, 1)
                        pe.wait_ge(cT_ready, seq + 2)
                        for n in range(NP2):
                            mm = pe.matmul(ps_m[:, n * S:(n + 1) * S], cT[:, n, :], wo[:, n, :], start=True, stop=True)
                        mm.then_inc(m_done, 1)
                        for n in range(NP2):
                            pe.wait_ge(q_ready, 4 * seq + 4)
                            for t in range(NB):
                                mm = pe.transpose(ps_w[:, n, t * P:(t + 1) * P], qs[:, t, n * P:(n + 1) * P], ident[:, :])
                            mm.then_inc(q_turned, 1)
                        pe.wait_ge(m_ready, seq + 1)
                        for n in range(NP2):
                            pe.wait_ge(qT_ready, 4 * seq + n + 5)
                            mm = pe.matmul(ps_f[at, :], m[:, n, :], qT[:, n, :], start=n == 0, stop=n == NP2 - 1,
                                           tile_position=(0, 64 * b))
                        mm.then_inc(f_done, 1)
                    pe.wait_ge(sq_ready, i + 1)
                    for t in range(NB):
                        mm = pe.matmul(ps_n[:, 2 * t:2 * t + 2], sq[:, t * P:(t + 1) * P], seqs[:, :], start=True, stop=True)
                    mm.then_inc(n_done, 1)
                    pe.wait_ge(rw_ready, i + 1)
                    for t in range(NB):
                        mm = pe.transpose(ps_n[:, t * P:(t + 1) * P], rw[:, t, :, :].rearrange("p b c -> p (b c)"), ident[:, :])
                    mm.then_inc(r_turned, 1)
                    pe.wait_ge(scaled, i + 1)

            @block.scalar
            def _(act):
                act.wait_ge(consts, N_CONST)
                with act.Fori(0, NT) as i:
                    for b in range(2):
                        seq = 2 * i + b
                        for n in range(NB):
                            act.wait_ge(q_centred, 4 * seq + n + 1)
                            nc.scalar.activation(qs[:, n, :], qd[:, n, :], ACT.Exp).then_inc(q_exp, 1)
                        for n in range(NP2):
                            act.wait_ge(kmx_ready, 4 * seq + n + 1)
                            nc.scalar.activation(ek[:, n, :], ps_w[:, n, :], ACT.Exp, bias=kmx[:, n:n + 1],
                                                 accum_out=ksm[:, n:n + 1]).then_inc(ek_ready, 1)
                        for n in range(NB):
                            act.wait_ge(v_done, 4 * seq + n + 1)
                            nc.scalar.copy(vT[:, n, :], ps_w[:, n, :]).then_inc(v_kept, 1)
                        for n in range(NP2):
                            act.wait_ge(k_turned, 4 * seq + n + 1)
                            nc.scalar.copy(ekT[:, :, n * P:(n + 1) * P],
                                           ps_w[:, n, :].rearrange("p (t d) -> p t d", t=NB)).then_inc(ekT_ready, 1)
                        for n in range(NP2):
                            act.wait_ge(q_turned, 4 * seq + n + 1)
                            nc.scalar.copy(qT[:, n, :], ps_w[:, n, :]).then_inc(qT_ready, 1)
                    act.wait_ge(f_done, 2 * i + 2)
                    nc.scalar.activation(fo[:, :], ps_f[:, :], ACT.Identity, bias=bo_g[:, 0:1]).then_inc(fo_ready, 1)
                    act.wait_ge(rn_ready, i + 1)
                    nc.scalar.copy(rw[:, :, :, :], rn[:, :].rearrange("p (t b) -> p t b", b=2).unsqueeze(3).broadcast_to(
                        [P, NB, 2, S])).then_inc(rw_ready, 1)

            @block.vector
            def _(dve):
                dve.sem_inc(norm.stored, 16)
                dve.sem_inc(cT_ready, 1)
                dve.sem_inc(qT_ready, 4)
                dve.wait_ge(consts, N_CONST)
                with dve.Fori(0, NT) as i:
                    for b in range(2):
                        seq = 2 * i + b
                        for n in range(NB):
                            dve.wait_ge(q_done, 4 * seq + n + 1)
                            src = ps_w[:, n, :].rearrange("p (h d) -> p h d", h=8)
                            nc.vector.tensor_reduce(qmx[:, n, :], src, AX.X, ALU.max).then_inc(qmx_ready, 1)
                            dve.wait_ge(qmx_ready, 4 * seq + n + 1)
                            nc.vector.tensor_tensor(qd[:, n, :].rearrange("p (h d) -> p h d", h=8), src,
                                                    qmx[:, n, :].unsqueeze(2).broadcast_to([P, 8, S]), ALU.subtract
                                                    ).then_inc(q_centred, 1)
                        for n in range(NP2):
                            dve.wait_ge(k_done, 4 * seq + n + 1)
                            nc.vector.tensor_reduce(kmx[:, n:n + 1], ps_w[:, n, :], AX.X, ALU.max, negate=True).then_inc(kmx_ready, 1)
                        dve.wait_ge(q_exp, 4 * seq + 4)
                        nc.vector.tensor_reduce(qsm[:, :, :], qs[:, :, :].rearrange("p t (h d) -> p t h d", h=8), AX.X,
                                                ALU.add).then_inc(q_sum, 1)
                        dve.wait_ge(q_sum, seq + 1)
                        nc.vector.reciprocal(qrs[:, :, :], qsm[:, :, :]).then_inc(q_inv, 1)
                        dve.wait_ge(q_inv, seq + 1)
                        for n in range(NB):
                            part = qs[:, n, :].rearrange("p (h d) -> p h d", h=8)
                            nc.vector.tensor_tensor(part, part, qrs[:, n, :].unsqueeze(2).broadcast_to([P, 8, S]), ALU.mult
                                                    ).then_inc(q_ready, 1)
                        dve.wait_ge(ek_ready, 4 * seq + 4)
                        nc.vector.reciprocal(krs[:, :], ksm[:, :]).then_inc(k_inv, 1)
                        dve.wait_ge(c_done, seq + 1)
                        nc.vector.tensor_tensor(cT[:, :, :], ps_c[:, :, :], same_head[:, :].unsqueeze(1).broadcast_to([P, NP2, P]),
                                                ALU.mult).then_inc(cT_ready, 1)
                        dve.wait_ge(m_done, seq + 1)
                        dve.wait_ge(k_inv, seq + 1)
                        nc.vector.scalar_tensor_tensor(m[:, :, :], ps_m[:, 0:NP2 * S].rearrange("p (n c) -> p n c", n=NP2),
                                                       S ** -0.5, krs[:, :].unsqueeze(2).broadcast_to([P, NP2, S]),
                                                       ALU.mult, ALU.mult).then_inc(m_ready, 1)
                    dve.wait_ge(fo_ready, i + 1)
                    nc.vector.tensor_tensor(sq[:, :], fo[:, :], fo[:, :], ALU.mult).then_inc(sq_ready, 1)
                    nc.vector.tensor_scalar(gf[:, :], fo[:, :], bo_g[:, 1:2], float(np.sqrt(S)), ALU.mult, ALU.mult).then_inc(gf_ready, 1)
                    dve.wait_ge(n_done, i + 1)
                    nc.vector.tensor_scalar(nn[:, :], ps_n[:, 0:NB * 2], 1e-24, None, ALU.max).then_inc(nn_ready, 1)
                    dve.wait_ge(r_turned, i + 1)
                    dve.wait_ge(gf_ready, i + 1)
                    nc.vector.tensor_tensor(gf[:, :], ps_n[:, :], gf[:, :], ALU.mult).then_inc(scaled, 1)
                    dve.wait_ge(scaled, i + 1)
                    dve.wait_ge(xres_in, 16 * i + 16)
                    nc.vector.tensor_tensor(norm.y[:, :], gf[:, :], xres[:, :], ALU.add).then_inc(norm.y_ready, 1)
                    norm.vector(dve, i + 1)
                norm.end(dve)

            @block.gpsimd
            def _(pool):
                pool.wait_ge(consts, N_CONST)
                with pool.Fori(0, NT) as i:
                    pool.wait_ge(nn_ready, i + 1)
                    nc.gpsimd.tensor_tensor(rn[:, :], nn[:, :], m_half8[:, :], ALU.pow).then_inc(rn_ready, 1)
                    norm.root(pool, i + 1, m_half)



def ffn1(nc, x_in, out, w, k):
    with Scope(nc, "f1") as s:
        ident = s.sb("ident", [P, P])
        m_half = s.sb("m_half", [P, 1])
        wg = s.sb("wg", [P, DC, INTER])
        wu = s.sb("wu", [P, DC, INTER])
        wd = s.sb("wd", [P, IT, D])
        unpack(nc, w, k, ident, m_half, (wg, wu, wd))
        swiglu(nc, x_in, out, ident, m_half, wg, wu, wd)


def unpack(nc, w, k, ident, m_half, weights):
    with Scope(nc, "f1u") as s:
        nibble = s.sb("nibble", [P, 1], I32)
        q = s.sb("q", [P, 2, IT * D], I32)
        zeros = s.sb("zeros", [P, 2, IT * D // 8], I32)
        z = s.sb("z", [P, 2, IT * D], I32)
        scale = s.sb("scale", [P, 2, IT * D], F16)
        consts = s.sem("consts")
        w_in = [s.sem(f"w_in{n}") for n in range(2)]
        q_ready = s.sem("q_ready")
        z_ready = s.sem("z_ready")
        diff = s.sem("diff")
        done = s.sem("done")
        mats = (("gate", DC, INTER), ("up", DC, INTER), ("down", IT, D))
        LOADS = (4, 4, 6)

        with s.block() as block:

            @block.sync
            def _(sp):
                sp.dma_start(ident[:, :], k["ident"]).then_inc(consts, 16)
                sp.dma_start(m_half[:, :], k["m_half"]).then_inc(consts, 16)
                sp.dma_start(nibble[:, :], k["nibble"]).then_inc(consts, 16)
                for i, (name, kt, n) in enumerate(mats):
                    b = i % 2
                    if i >= 2:
                        sp.wait_ge(done, i - 1)
                    qw = w[f"{name}_q"]
                    for t in range(kt):
                        r = min(P // 8, qw.shape[0] - t * P // 8)
                        src = qw[t * P // 8:t * P // 8 + r, :].unsqueeze(1).broadcast_to([r, 8, n])
                        sp.dma_start(q[0:8 * r, b, t * n:(t + 1) * n], src).then_inc(w_in[b], 16)
                    zs = w[f"{name}_z"].rearrange("g n -> (g n)").unsqueeze(0).broadcast_to([P, kt * n // 8])
                    sp.dma_start(zeros[:, b, 0:kt * n // 8], zs).then_inc(w_in[b], 16)
                    ss = w[f"{name}_s"].rearrange("g n -> (g n)").unsqueeze(0).broadcast_to([P, kt * n])
                    sp.dma_start(scale[:, b, 0:kt * n], ss).then_inc(w_in[b], 16)

            @block.vector
            def _(dve):
                dve.wait_ge(consts, 48)
                count = [0, 0]
                for i, (name, kt, n) in enumerate(mats):
                    b = i % 2
                    count[b] += 16 * (kt + 2)
                    dve.wait_ge(w_in[b], count[b])
                    parts = [(P, 0, kt * n)] if name != "down" else [(P, 0, (kt - 1) * n), (LAST, (kt - 1) * n, kt * n)]
                    for r, lo, hi in parts:
                        qp = q[0:r, b, lo:hi]
                        last = nc.vector.tensor_scalar(qp, qp, nibble[0:r, :], 15, ALU.logical_shift_right, ALU.bitwise_and)
                    last.then_inc(q_ready, 1)
                    zv = z[:, b, 0:kt * n].rearrange("p (m j) -> p m j", j=8)
                    for j in range(8):
                        last = nc.vector.tensor_scalar(zv[:, :, j], zeros[:, b, 0:kt * n // 8], 4 * j, 15,
                                                       ALU.logical_shift_right, ALU.bitwise_and)
                    last.then_inc(z_ready, 1)
                    dve.wait_ge(q_ready, i + 1)
                    dve.wait_ge(z_ready, i + 1)
                    dst = weights[i]
                    for r, lo, hi in parts:
                        out = dst[0:r, :, :].rearrange("p t n -> p (t n)")[:, lo:hi]
                        last = nc.vector.scalar_tensor_tensor(out, q[0:r, b, lo:hi], 1.0, z[0:r, b, lo:hi], ALU.subtract,
                                                              ALU.subtract)
                    last.then_inc(diff, 1)
                    dve.wait_ge(diff, i + 1)
                    for r, lo, hi in parts:
                        out = dst[0:r, :, :].rearrange("p t n -> p (t n)")[:, lo:hi]
                        last = nc.vector.tensor_tensor(out, out, scale[0:r, b, lo:hi], ALU.mult)
                    last.then_inc(done, 1)


def swiglu(nc, x_in, out, ident, m_half, wg, wu, wd):
    with Scope(nc, "f1m") as s:
        xt = s.sb("xt", [P, 4, D])
        xres = s.sb("xres", [P, 4, D])
        xT = s.sb("xT", [P, DC, D])
        th = s.sb("th", [P, 2, D])
        t1 = s.sb("t1", [P, 2, D])
        h = s.sb("h", [P, IT, D])
        y16 = s.sb("y16", [P, 2, D], F16)
        norm = Norm(nc, s, ahead=2)
        ps_t = s.ps("ps_t", [P, 2, DC, P])
        ps_g = s.ps("ps_g", [P, 2, D])
        ps_u = s.ps("ps_u", [P, 2, D])
        ps_y = s.ps("ps_y", [P, 2, D])
        xt_in = s.sem("xt_in")
        xres_in = s.sem("xres_in")
        x_turned = s.sem("x_turned")
        xT_ready = s.sem("xT_ready")
        g_done = s.sem("g_done")
        u_done = s.sem("u_done")
        th_ready = s.sem("th_ready")
        t1_ready = s.sem("t1_ready")
        h_ready = s.sem("h_ready")
        y_done = s.sem("y_done")
        y_kept = s.sem("y_kept")

        with s.block() as block:

            @block.sync
            def _(sp):
                def group(g):
                    return x_in[bass.ds(g * D, D), :].rearrange("(t p) n -> p t n", p=P)

                sp.dma_start(xt[:, :, :], group(0)).then_inc(xt_in, 16)
                sp.dma_start(xres[:, :, :], group(0)).then_inc(xres_in, 16)
                with sp.Fori(0, NG - 1) as g:
                    sp.wait_ge(x_turned, 4 * g + 4)
                    sp.dma_start(xt[:, :, :], group(g + 1)).then_inc(xt_in, 16)
                    for t in range(4):
                        norm.store(sp, out, 4 * g + t, 4 * g + t + 1)
                    sp.dma_start(xres[:, :, :], group(g + 1)).then_inc(xres_in, 16)
                for t in range(4):
                    norm.store(sp, out, 4 * (NG - 1) + t, 4 * (NG - 1) + t + 1)
                sp.wait_ge(norm.stored, 16 * (NT + 1))

            @block.tensor
            def _(pe):
                with pe.Fori(0, NG) as g:
                    pe.wait_ge(xt_in, 16 * g + 16)
                    for t in range(4):
                        pe.wait_ge(xT_ready, 4 * g + t + 1)
                        for c in range(DC):
                            mm = pe.transpose(ps_t[:, t % 2, c, :], xt[:, t, c * P:(c + 1) * P], ident[:, :])
                        mm.then_inc(x_turned, 1)
                    pe.wait_ge(xT_ready, 4 * g + 6)
                    for it in range(IT):
                        r = tile_rows(it)
                        u = g * IT + it
                        pe.wait_ge(t1_ready, u + 1 + (it == 0))
                        for c in range(DC):
                            mm = pe.matmul(ps_g[0:r, it % 2, :], wg[:, c, it * P:it * P + r], xT[:, c, :],
                                           start=c == 0, stop=c == DC - 1)
                        mm.then_inc(g_done, 1)
                        pe.wait_ge(h_ready, u + 1 + (it == 0))
                        for c in range(DC):
                            mm = pe.matmul(ps_u[0:r, it % 2, :], wu[:, c, it * P:it * P + r], xT[:, c, :],
                                           start=c == 0, stop=c == DC - 1)
                        mm.then_inc(u_done, 1)
                    for t in range(4):
                        pe.wait_ge(y_kept, 4 * g + t + 1)
                        for it in range(IT):
                            r = tile_rows(it)
                            if t == 0:
                                pe.wait_ge(h_ready, g * IT + it + 3)
                            mm = pe.matmul(ps_y[:, t % 2, :], h[0:r, it, t * P:(t + 1) * P], wd[0:r, it, :],
                                           start=it == 0, stop=it == IT - 1)
                        mm.then_inc(y_done, 1)

            @block.scalar
            def _(act):
                act.sem_inc(xT_ready, 2)
                act.sem_inc(y_kept, 2)
                with act.Fori(0, NG) as g:
                    for t in range(4):
                        act.wait_ge(x_turned, 4 * g + t + 1)
                        nc.scalar.copy(xT[:, :, t * P:(t + 1) * P], ps_t[:, t % 2, :, :]).then_inc(xT_ready, 1)
                    for it in range(IT):
                        r = tile_rows(it)
                        act.wait_ge(g_done, g * IT + it + 1)
                        nc.scalar.activation(th[0:r, it % 2, :], ps_g[0:r, it % 2, :], ACT.Tanh, scale=0.5).then_inc(th_ready, 1)
                    for t in range(4):
                        act.wait_ge(y_done, 4 * g + t + 1)
                        act.wait_ge(norm.y_ready, 4 * g + t + 1)
                        nc.scalar.copy(y16[:, t % 2, :], ps_y[:, t % 2, :]).then_inc(y_kept, 1)

            @block.vector
            def _(dve):
                dve.sem_inc(norm.stored, 16)
                dve.sem_inc(t1_ready, 2)
                dve.sem_inc(h_ready, 2)
                dve.sem_inc(norm.y_ready, 2)
                with dve.Fori(0, NG) as g:
                    for it in range(IT):
                        r = tile_rows(it)
                        u = g * IT + it
                        if it == 0:
                            dve.wait_ge(y_done, 4 * g)
                        dve.wait_ge(th_ready, u + 1)
                        nc.vector.scalar_tensor_tensor(t1[0:r, it % 2, :], th[0:r, it % 2, :], 1.0, ps_g[0:r, it % 2, :],
                                                       ALU.add, ALU.mult).then_inc(t1_ready, 1)
                        dve.wait_ge(t1_ready, u + 3)
                        dve.wait_ge(u_done, u + 1)
                        nc.vector.scalar_tensor_tensor(h[0:r, it, :], t1[0:r, it % 2, :], 0.5, ps_u[0:r, it % 2, :],
                                                       ALU.mult, ALU.mult).then_inc(h_ready, 1)
                    dve.wait_ge(xres_in, 16 * g + 16)
                    for t in range(4):
                        dve.wait_ge(y_kept, 4 * g + t + 3)
                        nc.vector.tensor_tensor(norm.y[:, :], y16[:, t % 2, :], xres[:, t, :], ALU.add).then_inc(norm.y_ready, 1)
                        norm.vector(dve, 4 * g + t + 1)
                norm.end(dve)

            @block.gpsimd
            def _(pool):
                with pool.Fori(0, NT) as i:
                    norm.root(pool, i + 1, m_half)



def program(nc, t, w, k, out):
    x = t["x"]
    ctx = t["ctx_4096"]
    stage = [x] + [nc.dram_tensor(f"x_after_{n}", (ROWS, D), F32).ap() for n in range(1, 6)] + [out]
    with Scope(nc, "keep") as keep:
        xq = Quant(keep, keep, "xq", NT)
        attention0(nc, stage[0], stage[1], t["L0_attn_Wq"], t["L0_attn_Wk"], t["L0_attn_Wv"], t["L0_attn_Wo"], k)
        cross0(nc, stage[1], ctx, stage[2], w["cross0"], k, xq)
        up_scratch = nc.dram_tensor("up_scratch", (IT, P, ROWS), F32).ap()
        ffn0(nc, stage[2], stage[3], t["L0_ffn_w_gate"], t["L0_ffn_w_up"], t["L0_ffn_w_down"], up_scratch, k, xq)
        lat_scratch = nc.dram_tensor("lat_scratch", (P, 4, ROWS), F32).ap()
        latent1(nc, stage[3], stage[4], w["latent1"], lat_scratch, k)
        cross1(nc, stage[4], ctx, stage[5], w["cross1"], k)
        ffn1(nc, stage[5], stage[6], w["ffn1"], k)


def constants():
    pos = np.tile(np.arange(S, dtype=np.float32), 2)
    freq = (1.0 / np.float32(10000.0) ** (np.arange(0, 16, 2, dtype=np.float32) / 16)).astype(np.float32)
    ang = (pos[:, None] * freq[None, :]).astype(np.float32)
    sin = np.stack([-np.sin(ang), np.sin(ang)], -1).reshape(P, 16)
    p = np.arange(P)
    return {
        "ident": np.eye(P, dtype=np.float32),
        "cos": np.repeat(np.cos(ang), 2, axis=1).astype(np.float32),
        "sin": sin.astype(np.float32),
        "causal": np.where(np.arange(S)[None, :] > (p % S)[:, None], NEG, 0.0).astype(np.float32),
        "half_mask": ((p % 32 // 16)[:, None] == np.arange(2)[None, :]).astype(np.float32),
        "m_half": np.full((P, 1), -0.5, np.float32),
        "m_half8": np.full((P, 8), -0.5, np.float32),
        "same_head": ((p // 64)[:, None] == (p // 64)[None, :]).astype(np.float32),
        "seqs": ((p // 64)[:, None] == np.arange(2)[None, :]).astype(np.float32),
        "nibble": (4 * (p % 8)).astype(np.int32)[:, None],
        "heads": ((p // 8)[:, None] == np.arange(16)[None, :]).astype(np.float32),
    }


def twice(w):
    out = np.zeros((P, P), w.dtype)
    out[:S, :S] = out[S:, S:] = w.T
    return out


def kernel(**inputs):
    import concourse.bacc as bacc
    from concourse.bass_utils import run_bass_kernel_spmd

    nc = bacc.Bacc("TRN2", target_bir_lowering=False, num_devices=1)
    arrays = {}

    def given(name, a):
        a = np.ascontiguousarray(a)
        arrays[name] = a
        return nc.dram_tensor(name, a.shape, mybir.dt.from_np(a.dtype), kind="ExternalInput").ap()

    g = {n: np.asarray(a) for n, a in inputs.items()}
    t = {n: given(f"in_{n}", g[n].reshape(ROWS, D)) for n in ("x", "ctx_4096")}
    for n in ("L0_attn_Wq", "L0_attn_Wk", "L0_attn_Wv", "L0_attn_Wo"):
        t[n] = given(f"in_{n}", g[n])
    for n in ("L0_ffn_w_gate", "L0_ffn_w_up", "L0_ffn_w_down"):
        t[n] = given(f"in_{n}", g[n])
    w = {"cross0": {
        "wts": given("in_cross0_weights", np.stack([twice(g[f"L0_xattn_W{n}"]) for n in "qkvo"], 1)),
        "bias": given("in_cross0_biases", np.stack([np.tile(g[f"L0_xattn_b{n}"], 2) for n in "qkvo"], 1)),
    }}
    w["latent1"] = {
        "q": given("in_latent1_q", g["L1_attn_Wq"].T),
        "down": given("in_latent1_down", np.concatenate([g["L1_attn_Wk_down"].T, g["L1_attn_Wv_down"].T], 1)),
        "k_up": given("in_latent1_k_up", g["L1_attn_Wk_up"].T),
        "v_up": given("in_latent1_v_up", g["L1_attn_Wv_up"].T),
        "o": given("in_latent1_o", g["L1_attn_Wo"].T),
    }
    both = lambda a: np.concatenate([a, a], 0)
    w["cross1"] = {
        "qkv": given("in_cross1_qkv", both(np.stack([g[f"L1_xattn_W{n}"].T for n in "qkv"], 1))),
        "o": given("in_cross1_o", g["L1_xattn_Wo"].T.reshape(4, P, S).transpose(1, 0, 2)),
        "bo_g": given("in_cross1_bo_g", both(np.stack([g["L1_xattn_bo"], g["L1_xattn_g"].reshape(S)], 1))),
    }
    w["ffn1"] = {f"{m}_{c}": given(f"in_ffn1_{m}_{c}", g[f"L1_ffn_{m}_{n}"])
                 for m in ("gate", "up", "down") for c, n in (("q", "qweight"), ("z", "zeros"), ("s", "scales"))}
    k = {n: given(f"const_{n}", a) for n, a in constants().items()}
    out = nc.dram_tensor("out_dram", (ROWS, D), F32, kind="ExternalOutput").ap()
    program(nc, t, w, k, out)
    r = run_bass_kernel_spmd(nc, [arrays], core_ids=[0])
    return r.results[0]["out_dram"].reshape(B, S, D)
```

```python
from contextlib import ExitStack

import numpy as np

import concourse.bass as bass
from concourse import mybir

ALU = mybir.AluOpType
ACT = mybir.ActivationFunctionType
AX = mybir.AxisListType
F32 = mybir.dt.float32
F16 = mybir.dt.float16
I32 = mybir.dt.int32
RMAX = bass.bass_isa.ReduceOp.max

P = 128
B, S, D = 32, 64, 512
ROWS = B * S
NT = ROWS // P
DC = D // P
EPS = 1e-5
NEG = -1e30
PARTS = ((0, 0), (0, 1), (1, 0))
SPLIT = 64.0




def split_high(nc, out, src):
    return nc.scalar.activation(out, src, ACT.Copy, scale=SPLIT)


def split_low(nc, out, src, high):
    return nc.vector.scalar_tensor_tensor(out, src, SPLIT, high, ALU.mult, ALU.subtract)


class Scope:

    def __init__(self, nc, name):
        self.nc, self.name, self.stack, self.sems = nc, name, ExitStack(), []

    def __enter__(self):
        self.stack.__enter__()
        return self

    def __exit__(self, *a):
        if self.sems and a[0] is None:
            self.nc.clear_and_free_semaphores(self.sems)
            self.nc.all_engine_barrier()
        return self.stack.__exit__(*a)

    def sb(self, name, shape, dt=F32):
        return self.stack.enter_context(self.nc.sbuf_tensor(f"{self.name}_{name}", shape, dt))

    def ps(self, name, shape):
        return self.stack.enter_context(self.nc.psum_tensor(f"{self.name}_{name}", shape, F32))

    def sem(self, name):
        self.sems.append(self.nc.alloc_semaphore(f"{self.name}_{name}"))
        return self.sems[-1]

    def block(self):
        return self.nc.Block()


def wait_apart(eng, sem, turn, held):
    eng.wait_ge(sem, turn)
    eng.sem_inc(held, 1)


class Norm:

    def __init__(self, nc, s, ahead=0):
        self.nc = nc
        self.ahead = ahead
        self.y = s.sb("y", [P, D])
        self.xn = s.sb("xn", [P, D])
        self.stats = s.sb("stats", [P, 6])
        self.mv = s.sb("mv", [P, 2])
        self.ve = s.sb("ve", [P, 1])
        self.rstd = s.sb("rstd", [P, 1])
        self.y_ready = s.sem("y_ready")
        self.stats_ready = s.sem("stats_ready")
        self.held = s.sem("held")
        self.mv_ready = s.sem("mv_ready")
        self.ve_ready = s.sem("ve_ready")
        self.rstd_ready = s.sem("rstd_ready")
        self.xn_ready = s.sem("xn_ready")
        self.stored = s.sem("stored")

    def vector(self, dve, turn):
        self.moments(dve, turn)
        self.normed(dve, turn)

    def moments(self, dve, turn):
        nc = self.nc
        dve.wait_ge(self.y_ready, turn + self.ahead)
        nc.vector.bn_stats(self.stats[:, :], self.y[:, :]).then_inc(self.stats_ready, 1)
        wait_apart(dve, self.stats_ready, turn, self.held)
        nc.vector.bn_aggr(self.mv[:, :], self.stats[:, :]).then_inc(self.mv_ready, 1)
        dve.wait_ge(self.mv_ready, turn)
        nc.vector.tensor_scalar(self.ve[:, :], self.mv[:, 1:2], EPS, None, ALU.add).then_inc(self.ve_ready, 1)

    def normed(self, dve, turn):
        dve.wait_ge(self.rstd_ready, turn)
        dve.wait_ge(self.stored, turn * 16)
        self.nc.vector.tensor_scalar(self.xn[:, :], self.y[:, :], self.mv[:, 0:1], self.rstd[:, :],
                                     ALU.subtract, ALU.mult).then_inc(self.xn_ready, 1)
        dve.wait_ge(self.xn_ready, turn)

    def end(self, dve):
        dve.wait_ge(self.held, NT)

    def root(self, pool, turn, m_half):
        pool.wait_ge(self.ve_ready, turn)
        self.nc.gpsimd.tensor_tensor(self.rstd[:, :], self.ve[:, :], m_half[:, :], ALU.pow).then_inc(self.rstd_ready, 1)

    def store(self, sp, x_out, i, turn):
        sp.wait_ge(self.xn_ready, turn)
        sp.dma_start(rows(x_out, i), self.xn[:, :]).then_inc(self.stored, 16)


def rows(dram, i):
    return dram[bass.ds(i * P, P), :]



def attention0(nc, x_in, x_out, wq, wk, wv, wo, k):
    NH, HD, NKV = 32, 16, 8
    NQK = (NH + NKV) * HD
    with Scope(nc, "a0") as s:
        ident = s.sb("ident", [P, P])
        cos = s.sb("cos", [P, HD])
        sin = s.sb("sin", [P, HD])
        causal = s.sb("causal", [P, S])
        half_mask = s.sb("half_mask", [P, 2])
        m_half = s.sb("m_half", [P, 1])
        w_qkv = s.sb("w_qkv", [P, DC, D + 2 * NKV * HD])
        w_o = s.sb("w_o", [P, DC, D])
        xt = s.sb("xt", [P, D])
        xres = s.sb("xres", [P, D])
        xT = s.sb("xT", [P, DC, P])
        rot_a = s.sb("rot_a", [P, NH + NKV, HD])
        rot_b = s.sb("rot_b", [P, NH + NKV, HD])
        qk = s.sb("qk", [P, NH + NKV, HD])
        krep = s.sb("krep", [P, NKV, 4, HD])
        qT = s.sb("qT", [P, DC, P])
        kpair = s.sb("kpair", [P, DC, 2, 2, S])
        v_hold = s.sb("v_hold", [P, NKV, HD])
        vpair = s.sb("vpair", [P, 2, NKV, 2, HD])
        sc = s.sb("sc", [P, NH, S])
        pr = s.sb("pr", [P, NH, S])
        mx = s.sb("mx", [P, NH])
        sm = s.sb("sm", [P, NH])
        rs = s.sb("rs", [P, NH])
        pT = s.sb("pT", [P, 16, P])
        oT = s.sb("oT", [P, DC, P])
        norm = Norm(nc, s, ahead=1)

        ps_t = s.ps("ps_t", [P, DC, P])
        ps_qkv = s.ps("ps_qkv", [P, 2 * D])
        ps_s = s.ps("ps_s", [P, 4, DC, 2, S])
        ps_y = s.ps("ps_y", [P, D])

        consts = s.sem("consts")
        weights = s.sem("weights")
        zeroed = s.sem("zeroed")
        xt_in = s.sem("xt_in")
        xres_in = s.sem("xres_in")
        xt_turned = s.sem("xt_turned")
        xT_ready = s.sem("xT_ready")
        qkv_ready = s.sem("qkv_ready")
        rot_ready = s.sem("rot_ready")
        qk_ready = s.sem("qk_ready")
        krep_ready = s.sem("krep_ready")
        q_turned = s.sem("q_turned")
        qT_ready = s.sem("qT_ready")
        k_turned = s.sem("k_turned")
        kpair_ready = s.sem("kpair_ready")
        scores_ready = s.sem("scores_ready")
        masked = s.sem("masked")
        mx_ready = s.sem("mx_ready")
        centred = s.sem("centred")
        exp_ready = s.sem("exp_ready")
        sum_ready = s.sem("sum_ready")
        inv_ready = s.sem("inv_ready")
        probs_ready = s.sem("probs_ready")
        probs_turned = s.sem("probs_turned")
        pT_ready = s.sem("pT_ready")
        o_ready = s.sem("o_ready")
        oT_ready = s.sem("oT_ready")
        v_held = s.sem("v_held")
        v_ready = s.sem("v_ready")
        proj_ready = s.sem("proj_ready")

        N_CONST = 6 * 16
        with s.block() as block:

            @block.sync
            def _(sp):
                for dst, src in ((ident, k["ident"]), (cos, k["cos"]), (sin, k["sin"]),
                                 (causal, k["causal"]), (half_mask, k["half_mask"]), (m_half, k["m_half"])):
                    sp.dma_start(dst[:, :], src).then_inc(consts, 16)
                sp.dma_start(xt[:, :], rows(x_in, 0)).then_inc(xt_in, 16)
                n = D
                sp.dma_start(w_qkv[:, :, 0:n], wq.rearrange("(c p) n -> p c n", p=P)).then_inc(weights, 16)
                sp.dma_start(w_qkv[:, :, n:n + P], wk.rearrange("(c p) n -> p c n", p=P)).then_inc(weights, 16)
                sp.dma_start(w_qkv[:, :, n + P:n + 2 * P], wv.rearrange("(c p) n -> p c n", p=P)).then_inc(weights, 16)
                sp.dma_start(w_o[:, :, :], wo.rearrange("(c p) n -> p c n", p=P)).then_inc(weights, 16)

                def load_xt(turn):
                    sp.wait_ge(xt_turned, turn - 1)
                    sp.dma_start(xt[:, :], rows(x_in, turn - 1)).then_inc(xt_in, 16)

                def load_xres(turn):
                    sp.wait_ge(norm.y_ready, turn)
                    sp.dma_start(xres[:, :], rows(x_in, turn - 1)).then_inc(xres_in, 16)

                load_xt(2)
                load_xres(1)
                load_xt(3)
                load_xt(4)
                with sp.Fori(2, NT - 2) as t:
                    load_xt(t + 3)
                    load_xres(t)
                    norm.store(sp, x_out, t - 2, t - 1)
                for t in range(NT - 2, NT + 1):
                    load_xres(t)
                    norm.store(sp, x_out, t - 2, t - 1)
                norm.store(sp, x_out, NT - 1, NT)
                sp.wait_ge(norm.stored, 16 * (NT + 1))

            @block.tensor
            def _(pe):
                def turn_x(turn):
                    pe.wait_ge(xt_in, turn * 16)
                    for c in range(DC):
                        mm = pe.transpose(ps_t[:, c, :], xt[:, c * P:(c + 1) * P], ident[:, :])
                    mm.then_inc(xt_turned, 1)

                def project(turn, held=True):
                    pe.wait_ge(xT_ready, turn)
                    if held:
                        pe.wait_ge(v_held, turn - 1)
                    for c in range(DC):
                        pe.matmul(ps_qkv[:, 0:D], xT[:, c, :], w_qkv[:, c, 0:D], start=c == 0, stop=c == DC - 1)
                    for c in range(DC):
                        mm = pe.matmul(ps_qkv[:, D:D + 256], xT[:, c, :], w_qkv[:, c, D:D + 256],
                                       start=c == 0, stop=c == DC - 1)
                    mm.then_inc(qkv_ready, 1)

                def turn_qk(turn):
                    pe.wait_ge(qk_ready, turn)
                    for c in range(DC):
                        mm = pe.transpose(ps_t[:, c, :], qk[:, 8 * c:8 * c + 8, :].rearrange("p h d -> p (h d)"), ident[:, :])
                    mm.then_inc(q_turned, 1)
                    pe.wait_ge(qT_ready, turn)
                    pe.wait_ge(krep_ready, turn)
                    for c in range(DC):
                        mm = pe.transpose(ps_t[:, c, :], krep[:, 2 * c:2 * c + 2, :, :].rearrange("p g r d -> p (g r d)"),
                                          ident[:, :])
                    mm.then_inc(k_turned, 1)

                def scores(turn):
                    pe.wait_ge(kpair_ready, turn)
                    for a in range(DC):
                        for b in range(2):
                            for j in range(4):
                                q4 = slice(32 * j, 32 * j + 32)
                                mm = pe.matmul(ps_s[64 * b:64 * b + 64, j, a, :, :].rearrange("p e k -> p (e k)"),
                                               qT[q4, a, 64 * b:64 * b + 64],
                                               kpair[q4, a, b, :, :].rearrange("p e k -> p (e k)"),
                                               start=True, stop=True)
                    mm.then_inc(scores_ready, 1)

                def turn_probs(turn, ahead=True):
                    pe.wait_ge(probs_ready, turn)
                    if ahead:
                        pe.wait_ge(masked, turn + 1)
                    for j in range(4):
                        for a in range(DC):
                            h = 8 * a + 2 * j
                            mm = pe.transpose(ps_s[:, j, a, :, :].rearrange("p e k -> p (e k)"),
                                              pr[:, h:h + 2, :].rearrange("p e k -> p (e k)"), ident[:, :])
                    mm.then_inc(probs_turned, 1)

                def attend(turn, ahead=True):
                    pe.wait_ge(pT_ready, turn)
                    pe.wait_ge(v_ready, turn)
                    if ahead:
                        pe.wait_ge(kpair_ready, turn + 2)
                    for a in range(DC):
                        for j in range(4):
                            for b in range(2):
                                mm = pe.matmul(ps_t[32 * j:32 * j + 32, a, 64 * b:64 * b + 64],
                                               vpair[:, b, 2 * a + j // 2, :, :].rearrange("p e d -> p (e d)"),
                                               pT[:, 4 * j + a, 64 * b:64 * b + 64], start=True, stop=True,
                                               tile_position=(0, 32 * j))
                    mm.then_inc(o_ready, 1)

                def output(turn):
                    pe.wait_ge(oT_ready, turn)
                    pe.wait_ge(norm.y_ready, turn)
                    for c in range(DC):
                        mm = pe.matmul(ps_y[:, :], oT[:, c, :], w_o[:, c, :], start=c == 0, stop=c == DC - 1)
                    mm.then_inc(proj_ready, 1)

                def turn_of(t, before=True):
                    scores(t + 1)
                    if before:
                        pe.wait_ge(oT_ready, t - 1)
                    turn_x(t + 2)
                    if before:
                        output(t - 1)
                    project(t + 2)
                    turn_probs(t)
                    turn_qk(t + 2)
                    attend(t)

                pe.wait_ge(consts, N_CONST)
                pe.wait_ge(weights, 64)
                turn_x(1)
                project(1, held=False)
                turn_qk(1)
                scores(1)
                turn_x(2)
                project(2)
                turn_qk(2)
                turn_of(1, before=False)
                with pe.Fori(2, NT - 1) as t:
                    turn_of(t)
                scores(NT)
                output(NT - 2)
                turn_probs(NT - 1)
                attend(NT - 1, ahead=False)
                output(NT - 1)
                turn_probs(NT, ahead=False)
                attend(NT, ahead=False)
                output(NT)

            @block.scalar
            def _(act):
                def front_x(turn):
                    act.wait_ge(xt_turned, turn)
                    nc.scalar.copy(xT[:, :, :], ps_t[:, :, :]).then_inc(xT_ready, 1)

                def front_q(turn):
                    act.wait_ge(q_turned, turn)
                    nc.scalar.copy(qT[:, :, :], ps_t[:, :, :]).then_inc(qT_ready, 1)

                def hold_values(turn, before=True):
                    act.wait_ge(rot_ready, turn)
                    if before:
                        act.wait_ge(v_ready, turn - 1)
                    nc.scalar.copy(v_hold[:, :, :], ps_qkv[:, NQK:NQK + NKV * HD].rearrange("p (g d) -> p g d", d=HD)
                                   ).then_inc(v_held, 1)

                def values(turn):
                    act.wait_ge(v_held, turn)
                    for b in range(2):
                        for e in range(2):
                            ins = nc.scalar.copy(vpair[64 * e:64 * e + 64, b, :, e, :], v_hold[64 * b:64 * b + 64, :, :])
                    ins.then_inc(v_ready, 1)

                def exps(turn, before=True):
                    act.wait_ge(centred, turn)
                    if before:
                        act.wait_ge(probs_turned, turn - 1)
                    nc.scalar.activation(pr[:, :, :], sc[:, :, :], ACT.Exp, scale=HD ** -0.5).then_inc(exp_ready, 1)

                def keep_probs(turn):
                    act.wait_ge(probs_turned, turn)
                    nc.scalar.copy(pT[:, :, :], ps_s[:, :, :, :, :].rearrange("p j a e k -> p (j a) (e k)")).then_inc(pT_ready, 1)

                def keep_attended(turn):
                    act.wait_ge(o_ready, turn)
                    nc.scalar.copy(oT[:, :, :], ps_t[:, :, :]).then_inc(oT_ready, 1)

                def turn_of(t):
                    front_x(t + 2)
                    keep_probs(t)
                    front_q(t + 2)
                    exps(t + 1)
                    keep_attended(t)
                    values(t + 1)
                    hold_values(t + 2)

                act.wait_ge(zeroed, 1)
                front_x(1)
                hold_values(1, before=False)
                values(1)
                front_q(1)
                front_x(2)
                exps(1, before=False)
                hold_values(2)
                front_q(2)
                with act.Fori(1, NT - 1) as t:
                    turn_of(t)
                keep_probs(NT - 1)
                exps(NT)
                keep_attended(NT - 1)
                values(NT)
                keep_probs(NT)
                keep_attended(NT)

            @block.vector
            def _(dve):
                def rotate(turn):
                    dve.wait_ge(qkv_ready, turn)
                    src = ps_qkv[:, 0:NQK].rearrange("p (h d) -> p h d", d=HD)
                    n = NH + NKV
                    nc.vector.tensor_tensor(rot_a[:, :, :], src, cos[:, :].unsqueeze(1).broadcast_to([P, n, HD]), ALU.mult)
                    for e in range(2):
                        ins = nc.vector.tensor_tensor(rot_b[:, :, e::2], src[:, :, 1 - e::2],
                                                      sin[:, e::2].unsqueeze(1).broadcast_to([P, n, HD // 2]), ALU.mult)
                    ins.then_inc(rot_ready, 1)
                    dve.wait_ge(rot_ready, turn)
                    nc.vector.tensor_tensor(qk[:, :, :], rot_a[:, :, :], rot_b[:, :, :], ALU.add).then_inc(qk_ready, 1)

                def pairs(turn):
                    dve.wait_ge(k_turned, turn)
                    for a in range(DC):
                        for b in range(2):
                            ins = nc.vector.tensor_tensor(
                                kpair[:, a, b, :, :],
                                ps_t[:, a, 64 * b:64 * b + 64].unsqueeze(1).broadcast_to([P, 2, S]),
                                half_mask[:, :].unsqueeze(2).broadcast_to([P, 2, S]), ALU.mult)
                    ins.then_inc(kpair_ready, 1)

                def softmax_a(turn):
                    dve.wait_ge(scores_ready, turn)
                    for j in range(4):
                        for a in range(DC):
                            h = 8 * a + 2 * j
                            ins = nc.vector.tensor_tensor(sc[:, h:h + 2, :], ps_s[:, j, a, :, :],
                                                          causal[:, :].unsqueeze(1).broadcast_to([P, 2, S]), ALU.add)
                    ins.then_inc(masked, 1)
                    dve.wait_ge(masked, turn)
                    nc.vector.tensor_reduce(mx[:, :], sc[:, :, :], AX.X, ALU.max).then_inc(mx_ready, 1)
                    dve.wait_ge(mx_ready, turn)
                    nc.vector.tensor_tensor(sc[:, :, :], sc[:, :, :], mx[:, :].unsqueeze(2).broadcast_to([P, NH, S]),
                                            ALU.subtract).then_inc(centred, 1)

                def softmax_b(turn):
                    dve.wait_ge(exp_ready, turn)
                    nc.vector.tensor_reduce(sm[:, :], pr[:, :, :], AX.X, ALU.add).then_inc(sum_ready, 1)
                    dve.wait_ge(sum_ready, turn)
                    nc.vector.reciprocal(rs[:, :], sm[:, :]).then_inc(inv_ready, 1)
                    dve.wait_ge(inv_ready, turn)
                    nc.vector.tensor_tensor(pr[:, :, :], pr[:, :, :], rs[:, :].unsqueeze(2).broadcast_to([P, NH, S]),
                                            ALU.mult).then_inc(probs_ready, 1)

                def normalise(turn):
                    dve.wait_ge(xres_in, turn * 16)
                    dve.wait_ge(proj_ready, turn)
                    nc.vector.tensor_tensor(norm.y[:, :], ps_y[:, :], xres[:, :], ALU.add).then_inc(norm.y_ready, 1)
                    norm.vector(dve, turn)

                nc.vector.memset(vpair[:, :, :, :, :], 0.0).then_inc(zeroed, 1)
                dve.sem_inc(norm.stored, 16)
                dve.sem_inc(norm.y_ready, 1)
                dve.wait_ge(consts, N_CONST)
                rotate(1)
                pairs(1)
                softmax_a(1)
                rotate(2)
                pairs(2)
                softmax_b(1)
                softmax_a(2)
                rotate(3)
                pairs(3)
                softmax_b(2)
                with dve.Fori(2, NT - 1) as t:
                    softmax_a(t + 1)
                    normalise(t - 1)
                    rotate(t + 2)
                    pairs(t + 2)
                    softmax_b(t + 1)
                softmax_a(NT)
                normalise(NT - 2)
                softmax_b(NT)
                normalise(NT - 1)
                normalise(NT)
                norm.end(dve)

            @block.gpsimd
            def _(pool):
                def copies(turn):
                    pool.wait_ge(rot_ready, turn)
                    nc.gpsimd.tensor_tensor(krep[:, :, :, :],
                                            rot_a[:, NH:NH + NKV, :].unsqueeze(2).broadcast_to([P, NKV, 4, HD]),
                                            rot_b[:, NH:NH + NKV, :].unsqueeze(2).broadcast_to([P, NKV, 4, HD]),
                                            ALU.add).then_inc(krep_ready, 1)

                pool.wait_ge(consts, N_CONST)
                for t in range(1, 4):
                    copies(t)
                with pool.Fori(2, NT - 1) as t:
                    norm.root(pool, t - 1, m_half)
                    copies(t + 2)
                norm.root(pool, NT - 2, m_half)
                norm.root(pool, NT - 1, m_half)
                norm.root(pool, NT, m_half)



MAGIC = 12582912.0
QMAX = 65535.0


class Quant:

    SCALE, INV, LO, HI = range(4)

    def __init__(self, s, keep, name, parts):
        self.ends = s.sb(f"{name}_ends", [P, 2, parts])
        self.mine = s.sb(f"{name}_mine", [P, 2])
        self.all = s.sb(f"{name}_all", [P, 2])
        self.tmp = s.sb(f"{name}_tmp", [P, 4])
        self.par = keep.sb(f"{name}_par", [P, 4])
        self.step = s.sem(f"{name}_step")

    def get(self, n):
        return self.par[:, n:n + 1]

    def vector(self, nc, dve):
        step, t = self.step, self.tmp
        nc.vector.tensor_reduce(self.mine[:, :], self.ends[:, :, :], AX.X, ALU.max).then_inc(step, 1)
        dve.wait_ge(step, 2)
        nc.vector.tensor_scalar(self.all[:, :], self.all[:, :], 0.0, None, ALU.max).then_inc(step, 1)
        dve.wait_ge(step, 3)
        nc.vector.tensor_tensor(t[:, 0:1], self.all[:, 0:1], self.all[:, 1:2], ALU.add).then_inc(step, 1)
        dve.wait_ge(step, 4)
        nc.vector.tensor_scalar(self.get(self.SCALE), t[:, 0:1], 1.0 / QMAX, 1e-12, ALU.mult, ALU.max).then_inc(step, 1)
        dve.wait_ge(step, 5)
        nc.vector.reciprocal(self.get(self.INV), self.get(self.SCALE)).then_inc(step, 1)
        dve.wait_ge(step, 6)
        nc.vector.tensor_scalar(t[:, 1:2], self.all[:, 1:2], self.get(self.INV), MAGIC, ALU.mult, ALU.add).then_inc(step, 1)
        dve.wait_ge(step, 7)
        nc.vector.tensor_scalar(t[:, 2:3], t[:, 1:2], MAGIC, QMAX, ALU.subtract, ALU.min).then_inc(step, 1)
        dve.wait_ge(step, 8)
        nc.vector.tensor_scalar(self.get(self.LO), t[:, 2:3], -1.0, MAGIC, ALU.mult, ALU.add).then_inc(step, 1)
        dve.wait_ge(step, 9)
        nc.vector.tensor_scalar(self.get(self.HI), self.get(self.LO), QMAX, None, ALU.add).then_inc(step, 1)

    DONE = 10

    def pool(self, nc, pool):
        pool.wait_ge(self.step, 1)
        nc.gpsimd.partition_all_reduce(self.all[:, :], self.mine[:, :], P, RMAX).then_inc(self.step, 1)



def cross0(nc, x_in, ctx, x_out, w, k, xq):
    H, HD, W, LEFT = 8, 8, 16, 8
    BH = 2 * H
    ON_POOL = (3, 7, 11, 15)
    ON_DVE = tuple(p for p in range(W) if p not in ON_POOL)
    NV, NP_, RV, RP = len(ON_DVE), len(ON_POOL), 4, 2
    SUM = 8
    SUMS, ADDS = W // SUM, SUM - 1
    with Scope(nc, "c0") as s:
        ident = s.sb("ident", [P, P])
        heads = s.sb("heads", [P, BH])
        m_half = s.sb("m_half", [P, 1])
        wts = s.sb("wts", [P, 4, P])
        bias = s.sb("bias", [P, 4])
        xt = s.sb("xt", [P, D])
        ct = s.sb("ct", [P, 2, D])
        xres = s.sb("xres", [P, D])
        q = s.sb("q", [P, D])
        kp = s.sb("kp", [P, D + W])
        vp = s.sb("vp", [P, 2, D + W])
        prod_v = s.sb("prod_v", [P, RV, D])
        prod_p = s.sb("prod_p", [P, RP, D])
        dots = s.sb("dots", [P, 4, W, BH])
        pr = s.sb("pr", [P, 4, W, BH])
        wide = s.sb("wide", [P, 2, 4, W, BH * HD])
        mx = s.sb("mx", [P, 4, BH])
        sm = s.sb("sm", [P, 4, BH])
        rs = s.sb("rs", [P, 4, BH])
        pv = s.sb("pv", [P, SUM, D])
        summed = s.sb("summed", [P, SUMS, D])
        norm = Norm(nc, s, ahead=1)

        ps_q = s.ps("ps_q", [P, D])
        ps_k = s.ps("ps_k", [P, D])
        ps_v = s.ps("ps_v", [P, D])
        ps_dots = s.ps("ps_dots", [P, 4, W, BH])
        ps_e = s.ps("ps_e", [P, 2, D])
        ps_y = s.ps("ps_y", [P, D])

        consts = s.sem("consts")
        padded = s.sem("padded")
        xt_in = s.sem("xt_in")
        ct_in = [s.sem(f"ct_in{n}") for n in range(2)]
        xres_in = s.sem("xres_in")
        q_done = s.sem("q_done")
        k_done = s.sem("k_done")
        v_done = s.sem("v_done")
        q_ready = s.sem("q_ready")
        k_ready = s.sem("k_ready")
        v_ready = s.sem("v_ready")
        prod_v_ready = s.sem("prod_v_ready")
        prod_p_ready = s.sem("prod_p_ready")
        prod_used = s.sem("prod_used")
        dots_ready = s.sem("dots_ready")
        mx_ready = s.sem("mx_ready")
        centred = s.sem("centred")
        exp_ready = s.sem("exp_ready")
        sum_ready = s.sem("sum_ready")
        inv_ready = s.sem("inv_ready")
        probs_ready = s.sem("probs_ready")
        wide_ready = s.sem("wide_ready")
        spread = s.sem("spread")
        pv_ready = s.sem("pv_ready")
        added = s.sem("added")
        sum_used = s.sem("sum_used")
        ends_ready = s.sem("ends_ready")

        N_CONST = 16 * 5

        with s.block() as block:

            @block.sync
            def _(sp):
                for dst, src in ((ident[:, :], k["ident"]), (heads[:, :], k["heads"]), (m_half[:, :], k["m_half"]),
                                 (wts[:, :, :], w["wts"]), (bias[:, :], w["bias"])):
                    sp.dma_start(dst, src).then_inc(consts, 16)

                def load_xt(turn):
                    if not (isinstance(turn, int) and turn == 1):
                        sp.wait_ge(q_done, turn - 1)
                    sp.dma_start(xt[:, :], rows(x_in, turn - 1)).then_inc(xt_in, 16)

                def load_ct(turn, n, free=True):
                    if free:
                        sp.wait_ge(v_done, turn - 2)
                    sp.dma_start(ct[:, n, :], rows(ctx, turn - 1)).then_inc(ct_in[n], 16)

                def load_xres(turn):
                    sp.wait_ge(norm.y_ready, turn)
                    sp.dma_start(xres[:, :], rows(x_in, turn - 1)).then_inc(xres_in, 16)

                load_xt(1)
                load_ct(1, 0, free=False)
                load_xt(2)
                load_ct(2, 1, free=False)
                load_xt(3)
                load_ct(3, 0)
                load_xres(1)
                with sp.Fori(0, NT // 2 - 2) as j:
                    for n in range(2):
                        t = 2 * j + n + 1
                        load_xt(t + 3)
                        load_ct(t + 3, 1 - n)
                        load_xres(t + 1)
                        norm.store(sp, x_out, t - 1, t)
                load_xt(NT)
                load_ct(NT, 1)
                for t in range(NT - 3, NT):
                    load_xres(t + 1)
                    norm.store(sp, x_out, t - 1, t)
                norm.store(sp, x_out, NT - 1, NT)
                sp.wait_ge(norm.stored, 16 * (NT + 1))

            @block.tensor
            def _(pe):
                def project_qk(turn, n, j):
                    pe.wait_ge(xt_in, turn * 16)
                    pe.matmul(ps_q[:, :], wts[:, 0, :], xt[:, :], start=True, stop=True).then_inc(q_done, 1)
                    pe.wait_ge(ct_in[n], j * 16)
                    pe.matmul(ps_k[:, :], wts[:, 1, :], ct[:, n, :], start=True, stop=True).then_inc(k_done, 1)

                def project_v(turn, n):
                    pe.wait_ge(v_ready, turn)
                    pe.matmul(ps_v[:, :], wts[:, 2, :], ct[:, n, :], start=True, stop=True).then_inc(v_done, 1)

                def score(turn, p):
                    if p == 0:
                        pe.wait_ge(centred, turn)
                    if p in ON_POOL:
                        m = ON_POOL.index(p)
                        src = prod_p[:, m % RP, :]
                        pe.wait_ge(prod_p_ready, (turn - 1) * NP_ + m + 1)
                    else:
                        m = ON_DVE.index(p)
                        src = prod_v[:, m % RV, :]
                        pe.wait_ge(prod_v_ready, (turn - 1) * NV + m + 1)
                    for t in range(4):
                        mm = pe.matmul(ps_dots[:, t, p, :], src[:, t * P:(t + 1) * P], heads[:, :], start=True, stop=True)
                    mm.then_inc(prod_used if p < W - 1 else dots_ready, 1)

                def out(turn, m):
                    if m == 0:
                        pe.wait_ge(norm.y_ready, turn)
                    pe.wait_ge(added, ((turn - 1) * SUMS + m + 2) * ADDS)
                    pe.matmul(ps_y[:, :], wts[:, 3, :], summed[:, m, :], start=m == 0, stop=m == SUMS - 1
                              ).then_inc(sum_used, 1)

                def attend(turn, n, scored=None, before=True):
                    for p in range(W):
                        if p % 4 == 0:
                            pe.wait_ge(wide_ready, turn * 4 + p // 4 + 1)
                        pe.wait_ge(pv_ready, turn * W + W - 1 + p)
                        for t in range(4):
                            mm = pe.transpose(ps_e[:, p % 2, t * P:(t + 1) * P], wide[:, n, t, p, :], ident[:, :])
                        mm.then_inc(spread, 1)
                        if scored is not None:
                            score(scored, p)
                        if p == 1 and before:
                            out(turn - 1, SUMS - 1)
                        if p == SUM + 3:
                            out(turn, 0)

                pe.wait_ge(consts, N_CONST)
                project_qk(1, 0, 1)
                project_v(1, 0)
                for p in range(W):
                    score(1, p)
                project_qk(2, 1, 1)
                for p in range(W):
                    score(2, p)
                def turn_of(t, n, j, before=True):
                    project_qk(t + 2, n, j + 2)
                    project_v(t + 1, 1 - n)
                    attend(t, n, t + 2, before)

                turn_of(1, 0, 0, before=False)
                turn_of(2, 1, 0)
                with pe.Fori(1, NT // 2 - 1) as j:
                    for n in range(2):
                        turn_of(2 * j + n + 1, n, j)
                project_v(NT, 1)
                attend(NT - 1, 0)
                attend(NT, 1)
                out(NT, SUMS - 1)

            @block.scalar
            def _(act):
                def evacuate_qk(turn):
                    act.wait_ge(q_done, turn)
                    act.wait_ge(dots_ready, turn)
                    nc.scalar.activation(q[:, :], ps_q[:, :], ACT.Identity, bias=bias[:, 0:1]).then_inc(q_ready, 1)
                    act.wait_ge(k_done, turn)
                    nc.scalar.activation(kp[:, LEFT:LEFT + D], ps_k[:, :], ACT.Identity, bias=bias[:, 1:2]).then_inc(k_ready, 1)

                def evacuate_v(turn, n):
                    act.wait_ge(v_done, turn)
                    act.wait_ge(pv_ready, turn * W)
                    nc.scalar.activation(vp[:, n, LEFT:LEFT + D], ps_v[:, :], ACT.Identity, bias=bias[:, 2:3]).then_inc(v_ready, 1)

                def exps(turn, n):
                    act.wait_ge(centred, turn + 1)
                    act.wait_ge(wide_ready, turn * 4)
                    nc.scalar.activation(pr[:, :, :, :], dots[:, :, :, :], ACT.Exp, scale=HD ** -0.5).then_inc(exp_ready, 1)
                    act.wait_ge(probs_ready, turn)
                    act.wait_ge(spread, turn * W)
                    for g in range(4):
                        nc.scalar.copy(
                            wide[:, n, :, 4 * g:4 * g + 4, :].rearrange("p t w (h d) -> p t (w h) d", d=HD),
                            pr[:, :, 4 * g:4 * g + 4, :].rearrange("p t w h -> p t (w h)").unsqueeze(3).broadcast_to(
                                [P, 4, 4 * BH, HD])).then_inc(wide_ready, 1)

                act.wait_ge(consts, N_CONST)
                act.wait_ge(padded, 1)
                evacuate_qk(1)
                evacuate_v(1, 0)
                evacuate_qk(2)
                exps(1, 0)
                with act.Fori(0, NT // 2 - 1) as j:
                    for n in range(2):
                        t = 2 * j + n + 1
                        evacuate_qk(t + 2)
                        evacuate_v(t + 1, 1 - n)
                        exps(t + 1, 1 - n)
                evacuate_v(NT, 1)
                exps(NT, 1)

            @block.vector
            def _(dve):
                def product(turn, p):
                    if p in ON_POOL or p >= W:
                        return
                    if p == 0:
                        dve.wait_ge(q_ready, turn)
                        dve.wait_ge(k_ready, turn)
                    m = ON_DVE.index(p)
                    if m >= RV:
                        dve.wait_ge(prod_used, (turn - 1) * (W - 1) + ON_DVE[m - RV] + 1)
                    nc.vector.tensor_tensor(prod_v[:, m % RV, :], q[:, :], kp[:, p:p + D], ALU.mult).then_inc(prod_v_ready, 1)

                def softmax_a(turn):
                    dve.wait_ge(dots_ready, turn + 1)
                    nc.vector.tensor_reduce(mx[:, :, :], ps_dots[:, :, :, :].rearrange("p t w h -> p t h w"), AX.X,
                                            ALU.max).then_inc(mx_ready, 1)
                    dve.wait_ge(mx_ready, turn)
                    nc.vector.tensor_tensor(dots[:, :, :, :], ps_dots[:, :, :, :],
                                            mx[:, :, :].unsqueeze(2).broadcast_to([P, 4, W, BH]), ALU.subtract
                                            ).then_inc(centred, 1)

                def softmax_b(turn):
                    dve.wait_ge(exp_ready, turn)
                    nc.vector.tensor_reduce(sm[:, :, :], pr[:, :, :, :].rearrange("p t w h -> p t h w"), AX.X,
                                            ALU.add).then_inc(sum_ready, 1)
                    dve.wait_ge(sum_ready, turn)
                    nc.vector.reciprocal(rs[:, :, :], sm[:, :, :]).then_inc(inv_ready, 1)
                    dve.wait_ge(inv_ready, turn)
                    nc.vector.tensor_tensor(pr[:, :, :, :], pr[:, :, :, :],
                                            rs[:, :, :].unsqueeze(2).broadcast_to([P, 4, W, BH]), ALU.mult
                                            ).then_inc(probs_ready, 1)

                def value(turn, n, p):
                    dve.wait_ge(spread, (turn + 1) * W + p + 1)
                    dve.wait_ge(added, ((turn - 1) * SUMS + p // SUM) * ADDS + max(p % SUM, 1))
                    nc.vector.tensor_tensor(pv[:, p % SUM, :], ps_e[:, p % 2, :], vp[:, n, p:p + D], ALU.mult).then_inc(pv_ready, 1)

                def residual(turn):
                    dve.wait_ge(sum_used, turn * SUMS + SUMS)
                    dve.wait_ge(xres_in, turn * 16)
                    nc.vector.scalar_tensor_tensor(norm.y[:, :], ps_y[:, :], bias[:, 3:4], xres[:, :], ALU.add, ALU.add
                                                   ).then_inc(norm.y_ready, 1)

                def ends(turn):
                    nc.vector.tensor_reduce(xq.ends[:, 0, bass.ds(turn - 1, 1)], norm.xn[:, :], AX.X, ALU.max)
                    nc.vector.tensor_reduce(xq.ends[:, 1, bass.ds(turn - 1, 1)], norm.xn[:, :], AX.X, ALU.min, negate=True
                                            ).then_inc(ends_ready, 1)

                def turn_of(t, n, before=True, soft=True, scored=True):
                    if soft:
                        softmax_a(t + 1)
                    if scored:
                        product(t + 2, 0)
                        product(t + 2, 1)
                    dve.wait_ge(v_ready, t + 1)
                    for p in range(W):
                        if scored:
                            product(t + 2, p + 2)
                        value(t, n, p)
                        if p == 2 and before:
                            residual(t - 1)
                        if p == 3 and before:
                            norm.moments(dve, t - 1)
                        if p == 5 and before:
                            norm.normed(dve, t - 1)
                            ends(t - 1)
                        if p == 7 and soft:
                            softmax_b(t + 1)

                nc.vector.memset(xq.ends[:, :, :], 0.0)
                nc.vector.memset(kp[:, :], 0.0)
                nc.vector.memset(vp[:, :, :], 0.0).then_inc(padded, 1)
                dve.sem_inc(norm.stored, 16)
                dve.sem_inc(norm.y_ready, 1)
                dve.sem_inc(centred, 1)
                dve.sem_inc(dots_ready, 1)
                dve.sem_inc(v_ready, 1)
                dve.sem_inc(wide_ready, 4)
                dve.sem_inc(spread, 2 * W)
                dve.sem_inc(pv_ready, 2 * W)
                dve.sem_inc(added, ADDS)
                dve.sem_inc(sum_used, SUMS)
                dve.wait_ge(padded, 1)
                for p in range(W):
                    product(1, p)
                softmax_a(1)
                for p in range(W):
                    product(2, p)
                    if p == 5:
                        softmax_b(1)
                turn_of(1, 0, before=False)
                turn_of(2, 1)
                with dve.Fori(1, NT // 2 - 1) as j:
                    for n in range(2):
                        turn_of(2 * j + n + 1, n)
                turn_of(NT - 1, 0, scored=False)
                turn_of(NT, 1, soft=False, scored=False)
                residual(NT)
                norm.vector(dve, NT)
                ends(NT)
                norm.end(dve)
                dve.wait_ge(ends_ready, NT)
                xq.vector(nc, dve)
                dve.wait_ge(xq.step, Quant.DONE)

            @block.gpsimd
            def _(pool):
                def product(turn, m):
                    if m == 0:
                        pool.wait_ge(q_ready, turn)
                        pool.wait_ge(k_ready, turn)
                    if m >= RP:
                        pool.wait_ge(prod_used, (turn - 1) * (W - 1) + ON_POOL[m - RP] + 1)
                    p = ON_POOL[m]
                    nc.gpsimd.tensor_tensor(prod_p[:, m % RP, :], q[:, :], kp[:, p:p + D], ALU.mult).then_inc(prod_p_ready, 1)

                def add(turn, p):
                    m, e = divmod(p, SUM)
                    pool.wait_ge(pv_ready, (turn + 1) * W + p + 1)
                    if e == 1:
                        pool.wait_ge(sum_used, (turn - 1) * SUMS + m + 1)
                    else:
                        pool.wait_ge(added, ((turn - 1) * SUMS + m + 1) * ADDS + e - 1)
                    a = pv[:, 0, :] if e == 1 else summed[:, m, :]
                    nc.gpsimd.tensor_tensor(summed[:, m, :], a, pv[:, e, :], ALU.add).then_inc(added, 1)

                def turn_of(t, before=True, scored=True):
                    for p in range(W):
                        if scored and p % 4 == 0:
                            product(t + 2, p // 4)
                        if p % SUM:
                            add(t, p)
                        if p == 3 and before:
                            norm.root(pool, t - 1, m_half)

                pool.wait_ge(consts, N_CONST)
                for turn in (1, 2):
                    for m in range(NP_):
                        product(turn, m)
                turn_of(1, before=False)
                turn_of(2)
                with pool.Fori(1, NT // 2 - 1) as j:
                    for n in range(2):
                        turn_of(2 * j + n + 1)
                turn_of(NT - 1, scored=False)
                turn_of(NT, scored=False)
                norm.root(pool, NT, m_half)
                xq.pool(nc, pool)



INTER = 1376
IT = (INTER + P - 1) // P
LAST = INTER - (IT - 1) * P
NG = ROWS // D


def tile_rows(it):
    return LAST if it == IT - 1 else P


def ffn0(nc, x_in, x_out, w_gate, w_up, w_down, up_scratch, k, xq):
    with Scope(nc, "f0") as s:
        ident = s.sb("ident", [P, P])
        m_half = s.sb("m_half", [P, 1])
        inner = s.sb("inner", [P, IT, ROWS])
        wd = s.sb("wd", [P, IT, D])
        gq, uq, sq, oq = (Quant(s, s, n, NG * IT) for n in ("gate", "up", "silu", "prod"))
        with Scope(nc, "f0w") as sw:
            wgu = sw.sb("wgu", [P, 2, DC, INTER])
            quantise_weights(nc, w_gate, w_up, w_down, k, ident, m_half, inner, wgu, wd, (gq, uq, sq, oq))
            gate_up(nc, x_in, up_scratch, ident, xq, wgu, inner, gq, uq, sq)
        product(nc, up_scratch, inner, uq, sq, oq)
        down0(nc, x_in, x_out, inner, wd, oq, m_half)


def quantise_weights(nc, w_gate, w_up, w_down, k, ident, m_half, inner, wgu, wd, quants):
    BLK = 32
    with Scope(nc, "f0q") as s:
        nat = s.sb("nat", [P, 2, INTER])
        rnd = s.sb("rnd", [P, 2, INTER])
        nb = 2 * DC * P // BLK
        big = s.sb("big", [P, 64])
        scale = s.sb("scale", [P, 2, 64])
        inv = s.sb("inv", [P, 64])
        ps = s.ps("ps", [P, 2, 3 * D])
        consts = s.sem("consts")
        nat_in = [s.sem(f"nat_loaded{n}") for n in range(2)]
        step = s.sem("step")
        nat_used = s.sem("nat_used")
        rounded = s.sem("rounded")
        turned = s.sem("turned")
        kept = s.sem("kept")
        zeroed = s.sem("zeroed")
        GU, DN = IT, DC
        STEPS = 5

        with s.block() as block:

            @block.sync
            def _(sp):
                sp.dma_start(ident[:, :], k["ident"]).then_inc(consts, 16)
                sp.dma_start(m_half[:, :], k["m_half"]).then_inc(consts, 16)

                def load(n, r0, rows_, turn, down=False):
                    if down:
                        sp.dma_start(nat[0:rows_, n, :], w_down[r0:r0 + rows_, :] if isinstance(r0, int) else
                                     w_down[bass.ds(r0, rows_), :]).then_inc(nat_in[n], 16)
                    else:
                        for m, src in enumerate((w_gate, w_up)):
                            sp.dma_start(nat[0:rows_, n, m * D:m * D + D], src[bass.ds(r0, rows_), :]
                                         ).then_inc(nat_in[n], 16)

                load(0, 0, P, 1)
                load(1, P, P, 2)
                with sp.Fori(0, GU // 2 - 1) as j:
                    for n in range(2):
                        sp.wait_ge(nat_used, 2 * j + n + 1)
                        load(n, (2 * j + n + 2) * P, P, 0)
                sp.wait_ge(nat_used, GU - 2)
                load(0, (IT - 1) * P, LAST, GU)
                for d in range(DN):
                    sp.wait_ge(nat_used, GU - 1 + d)
                    load((GU + d) % 2, d * P, P, 0, down=True)

            def piece_counts(t):
                return sum(16 * (2 if u < GU else 1) for u in range(t % 2, t + 1, 2))

            @block.vector
            def _(dve):
                def piece(n, rows_, width, base, loaded, turn):
                    nbk = width // BLK
                    src = nat[0:rows_, n, 0:width].rearrange("p (b e) -> p b e", e=BLK)
                    dst = rnd[0:rows_, n, 0:width].rearrange("p (b e) -> p b e", e=BLK)
                    flat = rnd[0:rows_, n, 0:width]
                    dve.wait_ge(nat_in[n], loaded)
                    nc.vector.tensor_reduce(big[0:rows_, 0:nbk], src, AX.X, ALU.max, apply_absolute_value=True).then_inc(step, 1)
                    dve.wait_ge(step, base + 1)
                    dve.wait_ge(rounded, turn + 1)
                    nc.vector.tensor_scalar(scale[0:rows_, n, 0:nbk], big[0:rows_, 0:nbk], 1.0 / 7.0, 1e-12, ALU.mult,
                                            ALU.max).then_inc(step, 1)
                    dve.wait_ge(step, base + 2)
                    nc.vector.reciprocal(inv[0:rows_, 0:nbk], scale[0:rows_, n, 0:nbk]).then_inc(step, 1)
                    dve.wait_ge(step, base + 3)
                    return src, dst, flat, nbk

                def rest(n, rows_, base, turn, src, dst, flat, nbk):
                    dve.wait_ge(turned, turn)
                    nc.vector.tensor_tensor(dst, src, inv[0:rows_, 0:nbk].unsqueeze(2).broadcast_to([rows_, nbk, BLK]),
                                            ALU.mult).then_inc(nat_used, 1)
                    dve.wait_ge(nat_used, turn)
                    nc.vector.tensor_scalar(flat, flat, MAGIC, MAGIC + 7.0, ALU.add, ALU.min).then_inc(step, 1)
                    dve.wait_ge(step, base + 4)
                    nc.vector.tensor_scalar(flat, flat, MAGIC - 8.0, MAGIC, ALU.max, ALU.subtract).then_inc(step, 1)

                for q in quants:
                    nc.vector.memset(q.ends[:, :, :], 0.0)
                nc.vector.memset(inner[96:P, IT - 1, :], 0.0).then_inc(zeroed, 1)
                dve.sem_inc(turned, 2)
                with dve.Fori(0, GU // 2) as j:
                    for n in range(2):
                        base = (2 * j + n) * STEPS
                        a = piece(n, P, 2 * D, base, 32 * j + 32, 2 * j + n + 1)
                        rest(n, P, base, 2 * j + n + 1, *a)
                for t in range(GU - 1, GU + DN):
                    r, width = (LAST, 2 * D) if t < GU else (P, INTER)
                    a = piece(t % 2, r, width, t * STEPS, piece_counts(t), t + 1)
                    rest(t % 2, r, t * STEPS, t + 1, *a)
                dve.wait_ge(zeroed, 1)

            @block.gpsimd
            def _(pool):
                def scaled(n, rows_, width, turn):
                    nbk = width // BLK
                    part = rnd[0:rows_, n, 0:width].rearrange("p (b e) -> p b e", e=BLK)
                    pool.wait_ge(step, turn * STEPS)
                    nc.gpsimd.tensor_tensor(part, part, scale[0:rows_, n, 0:nbk].unsqueeze(2).broadcast_to([rows_, nbk, BLK]),
                                            ALU.mult).then_inc(rounded, 1)

                pool.sem_inc(rounded, 2)
                with pool.Fori(0, GU // 2) as j:
                    for n in range(2):
                        scaled(n, P, 2 * D, 2 * j + n + 1)
                for t in range(GU - 1, GU + DN):
                    scaled(t % 2, *((LAST, 2 * D) if t < GU else (P, INTER)), t + 1)

            @block.tensor
            def _(pe):
                def gate_up_piece(n, rows_, turn):
                    pe.wait_ge(rounded, turn + 2)
                    pe.wait_ge(kept, turn)
                    for c in range(2 * DC):
                        mm = pe.transpose(ps[:, n, c * P:c * P + rows_], rnd[0:rows_, n, c * P:(c + 1) * P],
                                          ident[0:rows_, 0:rows_])
                    mm.then_inc(turned, 1)

                def down_piece(n, turn):
                    pe.wait_ge(rounded, turn + 2)
                    pe.wait_ge(kept, turn)
                    for it in range(IT):
                        r = tile_rows(it)
                        mm = pe.transpose(ps[0:r, n, it * P:(it + 1) * P], rnd[:, n, it * P:it * P + r], ident[:, :])
                    mm.then_inc(turned, 1)

                pe.wait_ge(consts, 32)
                with pe.Fori(0, GU // 2) as j:
                    for n in range(2):
                        gate_up_piece(n, P, 2 * j + n + 1)
                gate_up_piece(0, LAST, GU)
                for t in range(GU, GU + DN):
                    down_piece(t % 2, t + 1)

            @block.scalar
            def _(act):
                def gate_up_piece(n, r0, rows_, turn):
                    act.wait_ge(turned, turn + 2)
                    nc.scalar.copy(wgu[:, :, :, bass.ds(r0, rows_)].rearrange("p m c r -> p (m c) r"),
                                   ps[:, n, 0:2 * DC * P].rearrange("p (c r) -> p c r", r=P)[:, :, 0:rows_]).then_inc(kept, 1)

                act.sem_inc(kept, 2)
                with act.Fori(0, GU // 2) as j:
                    for n in range(2):
                        gate_up_piece(n, (2 * j + n) * P, P, 2 * j + n + 1)
                gate_up_piece(0, (IT - 1) * P, LAST, GU)
                for d in range(DN):
                    t = GU + d
                    act.wait_ge(turned, t + 3)
                    nc.scalar.copy(wd[:, 0:IT - 1, d * P:(d + 1) * P],
                                   ps[:, t % 2, 0:(IT - 1) * P].rearrange("p (i r) -> p i r", r=P))
                    nc.scalar.copy(wd[0:LAST, IT - 1, d * P:(d + 1) * P],
                                   ps[0:LAST, t % 2, (IT - 1) * P:IT * P]).then_inc(kept, 1)
                act.wait_ge(kept, GU + DN + 2)


def gate_up(nc, x_in, up_scratch, ident, xq, wgu, inner, gq, uq, sq):
    SIG = 65536.0
    RU = 4
    with Scope(nc, "f0g") as s:
        xg = s.sb("xg", [P, 2, D])
        xr = s.sb("xr", [P, 2, D])
        xqT = s.sb("xqT", [P, DC, ROWS])
        up = s.sb("up", [P, RU, D])
        th = s.sb("th", [P, 2, D])
        ps_t = s.ps("ps_t", [P, 2, DC, P])
        ps_w = s.ps("ps_w", [P, 4, D])
        x_loaded = [s.sem(f"x_loaded{n}") for n in range(2)]
        x_step = s.sem("x_step")
        x_read = s.sem("x_read")
        x_rounded = s.sem("x_rounded")
        x_turned = s.sem("x_turned")
        xqT_ready = s.sem("xqT_ready")
        gate_done = s.sem("gate_done")
        gate_kept = s.sem("gate_kept")
        gate_ends = s.sem("gate_ends")
        up_done = s.sem("up_done")
        up_kept = s.sem("up_kept")
        up_ends = s.sem("up_ends")
        up_stored = [s.sem(f"up_stored{n}") for n in range(RU)]
        g_step = s.sem("g_step")
        g_ready = s.sem("g_ready")
        th_ready = s.sem("th_ready")
        silu_ready = s.sem("silu_ready")
        silu_ends = s.sem("silu_ends")
        sig_step = s.sem("sig_step")
        sig_ready = s.sem("sig_ready")
        held = s.sem("held")
        N = NG * IT

        with s.block() as block:

            @block.sync
            def _(sp):
                for n in range(2):
                    sp.dma_start(xg[:, n, :], rows(x_in, n)).then_inc(x_loaded[n], 16)
                with sp.Fori(0, NT // 2 - 1) as j:
                    for n in range(2):
                        sp.wait_ge(x_read, 2 * j + n + 1)
                        sp.dma_start(xg[:, n, :], rows(x_in, 2 * j + n + 2)).then_inc(x_loaded[n], 16)
                with sp.Fori(0, NG) as g:
                    for it in range(IT):
                        r = tile_rows(it)
                        sp.wait_ge(up_kept, g * IT + it + 3)
                        sp.dma_start(up_scratch[it, 0:r, bass.ds(g * D, D)], up[0:r, it % RU, :]).then_inc(up_stored[it % RU], 16)
                for n in range(RU):
                    sp.wait_ge(up_stored[n], 16 * (NG * len(range(n, IT, RU)) + 1))

            @block.tensor
            def _(pe):
                with pe.Fori(0, NT // 2) as j:
                    for n in range(2):
                        turn = 2 * j + n + 1
                        pe.wait_ge(x_rounded, turn)
                        pe.wait_ge(xqT_ready, turn)
                        for c in range(DC):
                            mm = pe.transpose(ps_t[:, n, c, :], xr[:, n, c * P:(c + 1) * P], ident[:, :])
                        mm.then_inc(x_turned, 1)
                pe.wait_ge(xqT_ready, NT + 2)
                for m, done, kept in ((0, gate_done, gate_kept), (1, up_done, up_kept)):
                    with pe.Fori(0, NG) as g:
                        for it in range(IT):
                            r = tile_rows(it)
                            bank = 2 * m + it % 2
                            pe.wait_ge(kept, g * IT + it + (2 if it == 0 else 1))
                            for c in range(DC):
                                mm = pe.matmul(ps_w[0:r, bank, :], wgu[:, m, c, it * P:it * P + r],
                                               xqT[:, c, bass.ds(g * D, D)], start=c == 0, stop=c == DC - 1)
                            mm.then_inc(done, 1)

            @block.scalar
            def _(act):
                act.sem_inc(xqT_ready, 2)
                with act.Fori(0, NT // 2) as j:
                    for n in range(2):
                        turn = 2 * j + n + 1
                        act.wait_ge(x_turned, turn + 2)
                        nc.scalar.copy(xqT[:, :, bass.ds((turn - 1) * P, P)], ps_t[:, n, :, :]).then_inc(xqT_ready, 1)
                with act.Fori(0, NG) as g:
                    for it in range(IT):
                        r = tile_rows(it)
                        act.wait_ge(gate_done, g * IT + it + 1)
                        nc.scalar.copy(inner[0:r, it, bass.ds(g * D, D)], ps_w[0:r, it % 2, :]).then_inc(gate_kept, 1)
                with act.Fori(0, NG) as g:
                    for it in range(IT):
                        r = tile_rows(it)
                        u = g * IT + it
                        act.wait_ge(up_done, u + 1)
                        act.wait_ge(up_ends, u + 1 + (it < RU - 1))
                        act.wait_ge(up_stored[it % RU], 16 * (g * len(range(it % RU, IT, RU)) + it // RU + 1))
                        nc.scalar.copy(up[0:r, it % RU, :], ps_w[0:r, 2 + it % 2, :]).then_inc(up_kept, 1)
                        act.wait_ge(g_ready, u + 1)
                        act.wait_ge(silu_ready, u + 1 + (it == 0))
                        nc.scalar.activation(th[0:r, it % 2, :], inner[0:r, it, bass.ds(g * D, D)], ACT.Tanh,
                                             scale=0.5).then_inc(th_ready, 1)

            @block.vector
            def _(dve):
                with dve.Fori(0, NT // 2) as j:
                    for n in range(2):
                        turn = 2 * j + n + 1
                        dve.wait_ge(x_loaded[n], 16 * j + 16)
                        dve.wait_ge(x_turned, turn)
                        nc.vector.tensor_scalar(xr[:, n, :], xg[:, n, :], xq.get(1), MAGIC, ALU.mult, ALU.add).then_inc(x_read, 1)
                        dve.wait_ge(x_read, turn)
                        nc.vector.tensor_scalar(xr[:, n, :], xr[:, n, :], xq.get(2), xq.get(3), ALU.max, ALU.min).then_inc(x_step, 1)
                        dve.wait_ge(x_step, turn)
                        nc.vector.tensor_scalar(xr[:, n, :], xr[:, n, :], MAGIC, xq.get(0), ALU.subtract, ALU.mult
                                                ).then_inc(x_rounded, 1)
                with dve.Fori(0, NG) as g:
                    for it in range(IT):
                        r = tile_rows(it)
                        u = g * IT + it
                        dve.wait_ge(gate_kept, u + 3)
                        part = inner[0:r, it, bass.ds(g * D, D)]
                        nc.vector.tensor_reduce(gq.ends[0:r, 0, bass.ds(u, 1)], part, AX.X, ALU.max)
                        nc.vector.tensor_reduce(gq.ends[0:r, 1, bass.ds(u, 1)], part, AX.X, ALU.min, negate=True).then_inc(gate_ends, 1)
                dve.wait_ge(gate_ends, N)
                gq.vector(nc, dve)
                dve.wait_ge(gq.step, Quant.DONE)

                with dve.Fori(0, NG) as g:
                    def ends(q, part, r, u, after):
                        nc.vector.tensor_reduce(q.ends[0:r, 0, bass.ds(u, 1)], part, AX.X, ALU.max)
                        nc.vector.tensor_reduce(q.ends[0:r, 1, bass.ds(u, 1)], part, AX.X, ALU.min, negate=True).then_inc(after, 1)

                    def first(it):
                        r = tile_rows(it)
                        u = g * IT + it
                        part = inner[0:r, it, bass.ds(g * D, D)]
                        nc.vector.tensor_scalar(part, part, gq.get(1)[0:r], MAGIC, ALU.mult, ALU.add).then_inc(g_step, 1)
                        dve.wait_ge(g_step, 2 * u + 1)
                        nc.vector.tensor_scalar(part, part, gq.get(2)[0:r], gq.get(3)[0:r], ALU.max, ALU.min).then_inc(g_step, 1)
                        dve.wait_ge(g_step, 2 * u + 2)
                        nc.vector.tensor_scalar(part, part, MAGIC, gq.get(0)[0:r], ALU.subtract, ALU.mult).then_inc(g_ready, 1)

                    def second(it):
                        r = tile_rows(it)
                        u = g * IT + it
                        part = inner[0:r, it, bass.ds(g * D, D)]
                        dve.wait_ge(up_kept, u + 3)
                        ends(uq, up[0:r, it % RU, :], r, u, up_ends)
                        dve.wait_ge(sig_ready, u + 1)
                        nc.vector.scalar_tensor_tensor(part, th[0:r, it % 2, :], 1.0 / SIG, part, ALU.mult, ALU.mult
                                                       ).then_inc(silu_ready, 1)
                        dve.wait_ge(silu_ready, u + 3)
                        ends(sq, part, r, u, silu_ends)

                    first(0)
                    for it in range(1, IT):
                        first(it)
                        second(it - 1)
                    second(IT - 1)
                dve.wait_ge(up_ends, RU + N)
                dve.wait_ge(silu_ends, N)
                uq.vector(nc, dve)
                sq.vector(nc, dve)
                dve.wait_ge(uq.step, Quant.DONE)
                dve.wait_ge(sq.step, Quant.DONE)

            @block.gpsimd
            def _(pool):
                pool.sem_inc(x_turned, 2)
                pool.sem_inc(gate_kept, 2)
                pool.sem_inc(up_kept, 2)
                pool.sem_inc(up_ends, RU)
                pool.sem_inc(silu_ready, 2)
                for n in range(RU):
                    pool.sem_inc(up_stored[n], 16)
                gq.pool(nc, pool)
                with pool.Fori(0, NG) as g:
                    for it in range(IT):
                        r = tile_rows(it)
                        u = g * IT + it
                        t = th[0:r, it % 2, :]
                        wait_apart(pool, th_ready, u + 1, held)
                        nc.gpsimd.tensor_scalar(t, t, SIG / 2, SIG / 2 + MAGIC, ALU.mult, ALU.add).then_inc(sig_step, 1)
                        wait_apart(pool, sig_step, u + 1, held)
                        nc.gpsimd.tensor_scalar(t, t, MAGIC + QMAX, -MAGIC, ALU.min, ALU.add).then_inc(sig_ready, 1)
                pool.wait_ge(held, 2 * N)
                uq.pool(nc, pool)
                sq.pool(nc, pool)


def product(nc, up_scratch, inner, uq, sq, oq):
    C = 1024
    PER = ROWS // C
    with Scope(nc, "f0p") as s:
        up = s.sb("up", [P, 2, PER, C])
        both = s.sb("both", [P, 1])
        both_ready = s.sem("both_ready")
        up_in = [s.sem(f"up_in{n}") for n in range(2)]
        up_read = s.sem("up_read")
        u_step = s.sem("u_step")
        held = s.sem("held")
        u_ready = s.sem("u_ready")
        g_step = s.sem("g_step")
        ends = s.sem("ends")
        done = s.sem("done")

        with s.block() as block:

            @block.sync
            def _(sp):
                def load(n, it, r):
                    sp.dma_start(up[0:r, n, :, :].rearrange("p h c -> p (h c)"),
                                 up_scratch[bass.ds(it, 1), 0:r, :].rearrange("o p c -> (o p) c")).then_inc(up_in[n], 16)

                load(0, 0, P)
                load(1, 1, P)
                with sp.Fori(0, (IT - 1) // 2 - 1) as j:
                    for n in range(2):
                        sp.wait_ge(done, PER * (2 * j + n + 1))
                        load(n, 2 * j + n + 2, P)
                sp.wait_ge(done, PER * (IT - 2))
                load(0, IT - 1, LAST)

            def each(loop_engine, body):
                with loop_engine.Fori(0, (IT - 1) // 2) as j:
                    for n in range(2):
                        for h in range(PER):
                            body(n, 2 * j + n, P, h, (2 * j + n) * PER + h, j + 1)
                for h in range(PER):
                    body(0, IT - 1, LAST, h, (IT - 1) * PER + h, (IT - 1) // 2 + 1)

            @block.gpsimd
            def _(pool):
                def body(n, it, r, h, u, loads):
                    part = up[0:r, n, h, :]
                    wait_apart(pool, up_in[n], loads * 16, held)
                    nc.gpsimd.tensor_scalar(part, part, uq.get(1)[0:r], MAGIC, ALU.mult, ALU.add).then_inc(u_step, 1)
                    wait_apart(pool, u_step, u + 1, held)
                    nc.gpsimd.tensor_scalar(part, part, uq.get(3)[0:r], uq.get(2)[0:r], ALU.min, ALU.max).then_inc(u_ready, 1)
                each(pool, body)
                pool.wait_ge(held, 2 * IT * PER)
                oq.pool(nc, pool)

            @block.vector
            def _(dve):
                def body(n, it, r, h, u, loads):
                    part = inner[0:r, bass.ds(it, 1), h * C:(h + 1) * C].rearrange("p o c -> p (o c)")
                    nc.vector.tensor_scalar(part, part, sq.get(1)[0:r], MAGIC, ALU.mult, ALU.add).then_inc(g_step, 1)
                    dve.wait_ge(g_step, 3 * u + 1)
                    nc.vector.tensor_scalar(part, part, sq.get(2)[0:r], sq.get(3)[0:r], ALU.max, ALU.min).then_inc(g_step, 1)
                    dve.wait_ge(g_step, 3 * u + 2)
                    nc.vector.tensor_scalar(part, part, MAGIC, both[0:r, :], ALU.subtract, ALU.mult).then_inc(g_step, 1)
                    dve.wait_ge(g_step, 3 * u + 3)
                    dve.wait_ge(u_ready, u + 1)
                    nc.vector.scalar_tensor_tensor(part, up[0:r, n, h, :], MAGIC, part, ALU.subtract, ALU.mult).then_inc(done, 1)
                    dve.wait_ge(done, u + 1)
                    nc.vector.tensor_reduce(oq.ends[0:r, 0, bass.ds(u, 1)], part, AX.X, ALU.max)
                    nc.vector.tensor_reduce(oq.ends[0:r, 1, bass.ds(u, 1)], part, AX.X, ALU.min, negate=True).then_inc(ends, 1)
                nc.vector.tensor_tensor(both[:, :], sq.get(0), uq.get(0), ALU.mult).then_inc(both_ready, 1)
                dve.wait_ge(both_ready, 1)
                each(dve, body)
                dve.wait_ge(ends, IT * PER)
                oq.vector(nc, dve)
                dve.wait_ge(oq.step, Quant.DONE)


def down0(nc, x_in, x_out, inner, wd, oq, m_half):
    with Scope(nc, "f0d") as s:
        xres = s.sb("xres", [P, D])
        o = s.sb("o", [P, 2, IT, P])
        norm = Norm(nc, s, ahead=2)
        ps_y = s.ps("ps_y", [P, 2, D])
        xres_in = s.sem("xres_in")
        o_step = s.sem("o_step")
        o_ready = s.sem("o_ready")
        y_done = s.sem("y_done")

        with s.block() as block:

            @block.sync
            def _(sp):
                sp.dma_start(xres[:, :], rows(x_in, 0)).then_inc(xres_in, 16)
                with sp.Fori(0, NT - 1) as i:
                    sp.wait_ge(norm.y_ready, i + 3)
                    sp.dma_start(xres[:, :], rows(x_in, i + 1)).then_inc(xres_in, 16)
                    norm.store(sp, x_out, i, i + 1)
                norm.store(sp, x_out, NT - 1, NT)
                sp.wait_ge(norm.stored, 16 * (NT + 1))

            @block.tensor
            def _(pe):
                with pe.Fori(0, NT // 2) as j:
                    for n in range(2):
                        turn = 2 * j + n + 1
                        pe.wait_ge(o_ready, turn)
                        pe.wait_ge(norm.y_ready, turn)
                        for it in range(IT):
                            r = tile_rows(it)
                            mm = pe.matmul(ps_y[:, n, :], o[0:r, n, it, :], wd[0:r, it, :], start=it == 0, stop=it == IT - 1)
                        mm.then_inc(y_done, 1)

            @block.vector
            def _(dve):
                def round_(turn, n):
                    part = inner[:, :, bass.ds((turn - 1) * P, P)]
                    dve.wait_ge(y_done, turn)
                    nc.vector.tensor_scalar(o[:, n, :, :], part, oq.get(1), MAGIC, ALU.mult, ALU.add).then_inc(o_step, 1)
                    dve.wait_ge(o_step, 2 * turn - 1)
                    nc.vector.tensor_scalar(o[:, n, :, :], o[:, n, :, :], oq.get(2), oq.get(3), ALU.max, ALU.min).then_inc(o_step, 1)
                    dve.wait_ge(o_step, 2 * turn)
                    nc.vector.tensor_scalar(o[:, n, :, :], o[:, n, :, :], MAGIC, oq.get(0), ALU.subtract, ALU.mult
                                            ).then_inc(o_ready, 1)

                def finish(turn, n):
                    dve.wait_ge(xres_in, turn * 16)
                    dve.wait_ge(y_done, turn + 2)
                    nc.vector.tensor_tensor(norm.y[:, :], ps_y[:, n, :], xres[:, :], ALU.add).then_inc(norm.y_ready, 1)
                    norm.vector(dve, turn)

                dve.sem_inc(norm.stored, 16)
                dve.sem_inc(y_done, 2)
                dve.sem_inc(norm.y_ready, 2)
                round_(1, 0)
                with dve.Fori(0, NT // 2 - 1) as j:
                    round_(2 * j + 2, 1)
                    finish(2 * j + 1, 0)
                    round_(2 * j + 3, 0)
                    finish(2 * j + 2, 1)
                round_(NT, 1)
                finish(NT - 1, 0)
                finish(NT, 1)
                norm.end(dve)

            @block.gpsimd
            def _(pool):
                with pool.Fori(0, NT) as i:
                    norm.root(pool, i + 1, m_half)



NH1, NKV1, HD1, LAT = 32, 8, 128, 32
STEP = 256
NS = ROWS // STEP


def latent1(nc, x_in, x_out, w, lat_scratch, k):
    with Scope(nc, "a1") as s:
        ident = s.sb("ident", [P, P])
        wq = s.sb("wq", [P, 2, DC, NH1 * HD1], F16)
        wo = s.sb("wo", [P, 2, NH1, D], F16)
        wku = s.sb("wku", [P, 2, NKV1 * HD1])
        wvu = s.sb("wvu", [P, 2, NKV1 * HD1])
        latents(nc, x_in, w, lat_scratch, k, ident, (wq, wo, wku, wvu))
        attend1(nc, x_in, x_out, lat_scratch, k, ident, (wq, wo, wku, wvu))


def latents(nc, x_in, w, lat_scratch, k, ident, weights):
    PIECE = 2048
    with Scope(nc, "l1") as s:
        stage = s.sb("stage", [P, 2, PIECE])
        wdn = s.sb("wdn", [P, DC, 2 * NKV1 * LAT])
        xt = s.sb("xt", [P, 4, D])
        xT = s.sb("xT", [P, DC, D])
        lat = s.sb("lat", [P, 2, 4, D])
        ps_t = s.ps("ps_t", [P, 2, DC, P])
        ps_c = s.ps("ps_c", [P, 4, D])
        small_in = s.sem("small_in")
        xt_in = s.sem("xt_in")
        x_turned = s.sem("x_turned")
        xT_ready = s.sem("xT_ready")
        c_done = s.sem("c_done")
        moved_act = s.sem("moved_act")
        moved_dve = s.sem("moved_dve")
        stored = [s.sem(f"stored{n}") for n in range(2)]
        up_in = s.sem("up_in")
        piece_in = [s.sem(f"piece_in{n}") for n in range(2)]
        high_ready = s.sem("high_ready")
        low_ready = s.sem("low_ready")
        wq, wo, wku, wvu = weights
        pieces = [(w["q"][c * P:(c + 1) * P, h * PIECE:(h + 1) * PIECE],
                   [wq[:, e, c, h * PIECE:(h + 1) * PIECE] for e in range(2)])
                  for c in range(DC) for h in range(2)]
        heads = PIECE // D
        pieces += [(w["o"].rearrange("(h p) n -> p h n", p=P)[:, c * heads:(c + 1) * heads, :],
                    [wo[:, e, c * heads:(c + 1) * heads, :].rearrange("p h n -> p (h n)") for e in range(2)])
                   for c in range(NH1 // heads)]
        per_group = len(pieces) // NG

        def move(copy, t, n):
            kv = t // 2
            for quad in range(4):
                h = 4 * (t % 2) + quad
                for j in range(8):
                    to = 32 * (2 * (j % 2) + kv)
                    ins = copy(
                        lat[to:to + 32, n, j // 2, :].rearrange("p (b h m) -> p b h m", h=8, m=8)[:, :, h, :],
                        ps_c[32 * quad:32 * quad + 32, t, :].rearrange("p (b m j) -> p b m j", m=8, j=8)[:, :, :, j])
            return ins

        with s.block() as block:

            @block.sync
            def _(sp):
                sp.dma_start(ident[:, :], k["ident"]).then_inc(small_in, 16)
                sp.dma_start(wdn[:, :, :], w["down"].rearrange("(c p) n -> p c n", p=P)).then_inc(small_in, 16)

                def load(g):
                    sp.dma_start(xt[:, :, :], x_in[bass.ds(g * D, D), :].rearrange("(t p) n -> p t n", p=P)).then_inc(xt_in, 16)

                load(0)
                sp.dma_start(wku[:, :, :], w["k_up"].rearrange("(c p) n -> p c n", p=P)).then_inc(up_in, 16)
                sp.dma_start(wvu[:, :, :], w["v_up"].rearrange("(c p) n -> p c n", p=P)).then_inc(up_in, 16)

                def load_piece(m):
                    if m >= 2:
                        sp.wait_ge(low_ready, m - 1)
                    dst = stage[:, m % 2, :]
                    if m >= 2 * DC:
                        dst = dst.rearrange("p (h n) -> p h n", n=D)
                    sp.dma_start(dst, pieces[m][0]).then_inc(piece_in[m % 2], 16)

                for g in range(NG):
                    if g + 1 < NG:
                        sp.wait_ge(x_turned, 4 * g + 4)
                        load(g + 1)
                    for m in range(per_group * g, per_group * (g + 1)):
                        load_piece(m)
                    sp.wait_ge(moved_act, g + 2)
                    sp.wait_ge(moved_dve, g + 2)
                    sp.dma_start(lat_scratch[:, :, g * D:(g + 1) * D], lat[:, g % 2, :, :]).then_inc(stored[g % 2], 16)
                for n in range(2):
                    sp.wait_ge(stored[n], 16 * NG // 2)
                sp.wait_ge(up_in, 32)

            @block.tensor
            def _(pe):
                pe.wait_ge(small_in, 32)
                with pe.Fori(0, NG) as g:
                    pe.wait_ge(xt_in, 16 * g + 16)
                    for t in range(4):
                        pe.wait_ge(xT_ready, 4 * g + t + 1)
                        for c in range(DC):
                            mm = pe.transpose(ps_t[:, t % 2, c, :], xt[:, t, c * P:(c + 1) * P], ident[:, :])
                        mm.then_inc(x_turned, 1)
                    pe.wait_ge(xT_ready, 4 * g + 6)
                    pe.wait_ge(moved_act, g + 1)
                    pe.wait_ge(moved_dve, g + 1)
                    for t in range(4):
                        for c in range(DC):
                            mm = pe.matmul(ps_c[:, t, :], wdn[:, c, t * P:(t + 1) * P], xT[:, c, :],
                                           start=c == 0, stop=c == DC - 1)
                        mm.then_inc(c_done, 1)

            @block.scalar
            def _(act):
                def split(m):
                    act.wait_ge(piece_in[m % 2], 16 * (m // 2 + 1))
                    split_high(nc, pieces[m][1][0], stage[:, m % 2, :]).then_inc(high_ready, 1)

                act.sem_inc(xT_ready, 2)
                act.sem_inc(moved_act, 1)
                act.sem_inc(moved_dve, 1)
                for g in range(NG):
                    for t in range(4):
                        act.wait_ge(x_turned, 4 * g + t + 1)
                        if g > 0:
                            act.wait_ge(c_done, 4 * g)
                        nc.scalar.copy(xT[:, :, t * P:(t + 1) * P], ps_t[:, t % 2, :, :]).then_inc(xT_ready, 1)
                    split(per_group * g)
                    split(per_group * g + 1)
                    if g >= 2:
                        act.wait_ge(stored[g % 2], 16 * (g // 2))
                    for t in (0, 2):
                        act.wait_ge(c_done, 4 * g + t + 1)
                        ins = move(nc.scalar.copy, t, g % 2)
                    ins.then_inc(moved_act, 1)
                    for m in range(per_group * g + 2, per_group * (g + 1)):
                        split(m)

            @block.vector
            def _(dve):
                def split(m):
                    dve.wait_ge(high_ready, m + 1)
                    split_low(nc, pieces[m][1][1], stage[:, m % 2, :], pieces[m][1][0]).then_inc(low_ready, 1)

                for g in range(NG):
                    split(per_group * g)
                    split(per_group * g + 1)
                    if g >= 2:
                        dve.wait_ge(stored[g % 2], 16 * (g // 2))
                    for t in (1, 3):
                        dve.wait_ge(c_done, 4 * g + t + 1)
                        ins = move(nc.vector.tensor_copy, t, g % 2)
                    ins.then_inc(moved_dve, 1)
                    for m in range(per_group * g + 2, per_group * (g + 1)):
                        split(m)
                dve.wait_ge(low_ready, len(pieces))


def attend1(nc, x_in, x_out, lat_scratch, k, ident, weights):
    G, R = NKV1, NH1 // NKV1
    BB = STEP // S
    USES = 2 + 4 + 3 * G
    with Scope(nc, "m1") as s:
        causal = s.sb("causal", [P, S])
        m_half = s.sb("m_half", [P, 1])
        xt = s.sb("xt", [P, 2, D])
        xres = s.sb("xres", [P, 2, D])
        xT = s.sb("xT", [P, 2, DC, STEP], F16)
        lat = s.sb("lat", [P, 4, STEP])
        qT = s.sb("qT", [P, 2, BB, R, S])
        kT = s.sb("kT", [P, 2, STEP])
        v = s.sb("v", [P, 2, G * HD1])
        sc = s.sb("sc", [P, 2 * BB, S])
        pr = s.sb("pr", [P, 2 * BB, S])
        mx = s.sb("mx", [P, 2 * BB])
        sm = s.sb("sm", [P, 2 * BB])
        rs = s.sb("rs", [P, 2 * BB])
        pT = s.sb("pT", [P, 2, 2, P])
        aT = s.sb("aT", [P, 2, R, BB, S], F16)
        norm = Norm(nc, s, ahead=2)
        ps_w = s.ps("ps_w", [P, 2, D])
        ps_s = s.ps("ps_s", [P, 2, BB, S])
        ps_p = s.ps("ps_p", [P, 2, 2, P])
        ps_o = s.ps("ps_o", [P, 2, BB // 2, R * S])
        ps_y = s.ps("ps_y", [P, 2, D])
        consts = s.sem("consts")
        xt_in = s.sem("xt_in")
        xres_in = s.sem("xres_in")
        lat_in = s.sem("lat_in")
        w_done = s.sem("w_done")
        w_kept = s.sem("w_kept")
        scores_ready = s.sem("scores_ready")
        masked = s.sem("masked")
        mx_ready = s.sem("mx_ready")
        centred = s.sem("centred")
        exp_ready = s.sem("exp_ready")
        sum_ready = s.sem("sum_ready")
        inv_ready = s.sem("inv_ready")
        probs_ready = s.sem("probs_ready")
        turned = s.sem("turned")
        pT_ready = s.sem("pT_ready")
        o_done = s.sem("o_done")
        x_high = s.sem("x_high")
        a_high = s.sem("a_high")
        aT_ready = s.sem("aT_ready")
        used = s.sem("used")
        wq, wo, wku, wvu = weights

        def first_use(g):
            return 2 if g == 0 else 9 + 3 * (g - 1)

        with s.block() as block:

            @block.sync
            def _(sp):
                sp.dma_start(causal[:, :], k["causal"]).then_inc(consts, 16)
                sp.dma_start(m_half[:, :], k["m_half"]).then_inc(consts, 16)

                def pair(dram, i):
                    return dram[bass.ds(i * STEP, STEP), :].rearrange("(t p) n -> p t n", p=P)

                sp.dma_start(xt[:, :, :], pair(x_in, 0)).then_inc(xt_in, 16)
                sp.dma_start(lat[:, :, :], lat_scratch[:, :, 0:STEP]).then_inc(lat_in, 16)
                sp.dma_start(xres[:, :, :], pair(x_in, 0)).then_inc(xres_in, 16)

                def stores(i):
                    for t in range(2):
                        norm.store(sp, x_out, 2 * i + t, 2 * i + t + 1)

                def load_xt(i):
                    sp.wait_ge(w_done, (i - 1) * USES + 2)
                    sp.dma_start(xt[:, :, :], pair(x_in, i)).then_inc(xt_in, 16)

                def load_lat(i):
                    sp.wait_ge(w_done, i * USES)
                    sp.dma_start(lat[:, :, :], lat_scratch[:, :, bass.ds(i * STEP, STEP)]).then_inc(lat_in, 16)

                load_xt(1)
                with sp.Fori(0, NS - 2) as i:
                    load_lat(i + 1)
                    load_xt(i + 2)
                    stores(i)
                    sp.dma_start(xres[:, :, :], pair(x_in, i + 1)).then_inc(xres_in, 16)
                load_lat(NS - 1)
                stores(NS - 2)
                sp.dma_start(xres[:, :, :], pair(x_in, NS - 1)).then_inc(xres_in, 16)
                stores(NS - 1)
                sp.wait_ge(norm.stored, 16 * (NT + 1))

            @block.tensor
            def _(pe):
                def bank(i, n):
                    pe.wait_ge(w_kept, i * USES + n + 1)
                    return ps_w[:, n % 2, :]

                def turn_x(i):
                    pe.wait_ge(xt_in, 16 * i + 16)
                    for t in range(2):
                        b = bank(i, t)
                        for c in range(DC):
                            mm = pe.transpose(b[:, c * P:(c + 1) * P], xt[:, t, c * P:(c + 1) * P], ident[:, :])
                        mm.then_inc(w_done, 1)

                def values(i):
                    for t in range(2):
                        for h in range(2):
                            b = bank(i, 5 + 2 * t + h)
                            for f in range(2):
                                mm = pe.matmul(b, lat[:, 2 + f, t * P:(t + 1) * P], wvu[:, f, h * D:(h + 1) * D],
                                               start=f == 0, stop=f == 1)
                            mm.then_inc(w_done, 1)

                def queries(i, g, rp):
                    if g == 0 and rp == 0:
                        pe.wait_ge(w_kept, i * USES + 4)
                    b = bank(i, first_use(g) + rp)
                    for r in range(2):
                        h = R * g + 2 * rp + r
                        products = [(c, *parts) for c in range(DC) for parts in PARTS]
                        for c, m, n in products:
                            mm = pe.matmul(b[:, r * STEP:(r + 1) * STEP], wq[:, m, c, h * HD1:(h + 1) * HD1],
                                           xT[:, n, c, :], start=(c, m, n) == products[0], stop=(c, m, n) == products[-1])
                    mm.then_inc(w_done, 1)

                def keys(i, g):
                    if g == 0:
                        pe.wait_ge(lat_in, 16 * i + 16)
                    b = bank(i, first_use(g) + 2)
                    for f in range(2):
                        mm = pe.matmul(b[:, 0:STEP], wku[:, f, g * HD1:(g + 1) * HD1], lat[:, f, :],
                                       start=f == 0, stop=f == 1)
                    mm.then_inc(w_done, 1)

                def scores(i, g):
                    pe.wait_ge(w_kept, i * USES + first_use(g) + 3 + 2)
                    for bb in range(BB):
                        for rp in range(2):
                            mm = pe.matmul(ps_s[:, rp, bb, :],
                                           qT[:, g % 2, bb, 2 * rp:2 * rp + 2, :].rearrange("p r q -> p (r q)"),
                                           kT[:, g % 2, bb * S:(bb + 1) * S], start=True, stop=True)
                    mm.then_inc(scores_ready, 1)

                def turn_probs(unit):
                    pe.wait_ge(probs_ready, unit)
                    for t in range(2):
                        for rp in range(2):
                            mm = pe.transpose(ps_p[:, t, rp, :],
                                              pr[:, BB * rp + 2 * t:BB * rp + 2 * t + 2, :].rearrange("p b k -> p (b k)"),
                                              ident[:, :])
                    mm.then_inc(turned, 1)

                def attend(i, g, unit):
                    if g == 0:
                        pe.wait_ge(w_kept, i * USES + 9 + 2)
                    pe.wait_ge(pT_ready, unit)
                    for bb in range(BB):
                        at = slice(64 * (bb % 2), 64 * (bb % 2) + 64)
                        mm = pe.matmul(ps_o[:, bb % 2, bb // 2, :], v[at, bb // 2, g * HD1:(g + 1) * HD1],
                                       pT[at, bb // 2, :, :].rearrange("p r q -> p (r q)"), start=True, stop=True)
                    mm.then_inc(o_done, 1)

                def output(i, g, unit):
                    pe.wait_ge(aT_ready, 2 * unit)
                    if g == 0:
                        pe.wait_ge(norm.y_ready, 2 * i + 2)
                    for t in range(2):
                        products = [(r, *parts) for r in range(R) for parts in PARTS]
                        for r, m, n in products:
                            mm = pe.matmul(ps_y[:, t, :], aT[:, m, r, 2 * t:2 * t + 2, :].rearrange("p b q -> p (b q)"),
                                           wo[:, n, R * g + r, :], start=g == 0 and (r, m, n) == products[0],
                                           stop=g == G - 1 and (r, m, n) == products[-1])
                    mm.then_inc(used, 1)

                def step(i, more=True):
                    for g in range(G):
                        unit = i * G + g + 1
                        if g < G - 1:
                            queries(i, g + 1, 0)
                        elif more:
                            turn_x(i + 1)
                        if g > 0:
                            output(i, g - 1, unit - 1)
                        turn_probs(unit)
                        if g < G - 1:
                            queries(i, g + 1, 1)
                            keys(i, g + 1)
                        elif more:
                            queries(i + 1, 0, 0)
                            queries(i + 1, 0, 1)
                            keys(i + 1, 0)
                        attend(i, g, unit)
                        if g < G - 1:
                            scores(i, g + 1)
                        elif more:
                            scores(i + 1, 0)
                            values(i + 1)
                    output(i, G - 1, unit)

                turn_x(0)
                queries(0, 0, 0)
                queries(0, 0, 1)
                keys(0, 0)
                scores(0, 0)
                values(0)
                with pe.Fori(0, NS - 1) as i:
                    step(i)
                step(NS - 1, more=False)

            @block.scalar
            def _(act):
                def keep(i, n, dst, src, scale=1.0):
                    act.wait_ge(w_done, i * USES + n + 1)
                    nc.scalar.activation(dst, src(ps_w[:, n % 2, :]), ACT.Copy, scale=scale).then_inc(w_kept, 1)

                def keep_x(i):
                    for t in range(2):
                        act.wait_ge(w_done, i * USES + t + 1)
                        split_high(nc, xT[:, 0, :, t * P:(t + 1) * P], ps_w[:, t, :].rearrange("p (c r) -> p c r", c=DC)
                                   ).then_inc(x_high, 1)

                def keep_values(i, t):
                    for h in range(2):
                        keep(i, 5 + 2 * t + h, v[:, t, h * D:(h + 1) * D], lambda b: b)

                def keep_queries(i, g, rp):
                    keep(i, first_use(g) + rp, qT[:, g % 2, :, 2 * rp:2 * rp + 2, :].rearrange("p b r q -> p r b q"),
                         lambda b: b.rearrange("p (r b q) -> p r b q", r=2, q=S), scale=SPLIT ** -2)

                def keep_keys(i, g):
                    keep(i, first_use(g) + 2, kT[:, g % 2, :], lambda b: b[:, 0:STEP])

                def exps(unit):
                    act.wait_ge(centred, unit)
                    nc.scalar.activation(pr[:, :, :], sc[:, :, :], ACT.Exp, scale=HD1 ** -0.5).then_inc(exp_ready, 1)

                def step(i, more=True):
                    for g in range(G):
                        unit = i * G + g + 1
                        if g > 0:
                            exps(unit)
                        if g < G - 1:
                            keep_queries(i, g + 1, 0)
                        elif more:
                            keep_x(i + 1)
                        act.wait_ge(turned, unit)
                        nc.scalar.copy(pT[:, :, :, :], ps_p[:, :, :, :]).then_inc(pT_ready, 1)
                        if g < G - 1:
                            keep_queries(i, g + 1, 1)
                            keep_keys(i, g + 1)
                        elif more:
                            keep_queries(i + 1, 0, 0)
                            keep_queries(i + 1, 0, 1)
                            keep_keys(i + 1, 0)
                        act.wait_ge(o_done, unit)
                        act.wait_ge(used, unit)
                        for e in range(2):
                            split_high(nc, aT[:, 0, :, e::2, :].rearrange("p r t q -> p t r q"),
                                       ps_o[:, e, :, :].rearrange("p t (r q) -> p t r q", r=R)).then_inc(a_high, 1)
                    if more:
                        keep_values(i + 1, 0)
                        exps(unit + 1)
                        keep_values(i + 1, 1)

                act.sem_inc(w_kept, 2)
                keep_x(0)
                keep_queries(0, 0, 0)
                keep_queries(0, 0, 1)
                keep_keys(0, 0)
                keep_values(0, 0)
                exps(1)
                keep_values(0, 1)
                with act.Fori(0, NS - 1) as i:
                    step(i)
                step(NS - 1, more=False)

            @block.vector
            def _(dve):
                dve.sem_inc(norm.stored, 16)
                dve.sem_inc(norm.y_ready, 2)
                dve.sem_inc(used, 1)
                dve.wait_ge(consts, 32)
                n = 2 * BB

                def softmax(unit):
                    dve.wait_ge(scores_ready, unit)
                    nc.vector.tensor_tensor(sc[:, :, :], ps_s[:, :, :, :].rearrange("p r b k -> p (r b) k"),
                                            causal[:, :].unsqueeze(1).broadcast_to([P, n, S]), ALU.add).then_inc(masked, 1)
                    dve.wait_ge(masked, unit)
                    nc.vector.tensor_reduce(mx[:, :], sc[:, :, :], AX.X, ALU.max).then_inc(mx_ready, 1)
                    dve.wait_ge(mx_ready, unit)
                    nc.vector.tensor_tensor(sc[:, :, :], sc[:, :, :], mx[:, :].unsqueeze(2).broadcast_to([P, n, S]),
                                            ALU.subtract).then_inc(centred, 1)
                    dve.wait_ge(exp_ready, unit)
                    nc.vector.tensor_reduce(sm[:, :], pr[:, :, :], AX.X, ALU.add).then_inc(sum_ready, 1)
                    dve.wait_ge(sum_ready, unit)
                    nc.vector.reciprocal(rs[:, :], sm[:, :]).then_inc(inv_ready, 1)
                    dve.wait_ge(inv_ready, unit)
                    nc.vector.tensor_tensor(pr[:, :, :], pr[:, :, :], rs[:, :].unsqueeze(2).broadcast_to([P, n, S]),
                                            ALU.mult).then_inc(probs_ready, 1)

                def x_low(i):
                    for t in range(2):
                        dve.wait_ge(x_high, 2 * i + t + 1)
                        split_low(nc, xT[:, 1, :, t * P:(t + 1) * P], ps_w[:, t, :].rearrange("p (c r) -> p c r", c=DC),
                                  xT[:, 0, :, t * P:(t + 1) * P]).then_inc(w_kept, 1)

                def attended_low(unit):
                    for e in range(2):
                        dve.wait_ge(a_high, 2 * unit - 1 + e)
                        for t in range(BB // 2):
                            ins = split_low(nc, aT[:, 1, :, 2 * t + e, :], ps_o[:, e, t, :].rearrange("p (r q) -> p r q", r=R),
                                            aT[:, 0, :, 2 * t + e, :])
                        ins.then_inc(aT_ready, 1)

                def finish(i):
                    dve.wait_ge(xres_in, 16 * i + 16)
                    dve.wait_ge(used, i * G + G + 1)
                    for t in range(2):
                        nc.vector.scalar_tensor_tensor(norm.y[:, :], ps_y[:, t, :], SPLIT ** -2, xres[:, t, :], ALU.mult, ALU.add
                                                       ).then_inc(norm.y_ready, 1)
                        norm.vector(dve, 2 * i + t + 1)

                x_low(0)
                softmax(1)
                with dve.Fori(0, NS - 1) as i:
                    for g in range(G):
                        if g == G - 1:
                            x_low(i + 1)
                        attended_low(i * G + g + 1)
                        softmax(i * G + g + 2)
                    finish(i)
                for g in range(1, G):
                    attended_low((NS - 1) * G + g)
                    softmax((NS - 1) * G + g + 1)
                attended_low(NS * G)
                finish(NS - 1)
                norm.end(dve)

            @block.gpsimd
            def _(pool):
                pool.wait_ge(consts, 32)
                with pool.Fori(0, NT) as i:
                    norm.root(pool, i + 1, m_half)



def cross1(nc, x_in, ctx, x_out, w, k):
    NP2 = 4
    NB = D // P
    with Scope(nc, "c1") as s:
        ident = s.sb("ident", [P, P])
        m_half = s.sb("m_half", [P, 1])
        seqs = s.sb("seqs", [P, 2])
        w2 = s.sb("w2", [P, 2, D])
        wv = s.sb("wv", [P, NP2, S])
        wo = s.sb("wo", [P, NP2, S])
        wvo = s.sb("wvo", [S, 8, S])
        bo_g = s.sb("bo_g", [P, 2])
        xt = s.sb("xt", [P, D])
        ct = s.sb("ct", [P, D])
        ctT = s.sb("ctT", [P, NB, P])
        xres = s.sb("xres", [P, D])
        qd = s.sb("qd", [P, NB, D])
        qs = s.sb("qs", [P, 2, NB, D])
        qmx = s.sb("qmx", [P, NB, 8])
        qsm = s.sb("qsm", [P, NB, 8])
        qrs = s.sb("qrs", [P, NB, 8])
        kmx = s.sb("kmx", [P, NP2])
        ksm = s.sb("ksm", [P, NP2])
        krs = s.sb("krs", [P, NP2])
        ek = s.sb("ek", [P, NP2, D])
        ekT = s.sb("ekT", [P, NB, D])
        sums = s.sb("sums", [S, D])
        m = s.sb("m", [P, NP2, S])
        qT = s.sb("qT", [P, NP2, D])
        fo = s.sb("fo", [P, D])
        gf = s.sb("gf", [P, D])
        sq = s.sb("sq", [P, D])
        nn = s.sb("nn", [P, NB * 2])
        rn = s.sb("rn", [P, NB * 2])
        rw = s.sb("rw", [P, NB, 2, S])
        m_half8 = s.sb("m_half8", [P, NB * 2])
        norm = Norm(nc, s, ahead=1)
        ps_w = s.ps("ps_w", [P, 4, D])
        ps_t = s.ps("ps_t", [P, 2, D])
        ps_a = s.ps("ps_a", [P, D])
        ps_f = s.ps("ps_f", [P, D])
        consts = s.sem("consts")
        xt_in = s.sem("xt_in")
        ct_in = s.sem("ct_in")
        xres_in = s.sem("xres_in")
        wvo_done = s.sem("wvo_done")
        wvo_ready = s.sem("wvo_ready")
        q_done = s.sem("q_done")
        qmx_ready = s.sem("qmx_ready")
        q_centred = s.sem("q_centred")
        q_exp = s.sem("q_exp")
        q_sum = s.sem("q_sum")
        q_inv = s.sem("q_inv")
        q_ready = s.sem("q_ready")
        k_done = s.sem("k_done")
        kmx_ready = s.sem("kmx_ready")
        ek_ready = s.sem("ek_ready")
        k_inv = s.sem("k_inv")
        k_turned = s.sem("k_turned")
        ekT_ready = s.sem("ekT_ready")
        ct_turned = s.sem("ct_turned")
        ctT_ready = s.sem("ctT_ready")
        sums_done = s.sem("sums_done")
        sums_ready = s.sem("sums_ready")
        m_done = s.sem("m_done")
        m_ready = s.sem("m_ready")
        q_turned = s.sem("q_turned")
        qT_ready = s.sem("qT_ready")
        f_done = s.sem("f_done")
        fo_ready = s.sem("fo_ready")
        sq_ready = s.sem("sq_ready")
        n_done = s.sem("n_done")
        nn_ready = s.sem("nn_ready")
        rn_ready = s.sem("rn_ready")
        rw_ready = s.sem("rw_ready")
        r_turned = s.sem("r_turned")
        gf_ready = s.sem("gf_ready")
        scaled = s.sem("scaled")
        CONSTS = (("ident", ident), ("m_half", m_half), ("seqs", seqs), ("m_half8", m_half8))
        N_CONST = 16 * (len(CONSTS) + 4)

        with s.block() as block:

            @block.sync
            def _(sp):
                for name, dst in CONSTS:
                    sp.dma_start(dst[:, :], k[name]).then_inc(consts, 16)
                sp.dma_start(w2[:, :, :], w["qk"]).then_inc(consts, 16)
                sp.dma_start(wv[:, :, :], w["v"]).then_inc(consts, 16)
                sp.dma_start(wo[:, :, :], w["o"]).then_inc(consts, 16)
                sp.dma_start(bo_g[:, :], w["bo_g"]).then_inc(consts, 16)
                sp.dma_start(xt[:, :], rows(x_in, 0)).then_inc(xt_in, 16)
                sp.dma_start(ct[:, :], rows(ctx, 0)).then_inc(ct_in, 16)
                sp.dma_start(xres[:, :], rows(x_in, 0)).then_inc(xres_in, 16)

                def load_x_and_ctx(i):
                    sp.wait_ge(q_done, 8 * i)
                    sp.dma_start(xt[:, :], rows(x_in, i)).then_inc(xt_in, 16)
                    sp.wait_ge(k_done, 8 * i)
                    sp.dma_start(ct[:, :], rows(ctx, i)).then_inc(ct_in, 16)

                def load_xres(i):
                    sp.wait_ge(norm.y_ready, i + 1)
                    sp.dma_start(xres[:, :], rows(x_in, i)).then_inc(xres_in, 16)

                load_x_and_ctx(1)
                with sp.Fori(1, NT - 1) as i:
                    load_x_and_ctx(i + 1)
                    load_xres(i)
                    norm.store(sp, x_out, i - 1, i)
                load_xres(NT - 1)
                norm.store(sp, x_out, NT - 2, NT - 1)
                norm.store(sp, x_out, NT - 1, NT)
                sp.wait_ge(norm.stored, 16 * (NT + 1))

            @block.tensor
            def _(pe):
                def queries(seq, b, n):
                    at = slice(64 * b, 64 * b + 64)
                    pe.wait_ge(ek_ready, 4 * seq + n + 1)
                    pe.matmul(ps_w[:, n, :], xt[at, n * P:(n + 1) * P], w2[at, 0, :], start=True, stop=True
                              ).then_inc(q_done, 1)

                def keys(seq, b, n):
                    at = slice(64 * b, 64 * b + 64)
                    pe.wait_ge(q_centred, 4 * seq + n + 1)
                    pe.matmul(ps_w[:, n, :], w2[at, 1, n * P:(n + 1) * P], ct[at, :], start=True, stop=True
                              ).then_inc(k_done, 1)

                def turn_ctx(i):
                    for t in range(NB):
                        mm = pe.transpose(ps_a[:, t * P:(t + 1) * P], ct[:, t * P:(t + 1) * P], ident[:, :])
                    mm.then_inc(ct_turned, 1)

                def turn_keys(seq, n):
                    if n < 2:
                        pe.wait_ge(qT_ready, 4 * seq + n + 3)
                    else:
                        pe.wait_ge(ekT_ready, 4 * seq + n - 1)
                    pe.wait_ge(ek_ready, 4 * seq + n + 5)
                    for t in range(NB):
                        mm = pe.transpose(ps_t[:, n % 2, t * P:(t + 1) * P], ek[:, n, t * P:(t + 1) * P], ident[:, :])
                    mm.then_inc(k_turned, 1)

                def turn_queries(seq, b, n):
                    if n == 0:
                        pe.wait_ge(q_ready, 4 * seq + 4)
                    if n >= 2:
                        pe.wait_ge(qT_ready, 4 * seq + n + 3)
                    for t in range(NB):
                        mm = pe.transpose(ps_t[:, n % 2, t * P:(t + 1) * P], qs[:, b, t, n * P:(n + 1) * P], ident[:, :])
                    mm.then_inc(q_turned, 1)

                def add_keys(seq, b, t):
                    mm = pe.matmul(ps_a[0:S, :], ctT[:, t, S * b:S * b + S], ekT[:, t, :], start=t == 0, stop=t == NB - 1)
                    if t == NB - 1:
                        mm.then_inc(sums_done, 1)

                def turn_of(i, b, front=True, tail=True):
                    seq = 2 * i + b
                    if front and b == 1:
                        pe.wait_ge(xt_in, 16 * i + 32)
                    for n in range(4):
                        if front:
                            queries(seq + 1, 1 - b, n)
                        turn_keys(seq, n)
                    if tail and b == 0:
                        pe.wait_ge(sq_ready, i)
                        for t in range(NB):
                            mm = pe.matmul(ps_f[:, 2 * t:2 * t + 2], sq[:, t * P:(t + 1) * P], seqs[:, :], start=True, stop=True)
                        mm.then_inc(n_done, 1)
                    if front and b == 1:
                        pe.wait_ge(ct_in, 16 * i + 32)
                    pe.wait_ge(ctT_ready, i + 1)
                    for n in range(4):
                        if front:
                            keys(seq + 1, 1 - b, n)
                        if n == 0:
                            pe.wait_ge(ekT_ready, 4 * seq + 4)
                        add_keys(seq, b, n)
                    if tail and b == 0:
                        pe.wait_ge(rw_ready, i)
                        for t in range(NB):
                            mm = pe.transpose(ps_f[:, t * P:(t + 1) * P], rw[:, t, :, :].rearrange("p b c -> p (b c)"), ident[:, :])
                        mm.then_inc(r_turned, 1)
                    turn_queries(seq, b, 0)
                    turn_queries(seq, b, 1)
                    pe.wait_ge(sums_ready, seq + 1)
                    for n in range(NP2):
                        mm = pe.matmul(ps_a[:, n * P:(n + 1) * P], sums[:, n * P:(n + 1) * P],
                                       wvo[:, 2 * n:2 * n + 2, :].rearrange("p h c -> p (h c)"), start=True, stop=True)
                    mm.then_inc(m_done, 1)
                    turn_queries(seq, b, 2)
                    turn_queries(seq, b, 3)
                    pe.wait_ge(m_ready, seq + 1)
                    if front and b == 1:
                        turn_ctx(i + 1)
                    if b == 0:
                        pe.wait_ge(scaled, i + 1)
                    for n in range(NP2):
                        pe.wait_ge(qT_ready, 4 * seq + n + 5)
                        mm = pe.matmul(ps_f[64 * b:64 * b + 64, :], m[:, n, :], qT[:, n, :], start=n == 0, stop=n == NP2 - 1,
                                       tile_position=(0, 64 * b))
                    mm.then_inc(f_done, 1)

                pe.wait_ge(consts, N_CONST)
                for h in range(8):
                    at = slice(S * (h % 2), S * (h % 2) + S)
                    mm = pe.matmul((ps_a, ps_f)[h % 2][0:S, h // 2 * S:h // 2 * S + S], wv[at, h // 2, :], wo[at, h // 2, :],
                                   start=True, stop=True)
                mm.then_inc(wvo_done, 1)
                pe.wait_ge(xt_in, 16)
                for n in range(4):
                    queries(0, 0, n)
                pe.wait_ge(ct_in, 16)
                for n in range(4):
                    keys(0, 0, n)
                pe.wait_ge(wvo_ready, 1)
                turn_ctx(0)
                turn_of(0, 0, tail=False)
                turn_of(0, 1)
                with pe.Fori(1, NT - 1) as i:
                    turn_of(i, 0)
                    turn_of(i, 1)
                turn_of(NT - 1, 0)
                turn_of(NT - 1, 1, front=False)
                pe.wait_ge(sq_ready, NT)
                for t in range(NB):
                    mm = pe.matmul(ps_f[:, 2 * t:2 * t + 2], sq[:, t * P:(t + 1) * P], seqs[:, :], start=True, stop=True)
                mm.then_inc(n_done, 1)
                pe.wait_ge(rw_ready, NT)
                for t in range(NB):
                    mm = pe.transpose(ps_f[:, t * P:(t + 1) * P], rw[:, t, :, :].rearrange("p b c -> p (b c)"), ident[:, :])
                mm.then_inc(r_turned, 1)

            @block.scalar
            def _(act):
                def exp_queries(seq, b, n):
                    act.wait_ge(q_centred, 4 * seq + n + 1)
                    nc.scalar.activation(qs[:, b, n, :], qd[:, n, :], ACT.Exp).then_inc(q_exp, 1)

                def exp_keys(seq, n):
                    act.wait_ge(kmx_ready, 4 * seq + n + 1)
                    nc.scalar.activation(ek[:, n, :], ps_w[:, n, :], ACT.Exp, bias=kmx[:, n:n + 1],
                                         accum_out=ksm[:, n:n + 1]).then_inc(ek_ready, 1)

                def keep_ctx(i):
                    act.wait_ge(ct_turned, i + 1)
                    nc.scalar.copy(ctT[:, :, :], ps_a[:, :].rearrange("p (t c) -> p t c", t=NB)).then_inc(ctT_ready, 1)

                def keep_queries(seq, n):
                    act.wait_ge(q_turned, 4 * seq + n + 1)
                    nc.scalar.copy(qT[:, n, :], ps_t[:, n % 2, :]).then_inc(qT_ready, 1)

                def roots(i):
                    act.wait_ge(rn_ready, i)
                    nc.scalar.copy(rw[:, :, :, :], rn[:, :].rearrange("p (t b) -> p t b", b=2).unsqueeze(3).broadcast_to(
                        [P, NB, 2, S])).then_inc(rw_ready, 1)

                def turn_of(i, b, front=True, tail=True):
                    seq = 2 * i + b
                    for n in range(4):
                        if front:
                            exp_queries(seq + 1, 1 - b, n)
                        act.wait_ge(k_turned, 4 * seq + n + 1)
                        nc.scalar.copy(ekT[:, :, n * P:(n + 1) * P],
                                       ps_t[:, n % 2, :].rearrange("p (t d) -> p t d", t=NB)).then_inc(ekT_ready, 1)
                    if front:
                        exp_keys(seq + 1, 0)
                        exp_keys(seq + 1, 1)
                    if tail and b == 0:
                        roots(i)
                    if front:
                        exp_keys(seq + 1, 2)
                        exp_keys(seq + 1, 3)
                    act.wait_ge(sums_done, seq + 1)
                    nc.scalar.copy(sums[:, :], ps_a[0:S, :]).then_inc(sums_ready, 1)
                    keep_queries(seq, 0)
                    keep_queries(seq, 1)
                    keep_queries(seq, 2)
                    keep_queries(seq, 3)
                    if front and b == 1:
                        keep_ctx(i + 1)

                act.wait_ge(wvo_done, 1)
                for e in range(2):
                    ins = nc.scalar.copy(wvo[:, e::2, :], (ps_a, ps_f)[e][0:S, 0:4 * S].rearrange("p (n c) -> p n c", c=S))
                ins.then_inc(wvo_ready, 1)
                for n in range(4):
                    exp_queries(0, 0, n)
                for n in range(4):
                    exp_keys(0, n)
                keep_ctx(0)
                turn_of(0, 0, tail=False)
                turn_of(0, 1)
                with act.Fori(1, NT - 1) as i:
                    turn_of(i, 0)
                    turn_of(i, 1)
                turn_of(NT - 1, 0)
                turn_of(NT - 1, 1, front=False)
                roots(NT)

            @block.vector
            def _(dve):
                def centre_queries(seq, n):
                    dve.wait_ge(q_done, 4 * seq + n + 1)
                    src = ps_w[:, n, :].rearrange("p (h d) -> p h d", h=8)
                    nc.vector.tensor_reduce(qmx[:, n, :], src, AX.X, ALU.max).then_inc(qmx_ready, 1)
                    dve.wait_ge(qmx_ready, 4 * seq + n + 1)
                    nc.vector.tensor_tensor(qd[:, n, :].rearrange("p (h d) -> p h d", h=8), src,
                                            qmx[:, n, :].unsqueeze(2).broadcast_to([P, 8, S]), ALU.subtract
                                            ).then_inc(q_centred, 1)

                def key_max(seq, n):
                    dve.wait_ge(k_done, 4 * seq + n + 1)
                    nc.vector.tensor_reduce(kmx[:, n:n + 1], ps_w[:, n, :], AX.X, ALU.max, negate=True).then_inc(kmx_ready, 1)

                def query_sums(seq, b):
                    dve.wait_ge(q_exp, 4 * seq + 4)
                    nc.vector.tensor_reduce(qsm[:, :, :], qs[:, b, :, :].rearrange("p t (h d) -> p t h d", h=8), AX.X,
                                            ALU.add).then_inc(q_sum, 1)
                    dve.wait_ge(q_sum, seq + 1)
                    nc.vector.reciprocal(qrs[:, :, :], qsm[:, :, :]).then_inc(q_inv, 1)
                    dve.wait_ge(q_inv, seq + 1)

                def scale_queries(b, n):
                    part = qs[:, b, n, :].rearrange("p (h d) -> p h d", h=8)
                    nc.vector.tensor_tensor(part, part, qrs[:, n, :].unsqueeze(2).broadcast_to([P, 8, S]), ALU.mult
                                            ).then_inc(q_ready, 1)

                def key_inverse(seq):
                    dve.wait_ge(ek_ready, 4 * seq + 8)
                    nc.vector.reciprocal(krs[:, :], ksm[:, :]).then_inc(k_inv, 1)

                def output(i):
                    dve.wait_ge(f_done, 2 * i)
                    nc.vector.tensor_scalar(fo[:, :], ps_f[:, :], bo_g[:, 0:1], None, ALU.add).then_inc(fo_ready, 1)

                def squares(i):
                    dve.wait_ge(fo_ready, i)
                    nc.vector.tensor_scalar(gf[:, :], fo[:, :], bo_g[:, 1:2], float(np.sqrt(S)), ALU.mult, ALU.mult).then_inc(gf_ready, 1)
                    dve.wait_ge(n_done, i)
                    nc.vector.tensor_scalar(nn[:, :], ps_f[:, 0:NB * 2], 1e-24, None, ALU.max).then_inc(nn_ready, 1)

                def scale_output(i):
                    dve.wait_ge(r_turned, i)
                    dve.wait_ge(gf_ready, i)
                    nc.vector.tensor_tensor(gf[:, :], ps_f[:, :], gf[:, :], ALU.mult).then_inc(scaled, 1)

                def residual(i):
                    dve.wait_ge(scaled, i + 1)
                    dve.wait_ge(xres_in, 16 * i)
                    nc.vector.tensor_tensor(norm.y[:, :], gf[:, :], xres[:, :], ALU.add).then_inc(norm.y_ready, 1)
                    norm.vector(dve, i)

                def turn_of(i, b, front=True, tail=True):
                    seq = 2 * i + b
                    tail = tail and b == 0
                    if tail:
                        output(i)
                    if front:
                        for n in range(4):
                            centre_queries(seq + 1, n)
                    if tail:
                        squares(i)
                    if front:
                        for n in range(4):
                            key_max(seq + 1, n)
                        query_sums(seq + 1, 1 - b)
                    if tail:
                        scale_output(i)
                    dve.wait_ge(m_done, seq + 1)
                    dve.wait_ge(k_inv, seq + 1)
                    for e in range(2):
                        half = slice(S * e, S * e + S)
                        ins = nc.vector.scalar_tensor_tensor(
                            m[half, :, :], ps_a[half, :].rearrange("p (n h c) -> p n h c", n=NP2, h=2)[:, :, e, :],
                            S ** -0.5, krs[half, :].unsqueeze(2).broadcast_to([S, NP2, S]), ALU.mult, ALU.mult)
                    ins.then_inc(m_ready, 1)
                    if front:
                        dve.wait_ge(m_ready, seq + 1)
                        key_inverse(seq + 1)
                        for n in range(NB):
                            scale_queries(1 - b, n)
                    if tail:
                        residual(i)

                dve.sem_inc(norm.stored, 16)
                dve.sem_inc(norm.y_ready, 1)
                dve.sem_inc(scaled, 1)
                dve.sem_inc(ek_ready, 4)
                dve.sem_inc(qT_ready, 4)
                dve.wait_ge(consts, N_CONST)
                for n in range(4):
                    centre_queries(0, n)
                for n in range(4):
                    key_max(0, n)
                query_sums(0, 0)
                for n in range(4):
                    scale_queries(0, n)
                key_inverse(0)
                turn_of(0, 0, tail=False)
                turn_of(0, 1)
                with dve.Fori(1, NT - 1) as i:
                    turn_of(i, 0)
                    turn_of(i, 1)
                turn_of(NT - 1, 0)
                turn_of(NT - 1, 1, front=False)
                output(NT)
                squares(NT)
                scale_output(NT)
                residual(NT)
                norm.end(dve)

            @block.gpsimd
            def _(pool):
                pool.wait_ge(consts, N_CONST)
                with pool.Fori(0, NT) as i:
                    pool.wait_ge(fo_ready, i + 1)
                    nc.gpsimd.tensor_tensor(sq[:, :], fo[:, :], fo[:, :], ALU.mult).then_inc(sq_ready, 1)
                    pool.wait_ge(nn_ready, i + 1)
                    nc.gpsimd.tensor_tensor(rn[:, :], nn[:, :], m_half8[:, :], ALU.pow).then_inc(rn_ready, 1)
                    norm.root(pool, i + 1, m_half)



def ffn1(nc, x_in, out, w, k):
    with Scope(nc, "f1") as s:
        ident = s.sb("ident", [P, P])
        m_half = s.sb("m_half", [P, 1])
        wg = s.sb("wg", [P, DC, INTER])
        wu = s.sb("wu", [P, DC, INTER])
        wd = s.sb("wd", [P, IT, D])
        unpack(nc, w, k, ident, m_half, (wg, wu, wd))
        swiglu(nc, x_in, out, ident, m_half, wg, wu, wd)


def unpack(nc, w, k, ident, m_half, weights):
    with Scope(nc, "f1u") as s:
        nibble = s.sb("nibble", [P, 1], I32)
        q = s.sb("q", [P, 2, IT * D], I32)
        zeros = s.sb("zeros", [P, 2, IT * D // 8], I32)
        z = s.sb("z", [P, 2, IT * D], I32)
        scale = s.sb("scale", [P, 2, IT * D], F16)
        consts = s.sem("consts")
        w_in = [s.sem(f"w_in{n}") for n in range(2)]
        q_ready = s.sem("q_ready")
        z_ready = s.sem("z_ready")
        diff = s.sem("diff")
        done = s.sem("done")
        mats = (("gate", DC, INTER), ("up", DC, INTER), ("down", IT, D))
        LOADS = (4, 4, 6)

        with s.block() as block:

            @block.sync
            def _(sp):
                sp.dma_start(ident[:, :], k["ident"]).then_inc(consts, 16)
                sp.dma_start(m_half[:, :], k["m_half"]).then_inc(consts, 16)
                sp.dma_start(nibble[:, :], k["nibble"]).then_inc(consts, 16)
                for i, (name, kt, n) in enumerate(mats):
                    b = i % 2
                    if i >= 2:
                        sp.wait_ge(done, i - 1)
                    qw = w[f"{name}_q"]
                    for t in range(kt):
                        r = min(P // 8, qw.shape[0] - t * P // 8)
                        src = qw[t * P // 8:t * P // 8 + r, :].unsqueeze(1).broadcast_to([r, 8, n])
                        sp.dma_start(q[0:8 * r, b, t * n:(t + 1) * n], src).then_inc(w_in[b], 16)
                    zs = w[f"{name}_z"].rearrange("g n -> (g n)").unsqueeze(0).broadcast_to([P, kt * n // 8])
                    sp.dma_start(zeros[:, b, 0:kt * n // 8], zs).then_inc(w_in[b], 16)
                    ss = w[f"{name}_s"].rearrange("g n -> (g n)").unsqueeze(0).broadcast_to([P, kt * n])
                    sp.dma_start(scale[:, b, 0:kt * n], ss).then_inc(w_in[b], 16)

            @block.vector
            def _(dve):
                dve.wait_ge(consts, 48)
                count = [0, 0]
                for i, (name, kt, n) in enumerate(mats):
                    b = i % 2
                    count[b] += 16 * (kt + 2)
                    dve.wait_ge(w_in[b], count[b])
                    parts = [(P, 0, kt * n)] if name != "down" else [(P, 0, (kt - 1) * n), (LAST, (kt - 1) * n, kt * n)]
                    for r, lo, hi in parts:
                        qp = q[0:r, b, lo:hi]
                        last = nc.vector.tensor_scalar(qp, qp, nibble[0:r, :], 15, ALU.logical_shift_right, ALU.bitwise_and)
                    last.then_inc(q_ready, 1)
                    zv = z[:, b, 0:kt * n].rearrange("p (m j) -> p m j", j=8)
                    for j in range(8):
                        last = nc.vector.tensor_scalar(zv[:, :, j], zeros[:, b, 0:kt * n // 8], 4 * j, 15,
                                                       ALU.logical_shift_right, ALU.bitwise_and)
                    last.then_inc(z_ready, 1)
                    dve.wait_ge(q_ready, i + 1)
                    dve.wait_ge(z_ready, i + 1)
                    dst = weights[i]
                    for r, lo, hi in parts:
                        out = dst[0:r, :, :].rearrange("p t n -> p (t n)")[:, lo:hi]
                        last = nc.vector.scalar_tensor_tensor(out, q[0:r, b, lo:hi], 1.0, z[0:r, b, lo:hi], ALU.subtract,
                                                              ALU.subtract)
                    last.then_inc(diff, 1)
                    dve.wait_ge(diff, i + 1)
                    for r, lo, hi in parts:
                        out = dst[0:r, :, :].rearrange("p t n -> p (t n)")[:, lo:hi]
                        last = nc.vector.tensor_tensor(out, out, scale[0:r, b, lo:hi], ALU.mult)
                    last.then_inc(done, 1)


def swiglu(nc, x_in, out, ident, m_half, wg, wu, wd):
    with Scope(nc, "f1m") as s:
        xt = s.sb("xt", [P, 4, D])
        xres = s.sb("xres", [P, 4, D])
        xT = s.sb("xT", [P, DC, D])
        th = s.sb("th", [P, 2, D])
        t1 = s.sb("t1", [P, 2, D])
        h = s.sb("h", [P, IT, D])
        y16 = s.sb("y16", [P, 2, D], F16)
        norm = Norm(nc, s, ahead=2)
        ps_t = s.ps("ps_t", [P, 2, DC, P])
        ps_g = s.ps("ps_g", [P, 2, D])
        ps_u = s.ps("ps_u", [P, 2, D])
        ps_y = s.ps("ps_y", [P, 2, D])
        xt_in = s.sem("xt_in")
        xres_in = s.sem("xres_in")
        x_turned = s.sem("x_turned")
        xT_ready = s.sem("xT_ready")
        g_done = s.sem("g_done")
        u_done = s.sem("u_done")
        th_ready = s.sem("th_ready")
        t1_ready = s.sem("t1_ready")
        h_ready = s.sem("h_ready")
        y_done = s.sem("y_done")
        y_kept = s.sem("y_kept")

        with s.block() as block:

            @block.sync
            def _(sp):
                def group(g):
                    return x_in[bass.ds(g * D, D), :].rearrange("(t p) n -> p t n", p=P)

                sp.dma_start(xt[:, :, :], group(0)).then_inc(xt_in, 16)
                sp.dma_start(xres[:, :, :], group(0)).then_inc(xres_in, 16)
                with sp.Fori(0, NG - 1) as g:
                    sp.wait_ge(x_turned, 4 * g + 4)
                    sp.dma_start(xt[:, :, :], group(g + 1)).then_inc(xt_in, 16)
                    for t in range(4):
                        norm.store(sp, out, 4 * g + t, 4 * g + t + 1)
                    sp.dma_start(xres[:, :, :], group(g + 1)).then_inc(xres_in, 16)
                for t in range(4):
                    norm.store(sp, out, 4 * (NG - 1) + t, 4 * (NG - 1) + t + 1)
                sp.wait_ge(norm.stored, 16 * (NT + 1))

            @block.tensor
            def _(pe):
                with pe.Fori(0, NG) as g:
                    pe.wait_ge(xt_in, 16 * g + 16)
                    for t in range(4):
                        pe.wait_ge(xT_ready, 4 * g + t + 1)
                        for c in range(DC):
                            mm = pe.transpose(ps_t[:, t % 2, c, :], xt[:, t, c * P:(c + 1) * P], ident[:, :])
                        mm.then_inc(x_turned, 1)
                    pe.wait_ge(xT_ready, 4 * g + 6)
                    for it in range(IT):
                        r = tile_rows(it)
                        u = g * IT + it
                        pe.wait_ge(t1_ready, u + 1 + (it == 0))
                        for c in range(DC):
                            mm = pe.matmul(ps_g[0:r, it % 2, :], wg[:, c, it * P:it * P + r], xT[:, c, :],
                                           start=c == 0, stop=c == DC - 1)
                        mm.then_inc(g_done, 1)
                        pe.wait_ge(h_ready, u + 1 + (it == 0))
                        for c in range(DC):
                            mm = pe.matmul(ps_u[0:r, it % 2, :], wu[:, c, it * P:it * P + r], xT[:, c, :],
                                           start=c == 0, stop=c == DC - 1)
                        mm.then_inc(u_done, 1)
                    for t in range(4):
                        pe.wait_ge(y_kept, 4 * g + t + 1)
                        for it in range(IT):
                            r = tile_rows(it)
                            if t == 0:
                                pe.wait_ge(h_ready, g * IT + it + 3)
                            mm = pe.matmul(ps_y[:, t % 2, :], h[0:r, it, t * P:(t + 1) * P], wd[0:r, it, :],
                                           start=it == 0, stop=it == IT - 1)
                        mm.then_inc(y_done, 1)

            @block.scalar
            def _(act):
                act.sem_inc(xT_ready, 2)
                act.sem_inc(y_kept, 2)
                with act.Fori(0, NG) as g:
                    for t in range(4):
                        act.wait_ge(x_turned, 4 * g + t + 1)
                        nc.scalar.copy(xT[:, :, t * P:(t + 1) * P], ps_t[:, t % 2, :, :]).then_inc(xT_ready, 1)
                    for it in range(IT):
                        r = tile_rows(it)
                        act.wait_ge(g_done, g * IT + it + 1)
                        nc.scalar.activation(th[0:r, it % 2, :], ps_g[0:r, it % 2, :], ACT.Tanh, scale=0.5).then_inc(th_ready, 1)
                    for t in range(4):
                        act.wait_ge(y_done, 4 * g + t + 2)
                        act.wait_ge(norm.y_ready, 4 * g + t + 1)
                        nc.scalar.copy(y16[:, t % 2, :], ps_y[:, t % 2, :]).then_inc(y_kept, 1)

            @block.vector
            def _(dve):
                dve.sem_inc(norm.stored, 16)
                dve.sem_inc(t1_ready, 2)
                dve.sem_inc(h_ready, 2)
                dve.sem_inc(y_done, 1)
                dve.sem_inc(norm.y_ready, 2)
                with dve.Fori(0, NG) as g:
                    for it in range(IT):
                        r = tile_rows(it)
                        u = g * IT + it
                        if it == 0:
                            dve.wait_ge(y_done, 4 * g + 1)
                        dve.wait_ge(th_ready, u + 1)
                        nc.vector.scalar_tensor_tensor(t1[0:r, it % 2, :], th[0:r, it % 2, :], 1.0, ps_g[0:r, it % 2, :],
                                                       ALU.add, ALU.mult).then_inc(t1_ready, 1)
                        dve.wait_ge(t1_ready, u + 3)
                        dve.wait_ge(u_done, u + 1)
                        nc.vector.scalar_tensor_tensor(h[0:r, it, :], t1[0:r, it % 2, :], 0.5, ps_u[0:r, it % 2, :],
                                                       ALU.mult, ALU.mult).then_inc(h_ready, 1)
                    dve.wait_ge(xres_in, 16 * g + 16)
                    for t in range(4):
                        dve.wait_ge(y_kept, 4 * g + t + 3)
                        nc.vector.tensor_tensor(norm.y[:, :], y16[:, t % 2, :], xres[:, t, :], ALU.add).then_inc(norm.y_ready, 1)
                        norm.vector(dve, 4 * g + t + 1)
                norm.end(dve)

            @block.gpsimd
            def _(pool):
                with pool.Fori(0, NT) as i:
                    norm.root(pool, i + 1, m_half)



def program(nc, t, w, k, out):
    x = t["x"]
    ctx = t["ctx_4096"]
    stage = [x] + [nc.dram_tensor(f"x_after_{n}", (ROWS, D), F32).ap() for n in range(1, 6)] + [out]
    with Scope(nc, "keep") as keep:
        xq = Quant(keep, keep, "xq", NT)
        attention0(nc, stage[0], stage[1], t["L0_attn_Wq"], t["L0_attn_Wk"], t["L0_attn_Wv"], t["L0_attn_Wo"], k)
        cross0(nc, stage[1], ctx, stage[2], w["cross0"], k, xq)
        up_scratch = nc.dram_tensor("up_scratch", (IT, P, ROWS), F32).ap()
        ffn0(nc, stage[2], stage[3], t["L0_ffn_w_gate"], t["L0_ffn_w_up"], t["L0_ffn_w_down"], up_scratch, k, xq)
        lat_scratch = nc.dram_tensor("lat_scratch", (P, 4, ROWS), F32).ap()
        latent1(nc, stage[3], stage[4], w["latent1"], lat_scratch, k)
        cross1(nc, stage[4], ctx, stage[5], w["cross1"], k)
        ffn1(nc, stage[5], stage[6], w["ffn1"], k)


def constants():
    pos = np.tile(np.arange(S, dtype=np.float32), 2)
    freq = (1.0 / np.float32(10000.0) ** (np.arange(0, 16, 2, dtype=np.float32) / 16)).astype(np.float32)
    ang = (pos[:, None] * freq[None, :]).astype(np.float32)
    sin = np.stack([-np.sin(ang), np.sin(ang)], -1).reshape(P, 16)
    p = np.arange(P)
    return {
        "ident": np.eye(P, dtype=np.float32),
        "cos": np.repeat(np.cos(ang), 2, axis=1).astype(np.float32),
        "sin": sin.astype(np.float32),
        "causal": np.where(np.arange(S)[None, :] > (p % S)[:, None], NEG, 0.0).astype(np.float32),
        "half_mask": ((p % 32 // 16)[:, None] == np.arange(2)[None, :]).astype(np.float32),
        "m_half": np.full((P, 1), -0.5, np.float32),
        "m_half8": np.full((P, 8), -0.5, np.float32),
        "seqs": ((p // 64)[:, None] == np.arange(2)[None, :]).astype(np.float32),
        "nibble": (4 * (p % 8)).astype(np.int32)[:, None],
        "heads": ((p // 8)[:, None] == np.arange(16)[None, :]).astype(np.float32),
    }


def twice(w):
    out = np.zeros((P, P), w.dtype)
    out[:S, :S] = out[S:, S:] = w.T
    return out


def kernel(**inputs):
    import concourse.bacc as bacc
    from concourse.bass_utils import run_bass_kernel_spmd

    nc = bacc.Bacc("TRN2", target_bir_lowering=False, num_devices=1)
    arrays = {}

    def given(name, a):
        a = np.ascontiguousarray(a)
        arrays[name] = a
        return nc.dram_tensor(name, a.shape, mybir.dt.from_np(a.dtype), kind="ExternalInput").ap()

    g = {n: np.asarray(a) for n, a in inputs.items()}
    t = {n: given(f"in_{n}", g[n].reshape(ROWS, D)) for n in ("x", "ctx_4096")}
    for n in ("L0_attn_Wq", "L0_attn_Wk", "L0_attn_Wv", "L0_attn_Wo"):
        t[n] = given(f"in_{n}", g[n])
    for n in ("L0_ffn_w_gate", "L0_ffn_w_up", "L0_ffn_w_down"):
        t[n] = given(f"in_{n}", g[n])
    w = {"cross0": {
        "wts": given("in_cross0_weights", np.stack([twice(g[f"L0_xattn_W{n}"]) for n in "qkvo"], 1)),
        "bias": given("in_cross0_biases", np.stack([np.tile(g[f"L0_xattn_b{n}"], 2) for n in "qkvo"], 1)),
    }}
    w["latent1"] = {
        "q": given("in_latent1_q", g["L1_attn_Wq"].T),
        "down": given("in_latent1_down", np.concatenate([g["L1_attn_Wk_down"].T, g["L1_attn_Wv_down"].T], 1)),
        "k_up": given("in_latent1_k_up", g["L1_attn_Wk_up"].T),
        "v_up": given("in_latent1_v_up", g["L1_attn_Wv_up"].T),
        "o": given("in_latent1_o", g["L1_attn_Wo"].T),
    }
    both = lambda a: np.concatenate([a, a], 0)
    w["cross1"] = {
        "qk": given("in_cross1_qk", both(np.stack([g[f"L1_xattn_W{n}"].T for n in "qk"], 1))),
        "v": given("in_cross1_v", g["L1_xattn_Wv"].reshape(4, P, S).transpose(1, 0, 2)),
        "o": given("in_cross1_o", g["L1_xattn_Wo"].T.reshape(4, P, S).transpose(1, 0, 2)),
        "bo_g": given("in_cross1_bo_g", both(np.stack([g["L1_xattn_bo"], g["L1_xattn_g"].reshape(S)], 1))),
    }
    w["ffn1"] = {f"{m}_{c}": given(f"in_ffn1_{m}_{c}", g[f"L1_ffn_{m}_{n}"])
                 for m in ("gate", "up", "down") for c, n in (("q", "qweight"), ("z", "zeros"), ("s", "scales"))}
    k = {n: given(f"const_{n}", a) for n, a in constants().items()}
    out = nc.dram_tensor("out_dram", (ROWS, D), F32, kind="ExternalOutput").ap()
    program(nc, t, w, k, out)
    r = run_bass_kernel_spmd(nc, [arrays], core_ids=[0])
    return r.results[0]["out_dram"].reshape(B, S, D)
```
